# Optimizing a Trainium2 kernel written in Bass

```python
import numpy as np
import jax
import jax.numpy as jnp

def _softmax(x, axis=-1):
    return jax.nn.softmax(x, axis=axis)

def _gelu(x):
    return jax.nn.gelu(x, approximate=True)

def _silu(x):
    return jax.nn.silu(x)

def _sigmoid(x):
    return jax.nn.sigmoid(x)

def _layernorm(x, axis=-1, eps=1e-05):
    m = jnp.mean(x, axis=axis, keepdims=True)
    v = jnp.var(x, axis=axis, keepdims=True)
    return (x - m) / jnp.sqrt(v + eps)

def _scatter_add(tgt, idx, src, axis=0):
    return tgt.at[idx].add(src)

def _segment_sum(src, seg, n):
    return jax.ops.segment_sum(src, seg, n)
kernel_name = 'mk_adaln_ffn_d2_seqx_r8_23f270'

def setup_inputs(seed: int=0):
    np.random.seed(seed)
    _w = jnp.asarray

    def _rec_inputs():
        import jax
        import jax.numpy as jnp
        _rk = jax.random.key(seed)
        x = -0.0002919 + 1 * jax.random.normal(jax.random.fold_in(_rk, 1), (2, 512, 128), jnp.float32)
        _lenS = 512 - jax.random.randint(jax.random.fold_in(_rk, 7), (2,), 0, max(1, 512 // 4) + 1, jnp.int32)
        _lenS2 = 512 - jax.random.randint(jax.random.fold_in(_rk, 8), (2,), 0, max(1, 512 // 4) + 1, jnp.int32)
        cond_1024 = 0.0061147 + 1.02565 * jax.random.normal(jax.random.fold_in(_rk, 11), (2, 128), jnp.float32)
        _validS = jnp.arange(512)[None, :] < _lenS[:, None]
        _validS2 = jnp.arange(512)[None, :] < _lenS2[:, None]
        _causal = jnp.tril(jnp.ones((512, 512), dtype=bool))
        mask_Bx1x1xS_ff0 = jnp.where(jnp.ones((2, 1, 1, 512), dtype=bool), 0.0, -1000000000.0).astype(jnp.float32)
        return (x, cond_1024, mask_Bx1x1xS_ff0)
    x, cond_1024, mask_Bx1x1xS_ff0 = _rec_inputs()

    def _L0_cond_setup():
        import jax, jax.numpy as jnp
        import numpy as np
        EMBED = 128
        HEADS = 16
        HDIM = EMBED // HEADS
        MASK_OUT = -10000.0

        def _split_heads(t):
            B, T, _ = t.shape
            return t.reshape(B, T, HEADS, HDIM).transpose(0, 2, 1, 3)
        key = jax.random.key(seed)
        ks = jax.random.split(key, 12)
        B, S = (4, 1023)
        scale = 0.02
        return {'word_hidden_states': jax.random.normal(ks[0], (B, S, EMBED), jnp.float32), 'image_hidden_states': jax.random.normal(ks[1], (B, EMBED), jnp.float32), 'attention_mask': jnp.zeros((B, 1, 1, S), jnp.float32), 'c_attn_w': jax.random.normal(ks[2], (EMBED, 3 * EMBED), jnp.float32) * scale, 'c_attn_b': jnp.zeros((3 * EMBED,), jnp.float32), 'c_proj_w': jax.random.normal(ks[3], (EMBED, EMBED), jnp.float32) * scale, 'c_proj_b': jnp.zeros((EMBED,), jnp.float32), 'uk_w': jax.random.normal(ks[4], (EMBED, EMBED), jnp.float32) * scale, 'uk_b': jnp.zeros((EMBED,), jnp.float32), 'uv_w': jax.random.normal(ks[5], (EMBED, EMBED), jnp.float32) * scale, 'uv_b': jnp.zeros((EMBED,), jnp.float32)}
    _L0_cond_all = _L0_cond_setup()
    _L0_cond_in = {k: v for k, v in _L0_cond_all.items() if k in ('c_attn_w', 'c_attn_b', 'c_proj_w', 'c_proj_b', 'uk_w', 'uk_b', 'uv_w', 'uv_b')}
    del _L0_cond_all

    def _L0_ffn_setup():
        import jax, jax.numpy as jnp
        import numpy as np
        D_MODEL = 128
        D_HIDDEN = 512
        NUM_EXPERT = 8
        TOP_K = 2
        B, N = (1, 1024)

        def _expert_mlp(x, W1, b1, W2, b2, W3, b3):
            h = jax.nn.gelu(jnp.einsum('bnd,dh->bnh', x, W1) + b1, approximate=False)
            h = jax.nn.gelu(jnp.einsum('bnh,hk->bnk', h, W2) + b2, approximate=False)
            return jnp.einsum('bnh,hd->bnd', h, W3) + b3
        key = jax.random.key(seed)
        ks = jax.random.split(key, 8)
        s1 = 1.0 / np.sqrt(D_MODEL)
        s2 = 1.0 / np.sqrt(D_HIDDEN)
        return {'x': jax.random.normal(ks[0], (B, N, D_MODEL), jnp.float32), 'expert_tokens': jax.random.normal(ks[1], (NUM_EXPERT, D_MODEL), jnp.float32), 'W1': jax.random.normal(ks[2], (NUM_EXPERT, D_MODEL, D_HIDDEN), jnp.float32) * s1, 'b1': jnp.zeros((NUM_EXPERT, D_HIDDEN), jnp.float32), 'W2': jax.random.normal(ks[3], (NUM_EXPERT, D_HIDDEN, D_HIDDEN), jnp.float32) * s2, 'b2': jnp.zeros((NUM_EXPERT, D_HIDDEN), jnp.float32), 'W3': jax.random.normal(ks[4], (NUM_EXPERT, D_HIDDEN, D_MODEL), jnp.float32) * s2, 'b3': jnp.zeros((NUM_EXPERT, D_MODEL), jnp.float32)}
    _L0_ffn_all = _L0_ffn_setup()
    _L0_ffn_in = {k: v for k, v in _L0_ffn_all.items() if k in ('expert_tokens', 'W1', 'b1', 'W2', 'b2', 'W3', 'b3')}
    del _L0_ffn_all

    def _L1_cond_setup():
        import jax, jax.numpy as jnp
        import numpy as np
        import math
        IN_F = 128
        OUT_F = 128
        B = 16
        L = 512
        key = jax.random.key(seed)
        k1, k2, k3 = jax.random.split(key, 3)
        Efou = jax.random.normal(k1, (B, L, IN_F), dtype=jnp.float32)
        y = jax.random.normal(k2, (B, IN_F), dtype=jnp.float32)
        weight = jax.random.normal(k3, (1, OUT_F, IN_F, 1), dtype=jnp.float32)
        return {'Efou': Efou, 'y': y, 'weight': weight}
    _L1_cond_all = _L1_cond_setup()
    _L1_cond_in = {k: v for k, v in _L1_cond_all.items() if k in ('weight',)}
    del _L1_cond_all

    def _L1_ffn_setup():
        import jax, jax.numpy as jnp
        import numpy as np
        N_EXP = 8
        TOP_K = 2
        CAPACITY_FACTOR = 1.25
        key = jax.random.key(seed)
        ks = jax.random.split(key, 5)
        B, T, D = (4, 128, 128)
        H = 4 * D
        E = N_EXP
        x = jax.random.normal(ks[0], (B, T, D), jnp.float32)
        gate_w = jax.random.normal(ks[1], (D, E), jnp.float32) * 0.02
        c_fc = jax.random.normal(ks[2], (E, D, H), jnp.float32) * 0.02
        fc_bias = jnp.zeros((E, 1, H), jnp.float32)
        c_proj = jax.random.normal(ks[3], (E, H, D), jnp.float32) * 0.02
        proj_bias = jnp.zeros((E, 1, D), jnp.float32)
        return dict(x=x, gate_w=gate_w, c_fc=c_fc, fc_bias=fc_bias, c_proj=c_proj, proj_bias=proj_bias)
    _L1_ffn_all = _L1_ffn_setup()
    _L1_ffn_in = {k: v for k, v in _L1_ffn_all.items() if k in ('gate_w', 'c_fc', 'fc_bias', 'c_proj', 'proj_bias')}
    del _L1_ffn_all
    return {'x': x, 'cond_1024': cond_1024, 'mask_Bx1x1xS_ff0': mask_Bx1x1xS_ff0, 'L0_cond_c_attn_w': _L0_cond_in['c_attn_w'], 'L0_cond_c_attn_b': _L0_cond_in['c_attn_b'], 'L0_cond_c_proj_w': _L0_cond_in['c_proj_w'], 'L0_cond_c_proj_b': _L0_cond_in['c_proj_b'], 'L0_cond_uk_w': _L0_cond_in['uk_w'], 'L0_cond_uk_b': _L0_cond_in['uk_b'], 'L0_cond_uv_w': _L0_cond_in['uv_w'], 'L0_cond_uv_b': _L0_cond_in['uv_b'], 'L0_ffn_expert_tokens': _L0_ffn_in['expert_tokens'], 'L0_ffn_W1': _L0_ffn_in['W1'], 'L0_ffn_b1': _L0_ffn_in['b1'], 'L0_ffn_W2': _L0_ffn_in['W2'], 'L0_ffn_b2': _L0_ffn_in['b2'], 'L0_ffn_W3': _L0_ffn_in['W3'], 'L0_ffn_b3': _L0_ffn_in['b3'], 'L1_cond_weight': _L1_cond_in['weight'], 'L1_ffn_gate_w': _L1_ffn_in['gate_w'], 'L1_ffn_c_fc': _L1_ffn_in['c_fc'], 'L1_ffn_fc_bias': _L1_ffn_in['fc_bias'], 'L1_ffn_c_proj': _L1_ffn_in['c_proj'], 'L1_ffn_proj_bias': _L1_ffn_in['proj_bias']}

def reference(x, cond_1024, mask_Bx1x1xS_ff0, L0_cond_c_attn_w, L0_cond_c_attn_b, L0_cond_c_proj_w, L0_cond_c_proj_b, L0_cond_uk_w, L0_cond_uk_b, L0_cond_uv_w, L0_cond_uv_b, L0_ffn_expert_tokens, L0_ffn_W1, L0_ffn_b1, L0_ffn_W2, L0_ffn_b2, L0_ffn_W3, L0_ffn_b3, L1_cond_weight, L1_ffn_gate_w, L1_ffn_c_fc, L1_ffn_fc_bias, L1_ffn_c_proj, L1_ffn_proj_bias):
    import jax
    import jax.numpy as jnp

    def _L0_cond_ref(word_hidden_states, image_hidden_states, attention_mask, c_attn_w, c_attn_b, c_proj_w, c_proj_b, uk_w, uk_b, uv_w, uv_b):
        import jax, jax.numpy as jnp
        import numpy as np
        EMBED = 128
        HEADS = 16
        HDIM = EMBED // HEADS
        MASK_OUT = -10000.0

        def _split_heads(t):
            B, T, _ = t.shape
            return t.reshape(B, T, HEADS, HDIM).transpose(0, 2, 1, 3)
        B, S, _ = word_hidden_states.shape
        qkv = word_hidden_states @ c_attn_w + c_attn_b
        q_word, k_word, v_word = jnp.split(qkv, 3, axis=-1)
        img = image_hidden_states[:, None, :]
        k_img = img @ uk_w.T + uk_b
        v_img = img @ uv_w.T + uv_b
        k = jnp.concatenate([k_img, k_word], axis=1)
        v = jnp.concatenate([v_img, v_word], axis=1)
        q = _split_heads(q_word)
        k = _split_heads(k)
        v = _split_heads(v)
        scores = jnp.einsum('bhqd,bhkd->bhqk', q, k) / jnp.sqrt(jnp.float32(HDIM))
        qi = jnp.arange(S)[:, None]
        kj = jnp.arange(S + 1)[None, :]
        causal = kj <= qi + 1
        scores = jnp.where(causal[None, None], scores, jnp.float32(MASK_OUT))
        zero_col = jnp.zeros(attention_mask.shape[:-1] + (1,), attention_mask.dtype)
        mask = jnp.concatenate([zero_col, attention_mask], axis=-1)
        scores = scores + mask
        attn = jax.nn.softmax(scores, axis=-1)
        out = jnp.einsum('bhqk,bhkd->bhqd', attn, v)
        out = out.transpose(0, 2, 1, 3).reshape(B, S, EMBED)
        out = out @ c_proj_w + c_proj_b
        return out

    def _L0_ffn_ref(x, expert_tokens, W1, b1, W2, b2, W3, b3):
        import jax, jax.numpy as jnp
        import numpy as np
        D_MODEL = 128
        D_HIDDEN = 512
        NUM_EXPERT = 8
        TOP_K = 2
        B, N = (1, 1024)

        def _expert_mlp(x, W1, b1, W2, b2, W3, b3):
            h = jax.nn.gelu(jnp.einsum('bnd,dh->bnh', x, W1) + b1, approximate=False)
            h = jax.nn.gelu(jnp.einsum('bnh,hk->bnk', h, W2) + b2, approximate=False)
            return jnp.einsum('bnh,hd->bnd', h, W3) + b3
        scores = jnp.einsum('bnd,ed->bne', x, expert_tokens)
        _, topk_idx = jax.lax.top_k(scores, TOP_K)
        outputs = jnp.zeros_like(x)
        num_expert = W1.shape[0]
        for i in range(num_expert):
            w = jnp.mean((topk_idx == i).astype(x.dtype), axis=-1, keepdims=True)
            y = _expert_mlp(x, W1[i], b1[i], W2[i], b2[i], W3[i], b3[i])
            outputs = outputs + y * w
        return outputs

    def _L1_cond_ref(Efou, y, weight):
        import jax, jax.numpy as jnp
        import numpy as np
        import math
        IN_F = 128
        OUT_F = 128
        B = 16
        L = 512
        b, img_size, in_f = Efou.shape
        out_f = weight.shape[1]
        scale = 1.0 / math.sqrt(in_f)
        w = scale * weight[:, :, :, 0] * y[:, None, :]
        dnorm = jax.lax.rsqrt(jnp.sum(w * w, axis=2, keepdims=True) + 1e-08)
        w = w * dnorm
        E = Efou.reshape(b, in_f, img_size)
        x = jnp.einsum('boi,bil->bol', w, E)
        return x.reshape(b, img_size, out_f)

    def _L1_ffn_ref(x, gate_w, c_fc, fc_bias, c_proj, proj_bias):
        import jax, jax.numpy as jnp
        import numpy as np
        N_EXP = 8
        TOP_K = 2
        CAPACITY_FACTOR = 1.25
        B, T, D = x.shape
        n = B * T
        E, k = (N_EXP, TOP_K)
        cap = int(CAPACITY_FACTOR * n * k / E)
        xt = x.reshape(n, D)
        logits = xt @ gate_w
        top_logits, top_idx = jax.lax.top_k(logits, k)
        masked = jnp.full_like(logits, -jnp.inf)
        masked = masked.at[jnp.arange(n)[:, None], top_idx].set(top_logits)
        router_probs = jax.nn.softmax(masked, axis=-1)
        exp_mask = jax.nn.one_hot(top_idx, E, dtype=jnp.int32)
        exp_mask = jnp.transpose(exp_mask, (1, 0, 2))
        exp_rank = jnp.cumsum(exp_mask.reshape(k * n, E), axis=0) - 1
        exp_rank = exp_rank.reshape(k, n, E)
        exp_mask = exp_mask * (exp_rank < cap).astype(jnp.int32)
        used_capacity = jnp.sum(exp_mask, axis=(0, 1))
        exp_rank = jnp.sum(exp_mask * exp_rank, axis=-1)
        exp_weights = exp_mask.astype(x.dtype) * router_probs[None]
        rank_oh = jax.nn.one_hot(exp_rank, cap, dtype=x.dtype)
        cb_weight = jnp.einsum('kne,knc->nec', exp_weights, rank_oh)
        sec_mask = (cb_weight != 0).astype(x.dtype)
        exp_batches = jnp.einsum('nec,nd->ecd', sec_mask, xt)
        h = jnp.einsum('ecd,edh->ech', exp_batches, c_fc) + fc_bias
        h = jax.nn.gelu(h, approximate=False)
        exp_out = jnp.einsum('ech,ehd->ecd', h, c_proj) + proj_bias
        out = jnp.einsum('nec,ecd->nd', cb_weight, exp_out)
        return out.reshape(B, T, D)
    x = x + _L0_ffn_ref(_L0_cond_ref(x, cond_1024, mask_Bx1x1xS_ff0, L0_cond_c_attn_w, L0_cond_c_attn_b, L0_cond_c_proj_w, L0_cond_c_proj_b, L0_cond_uk_w, L0_cond_uk_b, L0_cond_uv_w, L0_cond_uv_b), L0_ffn_expert_tokens, L0_ffn_W1, L0_ffn_b1, L0_ffn_W2, L0_ffn_b2, L0_ffn_W3, L0_ffn_b3)
    x = x + _L1_ffn_ref(_L1_cond_ref(x, cond_1024, L1_cond_weight), L1_ffn_gate_w, L1_ffn_c_fc, L1_ffn_fc_bias, L1_ffn_c_proj, L1_ffn_proj_bias)
    return x

_drawn_inputs = setup_inputs


def setup_inputs(seed=0):
    import zlib

    import numpy as np

    out = dict(_drawn_inputs(seed))
    spreads = {'L0_cond_c_attn_b': (0.0, 0.615),
     'L0_cond_c_proj_b': (0.0, 0.1),
     'L0_cond_uk_b': (0.0, 0.8),
     'L0_cond_uv_b': (0.0, 0.8),
     'L0_ffn_b1': (0.0, 0.358),
     'L0_ffn_b2': (0.0, 0.1),
     'L0_ffn_b3': (0.0, 0.1),
     'L1_ffn_fc_bias': (0.0, 0.47),
     'L1_ffn_proj_bias': (0.0, 0.1)}
    factors = {'L0_cond_c_attn_w': 2.936, 'L0_cond_uk_w': 8.0, 'L0_cond_uv_w': 5.741, 'L0_ffn_W1': 2.865}
    for name, (base, spread) in spreads.items():
        noise = np.random.default_rng([zlib.crc32(name.encode()), seed]).standard_normal(out[name].shape)
        drawn = base * np.exp(spread * noise) if base else spread * noise
        out[name] = jnp.asarray(drawn.astype(out[name].dtype))
    for name, factor in factors.items():
        out[name] = (out[name] * factor).astype(out[name].dtype)
    return out
```

```python
from contextlib import ExitStack

import concourse.bass as bass
from concourse import mybir

ALU = mybir.AluOpType
ACT = mybir.ActivationFunctionType
F32 = mybir.dt.float32
BF16 = mybir.dt.bfloat16
I32 = mybir.dt.int32
U32 = mybir.dt.uint32
AX_X = mybir.AxisListType.X

P = 128
B, S, D = 2, 512, 128
R = S // P
H, HD = 16, 8
G = 4
NG = H // G
KC = S // P
E = 8
HID = 512
HC = HID // P
SM_SCALE = float(HD) ** -0.5
MASKED = -30000.0

Q_PART = (0, 0, 1, 1, 0, 2)
K_PART = (0, 1, 0, 1, 2, 0)
PROD_ROWS = len(Q_PART) * HD
MASK_ROW = PROD_ROWS
MAX_ROW = MASK_ROW + 3
ROWS = MAX_ROW + 3

IMG = 32

SLOTS0 = B * S
NB = (2 * B * S + E * (P - 1)) // P
CAP = int(1.25 * B * S * 2 / E)
CT = -(-CAP // P)
LAST = CAP - (CT - 1) * P
ZERO_COLS = 2048
DUMP1 = E * CAP

ROW_B1, ROW_B2, ROW_FC, ROW_QKV, ROW_PROJ, ROW_UK, ROW_UV, ROW_ET, ROW_IMG = (
    0, E * HC, 2 * E * HC, 3 * E * HC, 3 * E * HC + 3, 3 * E * HC + 4, 3 * E * HC + 5,
    3 * E * HC + 6, 3 * E * HC + 6 + E)
N_ROWS = ROW_IMG + B


def score_units():
    out = []
    for kc in range(KC):
        heads = 1 if kc < 2 else kc if kc == 2 else 4
        out += [(kc, heads, j) for j in range(0, G, heads)]
    return out


UNITS = score_units()
NU = len(UNITS)
P_RING = 8
LAG = 2


def build(nc, x, cond, mask, attn_w, attn_b, proj_w, proj_b, uk_w, uk_b, uv_w, uv_b,
          et, W1, b1, W2, b2, W3, b3, l1w, gate_w, c_fc, fc_b, c_proj, pr_b, out):
    ctx = ExitStack()
    with ctx:
        def dram(name, shape, dt):
            return nc.dram_tensor(name, shape, dt).ap()

        def sem(name):
            return ctx.enter_context(nc.semaphore(name))

        q_rows_d = [dram(f"q_rows{b}", (MAX_ROW, H, S), BF16) for b in range(B)]
        k_rows_d = [dram(f"k_rows{b}", (ROWS, H, IMG + S), BF16) for b in range(B)]
        x0_d = dram("x0_slots", (E * SLOTS0, D), F32)
        y0_d = dram("y0_slots", (NB * P, D), F32)
        x1_d = dram("x1_slots", (DUMP1 + P, D), F32)
        y1_d = dram("y1_slots", (DUMP1 + P, D), F32)

        def sb(name, shape, dt=F32, stack=ctx):
            return stack.enter_context(nc.sbuf_tensor(name, shape, dt))

        w1_sb = sb("w1_sb", [P, E * HID])
        w2_sb = sb("w2_sb", [P, E * HC * HID])
        w3_sb = sb("w3_sb", [P, E * HC * D])
        b3_sb = sb("b3_sb", [P, E * D])
        x_sb = sb("x_sb", [P, B, R, D])
        a_sb = sb("a_sb", [P, B, R, D])
        ident = sb("ident", [P, P])
        identb = sb("identb", [P, P], BF16)
        tri = sb("tri", [P, P], BF16)
        onesb = sb("onesb", [P, P], BF16)
        cols = sb("cols", [P, N_ROWS])
        projb_bc = sb("projb_bc", [P, D])
        gate_sb = sb("gate_sb", [P, E])
        wc_sb = sb("wc_sb", [P, B, P])
        wcT_sb = sb("wcT_sb", [P, B, P])
        iota_e = sb("iota_e", [P, R, E])
        base0 = sb("base0", [P, E])
        base1 = sb("base1", [P, E])
        tcut = sb("tcut", [P, E, SLOTS0 // P])
        bidx = sb("bidx", [1, NB, E])
        dump = sb("dump", [P, 1])
        lg = sb("lg", [P, B, R, E])
        top_v = sb("top_v", [P, B, R, 8])
        top_i = sb("top_i", [P, B, R, 8], U32)
        top_f = sb("top_f", [P, B, R, 8])
        oh = sb("oh", [P, 2, B, R, E])
        ohsum = sb("ohsum", [P, B, R, E])
        cnt = sb("cnt", [P, 2, B, E])
        cntb = sb("cntb", [P, 2, B, E], BF16)
        rank = sb("rank", [P, 2, B, R, E])
        pick = sb("pick", [P, 2, B, R, E])
        slot_f = sb("slot_f", [P, 2, B, R])
        rank_f = sb("rank_f", [P, 2, B, R])
        keep = sb("keep", [P, 2, B, R])
        slot0 = sb("slot0", [P, 2, B, R], I32)
        slot1 = sb("slot1", [P, 2, B, R], I32)
        p_sb = sb("p_sb", [P, 2, B, R])
        dl = sb("dl", [P, B, R])
        th = sb("th", [P, B, R])
        nbge = sb("nbge", [P, E, SLOTS0 // P])
        nblk = sb("nblk", [P, E])
        cumb = sb("cumb", [P, E])
        shift = sb("shift", [P, E])
        row0 = sb("row0", [P, 2, B, R], I32)
        ended = sb("ended", [1, NB, E])
        endblk = sb("endblk", [1, NB, E])
        tabf = sb("tabf", [1, 5, NB])
        tab = sb("tab", [1, 2, NB], I32)

        upper = w2_sb[:, E * HC * HID // 2:].rearrange("p (n c) -> p n c", c=HID)
        p_ring = upper[:, 0:P_RING, :]
        o_sb = upper[:, P_RING:P_RING + B * NG, :]
        zeros = w3_sb[:, 0:ZERO_COLS]
        res = w3_sb[:, ZERO_COLS:ZERO_COLS + 2 * (IMG + S)].rearrange("p (n c) -> p n c", n=2)
        early = w1_sb[:, 0:4 * HID].rearrange("p (n h c) -> p n h c", n=4, c=32)
        hsel = early[:, 0]
        place = early[:, 1]
        onec = early[:, 2]
        vplace = early[:, 3]
        at_w3 = ZERO_COLS + 2 * (IMG + S)
        uk_sb, uv_sb, ukT, uvT = (w3_sb[:, at_w3 + n * D:at_w3 + (n + 1) * D] for n in range(4))
        at_w1 = 4 * HID + B * (IMG + S)
        lw_sb, sq_sb = (w1_sb[:, at_w1 + n * P:at_w1 + (n + 1) * P] for n in range(2))
        k32 = w1_sb[:, 4 * HID:4 * HID + B * (IMG + S)].rearrange("p (b c) -> p b c", b=B)

        with ExitStack() as at:
            rows_sb = sb("rows_sb", [P, D], F32, at)
            wqkv = sb("wqkv", [P, 3 * D], F32, at)
            vb_bc = sb("vb_bc", [P, D], F32, at)
            proj_sb = sb("proj_sb", [P, D], F32, at)
            cond_bc = sb("cond_bc", [P, B, D], F32, at)
            nrm = sb("nrm", [P, B, 8], F32, at)
            mask_sb = sb("mask_sb", [B, S], F32, at)
            mres = sb("mres", [B, S], F32, at)
            mpart = sb("mpart", [B, 3, S], BF16, at)
            mrowone = sb("mrowone", [H, 3, IMG + S], BF16, at)
            mrowzero = sb("mrowzero", [H, 3, IMG], BF16, at)
            causal_a = sb("causal_a", [P, P], BF16, at)
            causal_b = sb("causal_b", [P, P], BF16, at)
            hmask = sb("hmask", [P, H], F32, at)
            xT = sb("xT", [P, B, S], F32, at)
            q32 = sb("q32", [P, B, S], F32, at)
            part = sb("part", [P, 2, 3, IMG + S], BF16, at)
            v_sb = sb("v_sb", [P, B, KC, H, HD + 1], F32, at)
            vimg = sb("vimg", [P, B], F32, at)
            kimg_bd = sb("kimg_bd", [P, B, H], F32, at)
            vimg_bd = sb("vimg_bd", [P, B, H, 32], F32, at)
            simg = sb("simg", [P, B, KC, H], F32, at)
            pimg = sb("pimg", [P, 2, S], F32, at)
            mA = sb("mA", [P, B, KC, H], F32, at)
            negm = sb("negm", [P, KC, G], F32, at)
            mr = sb("mr", [P, KC, G], F32, at)
            mp = sb("mp", [P, KC, 3, G], BF16, at)
            mrow = sb("mrow", [3 * G, 2, S], BF16, at)
            qa = sb("qa", [MAX_ROW, 2, G, S], BF16, at)
            ka = sb("ka", [MAX_ROW, 2, G, IMG + S], BF16, at)
            qb = sb("qb", [ROWS, 2, G, S], BF16, at)
            kb = sb("kb", [ROWS, 2, G, IMG + S], BF16, at)
            rden = sb("rden", [P, H], F32, at)
            on_sb = sb("on_sb", [P, 2, H, HD], F32, at)
            onT = sb("onT", [P, B, R, P], F32, at)
            aT = sb("aT", [P, B, R, P], F32, at)

        fc_sb = sb("fc_sb", [P, E, HID])
        cp_sb = sb("cp_sb", [P, E, HC, D])
        prb_sb = sb("prb_sb", [P, E, D])
        xg = sb("xg", [P, 2, D])
        xgT = sb("xgT", [P, 2, P])
        h1p = sb("h1p", [P, HID])
        h1T = sb("h1T", [P, 2, HC, P])
        h2p = sb("h2p", [P, HID])
        h2T = sb("h2T", [P, 2, HC, P])
        y_sb = sb("y_sb", [P, 2, D])
        back = sb("back", [P, B, R, 2, D])
        xcT = sb("xcT", [P, B, R, P])
        tg = sb("tg", [P, 2, CT, D])
        tgT = sb("tgT", [P, 2, CAP])
        hT = sb("hT", [P, 2, HC, CAP])
        z_sb = sb("z_sb", [P, 2, CT, D])
        r_sb = sb("r_sb", [P, B, R, D])

        def sems(names):
            return [sem(n) for n in names.split()]

        (x_in, rows_in, wqkv_in, uk_in, cond_in, mask_in, misc_in, w1_in, w2_in, w3_in, w2b_in, l1w_in,
         zero_out, const_out) = sems(
            "x_in rows_in wqkv_in uk_in cond_in mask_in misc_in w1_in w2_in w3_in w2b_in l1w_in "
            "zero_out const_out")
        pool_step, dve_step, act_step, consts, zeroed = sems("pool_step dve_step act_step consts zeroed")
        (xT_done, xT_ready, cols_done, cols_ready, img_done, img_ready, qkv_done, qkv_ready, hi_ready,
         mid_ready, parts_ready, v_done, v_ready, simg_done, simg_ready, vimg_done, vimg_ready,
         var_ready, sqrt_ready, wc_ready, wcT_done, wcT_ready, mask_ready, kbd_ready, vplace_ready) = sems(
            "xT_done xT_ready cols_done cols_ready img_done img_ready qkv_done qkv_ready hi_ready "
            "mid_ready parts_ready v_done v_ready simg_done simg_ready vimg_done vimg_ready "
            "var_ready sqrt_ready wc_ready wcT_done wcT_ready mask_ready kbd_ready vplace_ready")
        rows_out = [sem(f"rows_out{n}") for n in range(2 * B)]
        krest_out = [sem(f"krest_out{b}") for b in range(B)]
        a_done, a_used, m_parts, s_done, exp_done, pv_done, o_ready, cnt_ready, slot_ready, tab_ready, row0_ready = sems(
            "a_done a_used m_parts s_done exp_done pv_done o_ready cnt_ready slot_ready tab_ready row0_ready")
        qka_in = [sem(f"qka_in{n}") for n in range(2)]
        qkb_in = [sem(f"qkb_in{n}") for n in range(2)]
        sent0, tx_done, xgT_ready, mm1_done, h1p_ready, tr1_done, h1T_ready, mm2_done, h2p_ready, \
            tr2_done, h2T_ready, mm3_done, y_ready = sems(
                "sent0 tx_done xgT_ready mm1_done h1p_ready tr1_done h1T_ready mm2_done h2p_ready "
                "tr2_done h2T_ready mm3_done y_ready")
        xg_in = [sem(f"xg_in{n}") for n in range(2)]
        y_out = [sem(f"y_out{n}") for n in range(2)]
        back_in = [sem(f"back_in{n}") for n in range(B * R)]
        x1_ready, xc_done, xc_ready, lg_done, lg_ready, cnt1_ready, rank1_done, slot1_ready, dl_ready, \
            th_ready, sent1 = sems(
                "x1_ready xc_done xc_ready lg_done lg_ready cnt1_ready rank1_done slot1_ready dl_ready "
                "th_ready sent1")
        tt_done, tgT_ready, fc_done, hT_ready, z_done, z_ready, r_ready, out_sent = sems(
            "tt_done tgT_ready fc_done hT_ready z_done z_ready r_ready out_sent")
        tg_in = [sem(f"tg_in{n}") for n in range(2)]
        z_out = [sem(f"z_out{n}") for n in range(2)]
        back1_in = [sem(f"back1_in{n}") for n in range(B * R)]

        def stepper(eng, stepped):
            steps = 0

            def step(ins):
                nonlocal steps
                steps += 1
                ins.then_inc(stepped, 1)
                eng.wait_ge(stepped, steps)

            return step

        groups = B * NG

        def a_pieces(n):
            out = [("score", n, t, hp) for t in range(KC) for hp in range(G // 2)] if n < groups else []
            if 1 <= n <= groups:
                out.insert(2, ("maxT", n - 1))
            return out

        def s_pieces(n):
            return [("s", n, k) for k in range(NU + 1)]

        def chunk_units(kc):
            return [k + 1 for k, u in enumerate(UNITS) if u[0] == kc]

        def b_pieces():
            out = [[] for _ in range(groups + 1)]
            for c in range(groups * KC + 1):
                n, kc = divmod(c, KC)
                if c < groups * KC:
                    units = ([0] if kc == 0 else []) + chunk_units(kc)
                    out[n] += [("s", n, k) for k in units]
                if c:
                    out[n] += [("pv", *divmod(c - 1, KC))]
            out[groups - 1] += out.pop()
            return out

        def tail(b):
            out = [("on", b, 0), ("on", b, 1), ("onT", b, 0), ("on", b, 2), ("onT", b, 1), ("on", b, 3),
                   ("onT", b, 2), ("onT", b, 3)]
            return out + [("aT", b), ("route", b), ("a", b), ("count", b)]

        def merged(one, two):
            at = sorted([((i + 0.5) / len(one), 0, p) for i, p in enumerate(one)]
                        + [((i + 0.5) / len(two), 1, p) for i, p in enumerate(two)], key=lambda q: q[:2])
            return [p for _, _, p in at]

        by_group = b_pieces()
        schedule = []
        for n in range(groups + LAG):
            first = a_pieces(n) if n < groups + 1 else []
            if n == groups + LAG - 1:
                first = first + tail(0)
            schedule += merged(first, by_group[n - LAG] if n >= LAG else [])
        schedule += tail(1) + [("total",)]
        a_order = [p for p in schedule if p[0] not in ("s", "pv")]
        a_at = {p: i for i, p in enumerate(a_order)}

        pair = [ctx.enter_context(nc.psum_tensor(f"pair{n}", [P, 2, 512], F32)) for n in range(2)]
        single = [ctx.enter_context(nc.psum_tensor(f"bank{n}", [P, 512], F32)) for n in range(4, 8)]

        def bank(n):
            return pair[n // 2][:, n % 2, :] if n < 4 else single[n - 4][:, :]

        def a_bank(piece):
            return pair[a_at[piece] % 2]

        def s_index(n, k):
            return n * (NU + 1) + k

        def p_index(n, k):
            return n * NU + k - 1

        def chunk_of(w):
            n, k = divmod(w, NU)
            return n * KC + UNITS[k][0]

        block = ctx.enter_context(nc.Block())

        @block.sync
        def _(sp):
            sp.dma_start(x_sb[:, :, :, :], x.rearrange("b (p r) d -> p b r d", r=R)).then_inc(x_in, 16)
            for at_row, n, src in (
                    (ROW_B1, E * HC, b1.rearrange("e (c p) -> (e c) p", p=P)),
                    (ROW_B2, E * HC, b2.rearrange("e (c p) -> (e c) p", p=P)),
                    (ROW_FC, E * HC, fc_b.rearrange("e o (c p) -> (e o c) p", p=P)),
                    (ROW_QKV, 3, attn_b.rearrange("(c p) -> c p", p=P)),
                    (ROW_PROJ, 1, proj_b.rearrange("(c p) -> c p", p=P)),
                    (ROW_UK, 1, uk_b.rearrange("(c p) -> c p", p=P)),
                    (ROW_UV, 1, uv_b.rearrange("(c p) -> c p", p=P)),
                    (ROW_ET, E, et),
                    (ROW_IMG, B, cond)):
                sp.dma_start(rows_sb[at_row:at_row + n, :], src).then_inc(rows_in, 16)

            def store_parts(b):
                for i in range(2):
                    n = 2 * b + i
                    sp.wait_ge(parts_ready, n + 1)
                    rows, which = (k_rows_d[b], K_PART) if i else (q_rows_d[b], Q_PART)
                    width = IMG + S if i else S
                    for c, m in enumerate(which):
                        sp.dma_start(rows[c * HD:(c + 1) * HD].rearrange("d h t -> h d t"),
                                     part[:, i, m, 0:width]).then_inc(rows_out[n], 16)

            sp.wait_ge(consts, 1)
            for b in range(B):
                sp.dma_start(q_rows_d[b][MASK_ROW:MAX_ROW].rearrange("r h t -> h r t"),
                             mrowone[:, :, IMG:]).then_inc(krest_out[b], 16)
                sp.dma_start(k_rows_d[b][MAX_ROW:ROWS].rearrange("r h t -> h r t"),
                             mrowone[:, :, :]).then_inc(krest_out[b], 16)
                sp.dma_start(k_rows_d[b][MASK_ROW:MAX_ROW, :, 0:IMG].rearrange("r h t -> h r t"),
                             mrowzero[:, :, :]).then_inc(krest_out[b], 16)
            sp.wait_ge(mask_ready, 1)
            for b in range(B):
                for m in range(3):
                    sp.dma_start(k_rows_d[b][MASK_ROW + m:MASK_ROW + m + 1, :, IMG:],
                                 mpart[b:b + 1, m:m + 1, :].broadcast_to([1, H, S])
                                 ).then_inc(krest_out[b], 16)

            def rows_stored(b):
                sp.wait_ge(rows_out[2 * b], 16 * len(Q_PART))
                sp.wait_ge(rows_out[2 * b + 1], 16 * len(K_PART))
                sp.wait_ge(krest_out[b], 16 * 6)

            def load_a(n):
                b, g = divmod(n, NG)
                if n >= 2:
                    sp.wait_ge(a_done, a_at[("score", n - 2, KC - 1, G // 2 - 1)] + 1)
                sp.dma_start(qa[:, n % 2], q_rows_d[b][:, g * G:(g + 1) * G, :]).then_inc(qka_in[n % 2], 16)
                sp.dma_start(ka[:, n % 2], k_rows_d[b][0:MAX_ROW, g * G:(g + 1) * G, :]
                             ).then_inc(qka_in[n % 2], 16)

            def load_b(n):
                b, g = divmod(n, NG)
                if n >= 2:
                    sp.wait_ge(s_done, s_index(n - 1, 0))
                sp.dma_start(qb[0:MAX_ROW, n % 2], q_rows_d[b][:, g * G:(g + 1) * G, :]
                             ).then_inc(qkb_in[n % 2], 16)
                sp.dma_start(kb[:, n % 2], k_rows_d[b][:, g * G:(g + 1) * G, :]).then_inc(qkb_in[n % 2], 16)
                sp.wait_ge(a_used, a_at[("maxT", n)] + 1)
                for m in range(3):
                    sp.dma_start(qb[MAX_ROW + m:MAX_ROW + m + 1, n % 2], mrow[m * G:(m + 1) * G, n % 2, :]
                                 ).then_inc(qkb_in[n % 2], 16)

            store_parts(0)
            rows_stored(0)
            load_a(0)
            load_a(1)
            store_parts(1)
            rows_stored(1)
            for n in range(groups):
                if n + 2 < groups:
                    load_a(n + 2)
                load_b(n)

            def load_block(i, s):
                first = sp.value_load(tab[0:1, 1, bass.ds(i, 1)], min_val=0, max_val=E * SLOTS0 - P)
                sp.dma_start(xg[:, s, :], x0_d[bass.ds(first, P), :]).then_inc(xg_in[s], 16)

            def store_block(i, s):
                sp.wait_ge(y_ready, i + 1)
                sp.dma_start(y0_d[bass.ds(i * P, P), :], y_sb[:, s, :]).then_inc(y_out[s], 16)

            sp.wait_ge(tab_ready, 1)
            sp.wait_ge(a_used, len(a_order))
            sp.wait_ge(sent0, 16 * B * R * 2)
            load_block(0, 0)
            load_block(1, 1)
            for i in range(NB):
                if i + 2 < NB:
                    sp.wait_ge(tx_done, i + 1)
                    load_block(i + 2, i % 2)
                if i >= 2:
                    store_block(i - 2, i % 2)
            store_block(NB - 2, (NB - 2) % 2)
            store_block(NB - 1, (NB - 1) % 2)

            def load_expert(e):
                if e >= 2:
                    sp.wait_ge(tt_done, e - 1)
                whole = e * CAP + (CT - 1) * P
                sp.dma_start(tg[:, e % 2, 0:CT - 1], x1_d[e * CAP:whole, :]
                             .rearrange("(c p) d -> p c d", p=P)).then_inc(tg_in[e % 2], 16)
                sp.dma_start(tg[0:LAST, e % 2, CT - 1], x1_d[whole:whole + LAST, :]
                             ).then_inc(tg_in[e % 2], 16)

            def store_expert(e):
                sp.wait_ge(z_ready, e + 1)
                whole = e * CAP + (CT - 1) * P
                sp.dma_start(y1_d[e * CAP:whole, :].rearrange("(c p) d -> p c d", p=P),
                             z_sb[:, e % 2, 0:CT - 1, :]).then_inc(z_out[e % 2], 16)
                sp.dma_start(y1_d[whole:whole + LAST, :], z_sb[0:LAST, e % 2, CT - 1, :]
                             ).then_inc(z_out[e % 2], 16)

            sp.wait_ge(sent1, 16 * B * R * 2)
            load_expert(0)
            load_expert(1)
            for e in range(E):
                if e + 2 < E:
                    load_expert(e + 2)
                store_expert(e)
            for b in range(B):
                sp.wait_ge(r_ready, R * (b + 1))
                sp.dma_start(out[b].rearrange("(p r) d -> p r d", r=R), r_sb[:, b]).then_inc(out_sent, 16)
            sp.wait_ge(out_sent, 16 * B)

        @block.gpsimd
        def _(pool):
            step = stepper(pool, pool_step)
            for t, v in ((ident, 0.0), (identb, 0.0), (causal_a, 0.0), (causal_b, 0.0), (tri, 1.0),
                         (onesb, 1.0), (hmask, 1.0)):
                last = pool.memset(t[:, :], v)
            pool.memset(mrowzero[:, :, :], 0.0)
            pool.memset(mrowone[:, :, :], 1.0)
            step(pool.memset(early[:, 0:3], 0.0))
            pool.affine_select(out=ident[:, :], in_=ident[:, :], compare_op=ALU.not_equal, fill=1.0, base=0,
                               pattern=[[-1, P]], channel_multiplier=1)
            pool.affine_select(out=identb[:, :], in_=identb[:, :], compare_op=ALU.not_equal, fill=1.0,
                               base=0, pattern=[[-1, P]], channel_multiplier=1)
            pool.affine_select(out=causal_a[:, :], in_=causal_a[:, :], compare_op=ALU.is_ge, fill=MASKED,
                               base=0, pattern=[[-1, P]], channel_multiplier=1)
            pool.affine_select(out=causal_b[:, :], in_=causal_b[:, :], compare_op=ALU.is_ge, fill=MASKED,
                               base=0, pattern=[[1, P]], channel_multiplier=-1)
            pool.affine_select(out=tri[:, :], in_=tri[:, :], compare_op=ALU.is_ge, fill=0.0, base=-1,
                               pattern=[[1, P]], channel_multiplier=-1)
            pool.memset(mrowone[:, :, 1:IMG], 0.0)
            step(pool.affine_select(out=hmask[:, :], in_=hmask[:, :], compare_op=ALU.is_ge, fill=0.0,
                                    base=0, pattern=[[-HD, H]], channel_multiplier=1))
            step(pool.affine_select(out=hmask[:, :], in_=hmask[:, :], compare_op=ALU.is_ge, fill=0.0,
                                    base=HD - 1, pattern=[[HD, H]], channel_multiplier=-1))
            pool.tensor_copy(hsel[:, :, 0], hmask[:, :])
            pool.affine_select(out=place[:, :, 0:HD], in_=place[:, :, 0:HD], compare_op=ALU.not_equal,
                               fill=1.0, base=0, pattern=[[-HD, H], [-1, HD]], channel_multiplier=1)
            at_one = onec[:, :, HD].rearrange("p (g j) -> p g j", j=G)
            pool.affine_select(out=at_one, in_=at_one, compare_op=ALU.not_equal, fill=1.0, base=0,
                               pattern=[[0, NG], [-32, G]], channel_multiplier=1)
            any_f = {"allow_small_or_imprecise_dtypes": True}
            pool.iota(iota_e[:, :, :], [[0, R], [1, E]], base=0, channel_multiplier=0, **any_f)
            pool.iota(base0[:, :], [[SLOTS0, E]], base=0, channel_multiplier=0, **any_f)
            pool.iota(base1[:, :], [[CAP, E]], base=0, channel_multiplier=0, **any_f)
            pool.iota(tcut[:, :, :], [[0, E], [P, SLOTS0 // P]], base=0, channel_multiplier=0, **any_f)
            pool.iota(bidx[:, :, :], [[1, NB], [0, E]], base=0, channel_multiplier=0, **any_f)
            pool.iota(dump[:, :], [[0, 1]], base=DUMP1, channel_multiplier=1, **any_f).then_inc(consts, 1)

            pool.wait_ge(zeroed, 1)
            width = ZERO_COLS // D
            x0_clear = x0_d.rearrange("(n p w) d -> n p (w d)", p=P, w=width)
            for n in range(E * SLOTS0 // P // width):
                pool.dma_start(x0_clear[n], zeros).then_inc(zero_out, 16)
            x1_clear = x1_d[0:DUMP1].rearrange("(p w) d -> p (w d)", p=P)
            half = DUMP1 // P * D // 2
            for n in range(2):
                pool.dma_start(x1_clear[:, n * half:(n + 1) * half], zeros[:, 0:half]).then_inc(zero_out, 16)
            pool.dma_start(x1_d[DUMP1:, :], zeros[:, 0:D]).then_inc(zero_out, 16)
            pool.dma_start(y1_d[DUMP1:, :], zeros[:, 0:D]).then_inc(zero_out, 16)
            n_clear = E * SLOTS0 // P // width + 4

            pool.wait_ge(rows_out[2 * B - 1], 16 * len(K_PART))
            for k in range(HC):
                pool.dma_start(w2_sb[:, 0:E * HC * HID // 2].rearrange("p (e c n) -> p e c n", c=HC, n=HID)
                               [:, k], W2[k].rearrange("(c p) n -> p c n", p=P)).then_inc(w2_in, 16)
            pool.wait_ge(vimg_ready, B)
            pool.wait_ge(wc_ready, 1)
            pool.dma_start(w1_sb[:, :].rearrange("p (e n) -> p e n", e=E), W1.rearrange("e p n -> p e n")
                           ).then_inc(w1_in, 16)
            pool.wait_ge(zero_out, 16 * n_clear)
            pool.dma_start(w3_sb[:, :].rearrange("p (q n) -> p q n", n=D),
                           W3.rearrange("e (c p) n -> p (e c) n", p=P)).then_inc(w3_in, 16)
            pool.dma_start(b3_sb[:, :], b3.rearrange("e d -> (e d)").partition_broadcast(P)
                           ).then_inc(w3_in, 16)

            def dispatch(b, rows, slots, dst, signal):
                for r in range(R):
                    for k in range(2):
                        pool.indirect_dma_start(
                            dst, bass.IndirectOffsetOnAxis(ap=slots[:, k, b, r:r + 1], axis=0),
                            rows[:, b, r, :], None).then_inc(signal, 16)

            pool.wait_ge(slot_ready, 1)
            dispatch(0, a_sb, slot0, x0_d, sent0)
            pool.wait_ge(a_done, a_at[("on", B - 1, R - 1)] + 1)
            for k in range(HC):
                pool.dma_start(w2_sb[:, E * HC * HID // 2:].rearrange("p (e c n) -> p e c n", c=HC, n=HID)
                               [:, k], W2[HC + k].rearrange("(c p) n -> p c n", p=P)).then_inc(w2b_in, 16)
            pool.wait_ge(slot_ready, 2)
            dispatch(1, a_sb, slot0, x0_d, sent0)
            pool.wait_ge(a_used, len(a_order))
            pool.dma_start(fc_sb[:, :, :], c_fc.rearrange("e p n -> p e n")).then_inc(l1w_in, 16)
            pool.dma_start(cp_sb[:, :, :, :], c_proj.rearrange("e (c p) n -> p e c n", p=P)
                           ).then_inc(l1w_in, 16)
            pool.dma_start(prb_sb[:, :, :].rearrange("p e d -> p (e d)"),
                           pr_b.rearrange("e o d -> (e o d)").partition_broadcast(P)).then_inc(l1w_in, 16)

            def collect(slots, src, signals):
                for b in range(B):
                    for r in range(R):
                        for k in range(2):
                            pool.indirect_dma_start(
                                back[:, b, r, k, :], None, src,
                                bass.IndirectOffsetOnAxis(ap=slots[:, k, b, r:r + 1], axis=0)
                            ).then_inc(signals[b * R + r], 16)

            for s in range(2):
                pool.wait_ge(y_out[s], 16 * ((NB - s + 1) // 2))
            pool.wait_ge(row0_ready, 1)
            collect(row0, y0_d, back_in)
            pool.wait_ge(slot1_ready, 1)
            for b in range(B):
                dispatch(b, a_sb, slot1, x1_d, sent1)
            for s in range(2):
                pool.wait_ge(z_out[s], 32 * (E // 2))
            collect(slot1, y1_d, back1_in)

        @block.scalar
        def _(act):
            act.dma_start(wqkv[:, :], attn_w).then_inc(wqkv_in, 16)
            act.dma_start(uk_sb, uk_w).then_inc(uk_in, 16)
            act.dma_start(uv_sb, uv_w).then_inc(uk_in, 16)
            act.dma_start(vb_bc[:, :], attn_b[2 * D:3 * D].partition_broadcast(P)).then_inc(misc_in, 16)
            act.dma_start(lw_sb, l1w.rearrange("a o i c -> (a o) (i c)")).then_inc(cond_in, 16)
            for b in range(B):
                act.dma_start(cond_bc[:, b, :], cond[b].partition_broadcast(P)).then_inc(cond_in, 16)
            act.dma_start(mask_sb[:, :], mask.rearrange("b i j s -> (b i j) s")).then_inc(mask_in, 16)
            act.dma_start(proj_sb[:, :], proj_w).then_inc(misc_in, 16)
            act.dma_start(projb_bc[:, :], proj_b.partition_broadcast(P)).then_inc(misc_in, 16)
            act.dma_start(gate_sb[:, :], gate_w).then_inc(misc_in, 16)
            act.wait_ge(var_ready, 1)
            act.activation(nrm[:, :, 2], nrm[:, :, 1], ACT.Sqrt).then_inc(sqrt_ready, 1)
            for n in range(2 * B):
                b, i = divmod(n, 2)
                w = IMG + S if i else S
                src = k32[:, b, :] if i else q32[:, b, :]
                act.wait_ge(qkv_ready, n + 1)
                if n >= 2:
                    act.wait_ge(rows_out[n - 2], 16 * len(Q_PART))
                act.copy(part[:, i, 0, 0:w], src).then_inc(hi_ready, 1)
                act.wait_ge(mid_ready, n + 1)
                act.copy(part[:, i, 1, 0:w], res[:, i, 0:w]).then_inc(act_step, 1)

            for piece in schedule:
                if piece[0] != "s":
                    continue
                _, n, k = piece
                v = s_index(n, k)
                act.wait_ge(s_done, v + 1)
                if k == 0:
                    if n >= 2:
                        act.wait_ge(pv_done, (n - 2) * KC + 1)
                    act.activation(pimg[:, n % 2, :], bank(4 + v % 3), ACT.Exp).then_inc(exp_done, 1)
                    continue
                w = p_index(n, k)
                if w >= P_RING:
                    act.wait_ge(pv_done, chunk_of(w - P_RING) + 1)
                kc, heads, _ = UNITS[k - 1]
                width = heads * (S - kc * P)
                act.activation(p_ring[:, w % P_RING, 0:width], bank(4 + v % 3)[:, 0:width], ACT.Exp
                               ).then_inc(exp_done, 1)

            def gelu1(i, s, e):
                act.wait_ge(tr1_done, i + 1)
                if not isinstance(i, int) or i >= 2:
                    act.wait_ge(mm2_done, i - 1)
                for c in range(HC):
                    ins = act.activation(h1T[:, s, c, :], bank(2)[:, c * P:(c + 1) * P], ACT.Gelu,
                                         bias=cols[:, bass.ds(e * HC + (ROW_B1 + c), 1)])
                ins.then_inc(h1T_ready, 1)

            def gelu2(i, s, e):
                act.wait_ge(tr2_done, i + 1)
                if not isinstance(i, int) or i >= 2:
                    act.wait_ge(mm3_done, i - 1)
                for c in range(HC):
                    ins = act.activation(h2T[:, s, c, :], bank(4)[:, c * P:(c + 1) * P], ACT.Gelu,
                                         bias=cols[:, bass.ds(e * HC + (ROW_B2 + c), 1)])
                ins.then_inc(h2T_ready, 1)

            act.wait_ge(tab_ready, 1)

            def expert(i):
                return act.value_load(tab[0:1, 0, bass.ds(i, 1)], min_val=0, max_val=E - 1)

            gelu1(0, 0, expert(0))
            for i in range(NB):
                if i + 1 < NB:
                    gelu1(i + 1, (i + 1) % 2, expert(i + 1))
                gelu2(i, i % 2, expert(i))

            act.wait_ge(dl_ready, 1)
            act.activation(th[:, :, :], dl[:, :, :], ACT.Tanh, scale=0.5).then_inc(th_ready, 1)
            for e in range(E):
                for c in range(HC):
                    act.wait_ge(fc_done, e * HC + c + 1)
                    if e >= 2 and c == 0:
                        act.wait_ge(z_done, e - 1)
                    act.activation(hT[:, e % 2, c, :], bank(2 + c % 2)[:, 0:CAP], ACT.Gelu,
                                   bias=cols[:, ROW_FC + e * HC + c:ROW_FC + e * HC + c + 1]
                                   ).then_inc(hT_ready, 1)

        @block.tensor
        def _(pe):
            mm, tr = pe.matmul, pe.transpose
            pe.wait_ge(consts, 1)
            pe.wait_ge(x_in, 16)
            for b in range(B):
                for r in range(R):
                    ins = tr(bank(b)[:, r * P:(r + 1) * P], x_sb[:, b, r, :], ident[:, :])
                ins.then_inc(xT_done, 1)
            pe.wait_ge(rows_in, 16 * 9)
            pe.wait_ge(uk_in, 32)
            tr(bank(2)[:, 0:N_ROWS], rows_sb[0:N_ROWS, :], ident[0:N_ROWS, 0:N_ROWS])
            tr(bank(2)[:, P:2 * P], uk_sb, ident[:, :])
            tr(bank(2)[:, 2 * P:3 * P], uv_sb, ident[:, :]).then_inc(cols_done, 1)
            pe.wait_ge(xT_ready, 1)
            pe.wait_ge(wqkv_in, 16)
            mm(bank(4), wqkv[:, 0:D], xT[:, 0, :], start=True, stop=True).then_inc(qkv_done, 1)
            mm(bank(5), wqkv[:, D:2 * D], xT[:, 0, :], start=True, stop=True).then_inc(qkv_done, 1)
            pe.wait_ge(cols_ready, 1)
            mm(bank(3)[:, 0:B], ukT, cols[:, ROW_IMG:ROW_IMG + B], start=True, stop=True)
            mm(bank(3)[:, B:2 * B], uvT, cols[:, ROW_IMG:ROW_IMG + B], start=True, stop=True
               ).then_inc(img_done, 1)
            pe.wait_ge(xT_ready, 2)
            mm(bank(6), wqkv[:, 0:D], xT[:, 1, :], start=True, stop=True).then_inc(qkv_done, 1)
            mm(bank(7), wqkv[:, D:2 * D], xT[:, 1, :], start=True, stop=True).then_inc(qkv_done, 1)
            for b in range(B):
                for kc in range(KC):
                    ins = mm(bank(b)[:, kc * P:(kc + 1) * P], xT[:, b, kc * P:(kc + 1) * P],
                             wqkv[:, 2 * D:3 * D], start=True, stop=True)
                ins.then_inc(v_done, 1)
            for b in range(B):
                pe.wait_ge(vplace_ready, b + 1)
                for g in range(NG):
                    ins = mm(bank(3)[:, g * P:(g + 1) * P],
                             hsel[:, g * G:(g + 1) * G, :].rearrange("p h c -> p (h c)"),
                             vplace[:, g * G:(g + 1) * G, :].rearrange("p h c -> p (h c)"),
                             start=True, stop=True)
                ins.then_inc(vimg_done, 1)
            pe.wait_ge(kbd_ready, 1)
            for b in range(B):
                pe.wait_ge(qkv_ready, 2 * b + 1)
                for t in range(KC):
                    at_c = (b * KC + t) * H
                    ins = mm(bank(2)[:, at_c:at_c + H], q32[:, b, t * P:(t + 1) * P], kimg_bd[:, b, :],
                             start=True, stop=True)
            ins.then_inc(simg_done, 1)
            pe.wait_ge(wc_ready, 1)
            pe.wait_ge(vimg_ready, B)
            for b in range(B):
                ins = tr(bank(3)[:, b * P:(b + 1) * P], wc_sb[:, b, :], ident[:, :])
            ins.then_inc(wcT_done, 1)
            pe.wait_ge(v_ready, B)
            pe.wait_ge(simg_ready, 1)
            pe.wait_ge(wcT_ready, 1)
            pe.wait_ge(qkv_ready, 2 * B)

            def score(n, t, hp):
                b, g = divmod(n, NG)
                pe.wait_ge(qka_in[n % 2], 32 * (n // 2 + 1))
                n_keys = (t + 1) * P
                for i in range(2):
                    j = 2 * hp + i
                    to = a_bank(("score", n, t, hp))[:, i, :]
                    mm(to[:, 0:n_keys], qa[:, n % 2, j, t * P:(t + 1) * P],
                       ka[:, n % 2, j, IMG:IMG + n_keys], start=True, stop=False)
                    ins = mm(to[:, t * P:n_keys], identb[:, :], causal_a[:, :], start=False, stop=True)
                return ins

            def second_scores(n, k):
                v = s_index(n, k)
                to = bank(4 + v % 3)
                if v >= 3:
                    pe.wait_ge(exp_done, v - 2)
                if k == 0:
                    pe.wait_ge(qkb_in[n % 2], 80 * (n // 2 + 1))
                    for j in range(G):
                        ins = mm(to[32 * j:32 * (j + 1), :], kb[:, n % 2, j, 0:IMG], qb[:, n % 2, j, :],
                                 start=True, stop=True, tile_position=(0, 32 * j))
                    return ins
                kc, heads, j0 = UNITS[k - 1]
                width = S - kc * P
                for i in range(heads):
                    mm(to[:, i * width:(i + 1) * width],
                       kb[:, n % 2, j0 + i, IMG + kc * P:IMG + (kc + 1) * P], qb[:, n % 2, j0 + i, kc * P:],
                       start=True, stop=False, skip_group_check=True)
                    ins = mm(to[:, i * width:i * width + P], identb[:, :], causal_b[:, :],
                             start=False, stop=True, skip_group_check=True)
                return ins

            def values(n, kc):
                b, g = divmod(n, NG)
                pe.wait_ge(exp_done, s_index(n, chunk_units(kc)[-1]) + 1)
                if kc == 0:
                    if n:
                        pe.wait_ge(o_ready, n)
                    mm(bank(7), vimg_bd[:, b, g * G:(g + 1) * G, :].rearrange("p h c -> p (h c)"),
                       pimg[:, n % 2, :], start=True, stop=False, skip_group_check=True)
                width = S - kc * P
                for k in chunk_units(kc):
                    _, heads, j0 = UNITS[k - 1]
                    w = p_index(n, k)
                    for i in range(heads):
                        j = j0 + i
                        ins = mm(bank(7)[32 * j:32 * j + HD + 1, kc * P:], v_sb[:, b, kc, g * G + j, :],
                                 p_ring[:, w % P_RING, i * width:(i + 1) * width], start=False,
                                 stop=(kc == KC - 1), tile_position=(0, 32 * j), skip_group_check=True)
                return ins

            for piece in schedule:
                kind, *arg = piece
                if kind == "s":
                    second_scores(*arg).then_inc(s_done, 1)
                    continue
                if kind == "pv":
                    values(*arg).then_inc(pv_done, 1)
                    continue
                if a_at[piece] >= 2:
                    pe.wait_ge(a_used, a_at[piece] - 1)
                to = a_bank(piece)[:, 0, :]
                if kind == "score":
                    ins = score(*arg)
                elif kind == "maxT":
                    pe.wait_ge(m_parts, arg[0] + 1)
                    to = to.bitcast(BF16)
                    for t in range(KC):
                        ins = tr(to[0:3 * G, t * P:(t + 1) * P], mp[:, t, :, :].rearrange("p m h -> p (m h)"),
                                 identb[:, :])
                elif kind == "on":
                    b, r = arg
                    pe.wait_ge(o_ready, (b + 1) * NG)
                    for g in range(NG):
                        ins = tr(to[:, g * P:(g + 1) * P], o_sb[:, b * NG + g, r::R], ident[:, :])
                elif kind == "onT":
                    b, r = arg
                    pe.wait_ge(a_used, a_at[("on", b, r)] + 1)
                    ins = tr(to[:, 0:P], on_sb[:, r % 2].rearrange("p h d -> p (h d)"), ident[:, :])
                elif kind == "aT":
                    b, = arg
                    pe.wait_ge(misc_in, 64)
                    pe.wait_ge(a_used, a_at[("onT", b, R - 1)] + 1)
                    ins = mm(to, proj_sb[:, :], onT[:, b].rearrange("p r q -> p (r q)"), start=True, stop=True)
                elif kind == "a":
                    b, = arg
                    for r in range(R):
                        ins = mm(to[:, r * P:(r + 1) * P], onT[:, b, r, :], proj_sb[:, :], start=True,
                                 stop=True)
                elif kind == "route":
                    b, = arg
                    pe.wait_ge(a_used, a_at[("aT", b)] + 1)
                    for r in range(R):
                        ins = mm(to[:, r * E:(r + 1) * E], aT[:, b, r, :], cols[:, ROW_ET:ROW_ET + E],
                                 start=True, stop=True)
                elif kind == "count":
                    b, = arg
                    pe.wait_ge(cnt_ready, b + 1)
                    ins = mm(to[:, 0:E], tri[:, :], cntb[:, 0, b, :], start=True, stop=(b == 0))
                    for b_ in range(b):
                        ins = mm(to[:, 0:E], onesb[:, :], cntb[:, 0, b_, :], start=False, stop=(b_ == b - 1))
                else:
                    for b in range(B):
                        ins = mm(to[:, 0:E], onesb[:, :], cntb[:, 0, b, :], start=(b == 0), stop=(b == B - 1))
                ins.then_inc(a_done, 1)

            def expert(i):
                return pe.value_load(tab[0:1, 0, bass.ds(i, 1)], min_val=0, max_val=E - 1)

            def transpose_x(i, s):
                pe.wait_ge(xg_in[s], 16 * (i // 2 + 1))
                if i:
                    pe.wait_ge(xgT_ready, i)
                tr(bank(0)[:, 0:P], xg[:, s, :], ident[:, :]).then_inc(tx_done, 1)

            def first_layer(i, s):
                e = expert(i)
                pe.wait_ge(xgT_ready, i + 1)
                if i:
                    pe.wait_ge(h1p_ready, i)
                mm(bank(1), xgT[:, s, :], w1_sb[:, bass.ds(e * HID, HID)], start=True, stop=True
                   ).then_inc(mm1_done, 1)

            def transpose_1(i, s):
                pe.wait_ge(h1p_ready, i + 1)
                if i:
                    pe.wait_ge(h1T_ready, i)
                for c in range(HC):
                    ins = tr(bank(2)[:, c * P:(c + 1) * P], h1p[:, c * P:(c + 1) * P], ident[:, :])
                ins.then_inc(tr1_done, 1)

            def second_layer(i, s):
                e = expert(i)
                pe.wait_ge(h1T_ready, i + 1)
                if i:
                    pe.wait_ge(h2p_ready, i)
                for c in range(HC):
                    ins = mm(bank(3), h1T[:, s, c, :], w2_sb[:, bass.ds(e * (HC * HID) + c * HID, HID)],
                             start=(c == 0), stop=(c == HC - 1))
                ins.then_inc(mm2_done, 1)

            def transpose_2(i, s):
                pe.wait_ge(h2p_ready, i + 1)
                if i:
                    pe.wait_ge(h2T_ready, i)
                for c in range(HC):
                    ins = tr(bank(4)[:, c * P:(c + 1) * P], h2p[:, c * P:(c + 1) * P], ident[:, :])
                ins.then_inc(tr2_done, 1)

            def third_layer(i, s):
                e = expert(i)
                pe.wait_ge(h2T_ready, i + 1)
                if i:
                    pe.wait_ge(y_ready, i)
                for c in range(HC):
                    ins = mm(bank(5)[:, 0:D], h2T[:, s, c, :], w3_sb[:, bass.ds(e * (HC * D) + c * D, D)],
                             start=(c == 0), stop=(c == HC - 1))
                ins.then_inc(mm3_done, 1)

            pe.wait_ge(tab_ready, 1)
            pe.wait_ge(a_used, len(a_order))
            pe.wait_ge(w1_in, 16)
            pe.wait_ge(w2_in, 16 * HC)
            pe.wait_ge(w3_in, 32)
            pe.wait_ge(w2b_in, 16 * HC)
            transpose_x(0, 0)
            first_layer(0, 0)
            transpose_x(1, 1)
            first_layer(1, 1)
            transpose_1(0, 0)
            transpose_x(2, 0)
            for i in range(NB):
                s, o = i % 2, (i + 1) % 2
                if i + 1 < NB:
                    transpose_1(i + 1, o)
                second_layer(i, s)
                if i + 2 < NB:
                    first_layer(i + 2, s)
                transpose_2(i, s)
                if i:
                    third_layer(i - 1, o)
                if i + 3 < NB:
                    transpose_x(i + 3, o)
            third_layer(NB - 1, (NB - 1) % 2)

            for q in range(B * R):
                b, r = divmod(q, R)
                pe.wait_ge(x1_ready, q + 1)
                if q >= 2:
                    pe.wait_ge(xc_ready, q - 1)
                mm(bank(q % 2)[:, 0:D], wcT_sb[:, b, :], x_sb[:, b, r, :], start=True, stop=True)
                mm(bank(q % 2)[:, D:2 * D], x_sb[:, b, r, :], wcT_sb[:, b, :], start=True, stop=True
                   ).then_inc(xc_done, 1)
                if q:
                    pe.wait_ge(xc_ready, q)
                    ins = mm(bank(2)[:, (q - 1) * E:q * E], xcT[:, (q - 1) // R, (q - 1) % R, :],
                             gate_sb[:, :], start=True, stop=True)
            pe.wait_ge(xc_ready, B * R)
            mm(bank(2)[:, (B * R - 1) * E:B * R * E], xcT[:, B - 1, R - 1, :], gate_sb[:, :], start=True,
               stop=True).then_inc(lg_done, 1)
            pe.wait_ge(cnt1_ready, 1)
            c1 = cntb[:, :, :, :].rearrange("p k b e -> p (k b) e")
            for n in range(2 * B):
                to = bank(3)[:, n * E:(n + 1) * E]
                ins = mm(to, tri[:, :], c1[:, n, :], start=True, stop=(n == 0))
                for before in range(n):
                    ins = mm(to, onesb[:, :], c1[:, before, :], start=False, stop=(before == n - 1))
            ins.then_inc(rank1_done, 1)

            def transpose_t(e):
                pe.wait_ge(tg_in[e % 2], 32 * (e // 2 + 1))
                if e >= 2:
                    pe.wait_ge(tgT_ready, e - 1)
                for c in range(CT):
                    k = P if c < CT - 1 else LAST
                    ins = tr(bank(e % 2)[:, c * P:c * P + k], tg[0:k, e % 2, c, :], ident[0:k, 0:k])
                ins.then_inc(tt_done, 1)

            def hidden(e):
                pe.wait_ge(tgT_ready, e + 1)
                for c in range(HC):
                    n = e * HC + c
                    if n >= 2:
                        pe.wait_ge(hT_ready, n - 1)
                    mm(bank(2 + c % 2)[:, 0:CAP], fc_sb[:, e, c * P:(c + 1) * P], tgT[:, e % 2, :],
                       start=True, stop=True).then_inc(fc_done, 1)

            def project(e):
                pe.wait_ge(hT_ready, (e + 1) * HC)
                if e >= 2:
                    pe.wait_ge(z_ready, e - 1)
                for t in range(CT):
                    k = P if t < CT - 1 else LAST
                    for c in range(HC):
                        ins = mm(bank(4 + e % 2)[0:k, t * P:t * P + D], hT[:, e % 2, c, t * P:t * P + k],
                                 cp_sb[:, e, c, :], start=(c == 0), stop=(c == HC - 1))
                ins.then_inc(z_done, 1)

            pe.wait_ge(l1w_in, 48)
            transpose_t(0)
            hidden(0)
            transpose_t(1)
            for e in range(E):
                if e + 1 < E:
                    hidden(e + 1)
                if e + 2 < E:
                    transpose_t(e + 2)
                project(e)

        @block.vector
        def _(dve):
            step = stepper(dve, dve_step)
            tt, ts, copy = dve.tensor_tensor, dve.tensor_scalar, dve.tensor_copy
            dve.memset(zeros, 0.0).then_inc(zeroed, 1)
            dve.memset(v_sb[:, :, :, :, HD:HD + 1].rearrange("p b k h i -> p (b k h) i"), 1.0)

            dve.wait_ge(cond_in, 48)
            for b in range(B):
                step(dve.scalar_tensor_tensor(out=wc_sb[:, b, :], in0=lw_sb, scalar=float(D) ** -0.5,
                                              in1=cond_bc[:, b, :], op0=ALU.mult, op1=ALU.mult))
                step(dve.tensor_tensor_reduce(out=sq_sb, in0=wc_sb[:, b, :], in1=wc_sb[:, b, :], scale=1.0,
                                              scalar=0.0, op0=ALU.mult, op1=ALU.add,
                                              accum_out=nrm[:, b, 0:1]))
            ts(nrm[:, :, 1], nrm[:, :, 0], 1e-8, None, ALU.add).then_inc(var_ready, 1)
            dve.wait_ge(mask_in, 16)
            step(copy(mpart[:, 0, :], mask_sb[:, :]))
            step(tt(mres[:, :], mask_sb[:, :], mpart[:, 0, :], ALU.subtract))
            step(copy(mpart[:, 1, :], mres[:, :]))
            tt(mpart[:, 2, :], mres[:, :], mpart[:, 1, :], ALU.subtract).then_inc(mask_ready, 1)

            for b in range(B):
                dve.wait_ge(xT_done, b + 1)
                copy(xT[:, b, :].rearrange("d (p r) -> d r p", r=R),
                     bank(b).rearrange("d (r p) -> d r p", r=R)).then_inc(xT_ready, 1)
            dve.wait_ge(cols_done, 1)
            copy(cols[:, :], bank(2)[:, 0:N_ROWS])
            copy(ukT, bank(2)[:, P:2 * P])
            copy(uvT, bank(2)[:, 2 * P:3 * P]).then_inc(cols_ready, 1)
            dve.wait_ge(cols_ready, 1)

            def qkv(n):
                b, i = divmod(n, 2)
                dve.wait_ge(qkv_done, n + 1)
                if i == 0:
                    ts(q32[:, b, :], bank(4 + n), cols[:, ROW_QKV:ROW_QKV + 1], SM_SCALE, ALU.add, ALU.mult
                       ).then_inc(qkv_ready, 1)
                else:
                    ts(k32[:, b, IMG:], bank(4 + n), cols[:, ROW_QKV + 1:ROW_QKV + 2], None, ALU.add
                       ).then_inc(qkv_ready, 1)

            def residue(n):
                b, i = divmod(n, 2)
                w = IMG + S if i else S
                src = k32[:, b, :] if i else q32[:, b, :]
                dve.wait_ge(hi_ready, n + 1)
                tt(res[:, i, 0:w], src, part[:, i, 0, 0:w], ALU.subtract).then_inc(mid_ready, 1)

            def last_part(n):
                b, i = divmod(n, 2)
                w = IMG + S if i else S
                dve.wait_ge(act_step, n + 1)
                tt(part[:, i, 2, 0:w], res[:, i, 0:w], part[:, i, 1, 0:w], ALU.subtract
                   ).then_inc(parts_ready, 1)

            qkv(0)
            dve.wait_ge(img_done, 1)
            dve.memset(k32[:, :, 0:IMG], 0.0)
            step(ts(vimg[:, :], bank(3)[:, B:2 * B], cols[:, ROW_UV:ROW_UV + 1], None, ALU.add))
            step(ts(k32[:, :, 0], bank(3)[:, 0:B], cols[:, ROW_UK:ROW_UK + 1], None, ALU.add))
            qkv(1)
            residue(0)
            for b in range(B):
                ins = ts(kimg_bd[:, b, :], hmask[:, :], k32[:, b, 0:1], None, ALU.mult)
            ins.then_inc(kbd_ready, 1)
            dve.wait_ge(consts, 1)
            last_part(0)
            residue(1)
            ts(vplace, place, vimg[:, 0:1], None, ALU.mult).then_inc(vplace_ready, 1)
            qkv(2)
            last_part(1)
            qkv(3)
            for b in range(B):
                dve.wait_ge(v_done, b + 1)
                tt(v_sb[:, b, :, :, 0:HD], bank(b).rearrange("p (k h d) -> p k h d", k=KC, h=H),
                   vb_bc[:, :].rearrange("p (o h d) -> p o h d", o=1, h=H).broadcast_to([P, KC, H, HD]),
                   ALU.add).then_inc(v_ready, 1)
            dve.wait_ge(vimg_done, 1)
            tt(vimg_bd[:, 0], bank(3).rearrange("p (h c) -> p h c", c=32), onec, ALU.add
               ).then_inc(vimg_ready, 1)
            ts(vplace, place, vimg[:, 1:2], None, ALU.mult).then_inc(vplace_ready, 1)
            residue(2)
            dve.wait_ge(sqrt_ready, 1)
            step(dve.reciprocal(nrm[:, :, 3], nrm[:, :, 2]))
            step(tt(nrm[:, :, 4], nrm[:, :, 3], nrm[:, :, 3], ALU.mult))
            step(tt(nrm[:, :, 5], nrm[:, :, 4], nrm[:, :, 1], ALU.mult))
            step(ts(nrm[:, :, 6], nrm[:, :, 5], -0.5, 1.5, ALU.mult, ALU.add))
            step(tt(nrm[:, :, 7], nrm[:, :, 6], nrm[:, :, 3], ALU.mult))
            last_part(2)
            residue(3)
            for b in range(B):
                ins = ts(wc_sb[:, b, :], wc_sb[:, b, :], nrm[:, b, 7:8], None, ALU.mult)
            ins.then_inc(wc_ready, 1)
            last_part(3)
            dve.wait_ge(vimg_done, 2)
            tt(vimg_bd[:, 1], bank(3).rearrange("p (h c) -> p h c", c=32), onec, ALU.add
               ).then_inc(vimg_ready, 1)
            dve.wait_ge(simg_done, 1)
            copy(simg[:, :, :, :].rearrange("p b t h -> p (b t h)"), bank(2)[:, 0:B * KC * H]
                 ).then_inc(simg_ready, 1)
            dve.wait_ge(wcT_done, 1)
            copy(wcT_sb[:, :, :].rearrange("p b i -> p (b i)"), bank(3)[:, 0:B * P]).then_inc(wcT_ready, 1)
            dve.wait_ge(simg_ready, 1)

            def maxima(n):
                b, g = divmod(n, NG)
                mine = slice(g * G, (g + 1) * G)
                dve.wait_ge(a_used, a_at[("score", n, KC - 1, G // 2 - 1)] + 1)
                if n:
                    dve.wait_ge(a_done, a_at[("maxT", n - 1)] + 1)
                step(tt(mr[:, :, :], mA[:, b, :, mine], simg[:, b, :, mine], ALU.max))
                step(ts(negm[:, :, :], mr[:, :, :], -1.0, None, ALU.mult))
                step(copy(mp[:, :, 0, :], negm[:, :, :]))
                step(tt(mr[:, :, :], negm[:, :, :], mp[:, :, 0, :], ALU.subtract))
                step(copy(mp[:, :, 1, :], mr[:, :, :]))
                tt(mp[:, :, 2, :], mr[:, :, :], mp[:, :, 1, :], ALU.subtract).then_inc(m_parts, 1)

            def choose(b):
                for r in range(R):
                    ins = dve.max(top_v[:, b, r, :], lg[:, b, r, :])
                step(ins)
                for r in range(R):
                    ins = dve.max_index(top_i[:, b, r, :], top_v[:, b, r, :], lg[:, b, r, :])
                step(ins)
                step(copy(top_f[:, b, :, 0:2], top_i[:, b, :, 0:2]))
                for k in range(2):
                    ins = tt(oh[:, k, b], iota_e[:, :, :], top_f[:, b, :, k:k + 1].broadcast_to([P, R, E]),
                             ALU.is_equal)
                step(ins)

            for piece in schedule:
                kind, *arg = piece
                if kind == "s":
                    continue
                if kind == "pv":
                    n, kc = arg
                    if kc == KC - 1:
                        dve.wait_ge(pv_done, (n + 1) * KC)
                        copy(o_sb[:, n, :], bank(7)).then_inc(o_ready, 1)
                    continue
                dve.wait_ge(a_done, a_at[piece] + 1)
                got = a_bank(piece)
                flat = got[:, 0, :]
                if kind == "score":
                    n, t, hp = arg
                    b, g = divmod(n, NG)
                    dve.tensor_reduce(mA[:, b, t, g * G + 2 * hp:g * G + 2 * hp + 2],
                                      got[:, :, 0:(t + 1) * P], AX_X, ALU.max).then_inc(a_used, 1)
                    if (t, hp) == (KC - 1, G // 2 - 1):
                        maxima(n)
                elif kind == "maxT":
                    n, = arg
                    if n >= 2:
                        dve.wait_ge(qkb_in[n % 2], 80 * (n // 2))
                    copy(mrow[:, n % 2, :], flat.bitcast(BF16)[0:3 * G, 0:S]).then_inc(a_used, 1)
                elif kind == "on":
                    b, r = arg
                    view = flat.rearrange("p (h c) -> p h c", c=32)
                    dve.wait_ge(a_used, a_at[piece])
                    step(dve.reciprocal(rden[:, :], view[:, :, HD]))
                    tt(on_sb[:, r % 2], view[:, :, 0:HD],
                       rden[:, :].rearrange("p (h o) -> p h o", o=1).broadcast_to([P, H, HD]), ALU.mult
                       ).then_inc(a_used, 1)
                elif kind == "onT":
                    b, r = arg
                    copy(onT[:, b, r, :], flat[:, 0:P]).then_inc(a_used, 1)
                elif kind == "aT":
                    b, = arg
                    ts(aT[:, b].rearrange("p r q -> p (r q)"), flat, cols[:, ROW_PROJ:ROW_PROJ + 1], None,
                       ALU.add).then_inc(a_used, 1)
                elif kind == "a":
                    b, = arg
                    tt(a_sb[:, b], flat.rearrange("p (r d) -> p r d", r=R),
                       projb_bc[:, :].rearrange("p (o d) -> p o d", o=1).broadcast_to([P, R, D]), ALU.add
                       ).then_inc(a_used, 1)
                elif kind == "route":
                    b, = arg
                    copy(lg[:, b].rearrange("p r e -> p (r e)"), flat[:, 0:R * E]).then_inc(a_used, 1)
                    dve.wait_ge(a_used, a_at[piece] + 1)
                    choose(b)
                    step(tt(ohsum[:, b], oh[:, 0, b], oh[:, 1, b], ALU.add))
                    step(dve.tensor_reduce(cnt[:, 0, b, :], ohsum[:, b].rearrange("p r e -> p e r"), AX_X,
                                           ALU.add))
                    copy(cntb[:, 0, b, :], cnt[:, 0, b, :]).then_inc(cnt_ready, 1)
                elif kind == "count":
                    b, = arg
                    tt(rank[:, 0, b, 0, :], flat[:, 0:E], base0[:, :], ALU.add).then_inc(a_used, 1)
                    dve.wait_ge(a_used, a_at[piece] + 1)
                    for r in range(1, R):
                        step(tt(rank[:, 0, b, r, :], rank[:, 0, b, r - 1, :], ohsum[:, b, r - 1, :], ALU.add))
                    for k in range(2):
                        ins = tt(pick[:, k, b], oh[:, k, b], rank[:, 0, b], ALU.mult)
                    step(ins)
                    step(dve.tensor_reduce(slot_f[:, :, b, :], pick[:, :, b], AX_X, ALU.add))
                    copy(slot0[:, :, b, :], slot_f[:, :, b, :]).then_inc(slot_ready, 1)
                else:
                    tot = flat[:, 0:E]
                    tt(nbge[:, :, :], tcut[:, :, :],
                       tot.rearrange("p (e o) -> p e o", o=1).broadcast_to([P, E, SLOTS0 // P]), ALU.is_lt
                       ).then_inc(a_used, 1)
                    dve.wait_ge(a_used, a_at[piece] + 1)
                    step(dve.tensor_reduce(nblk[:, :], nbge[:, :, :], AX_X, ALU.add))
                    step(dve.tensor_tensor_scan(cumb[:, :], nblk[:, :], nblk[:, :], 0.0, ALU.add, ALU.bypass))
                    wide = [1, NB, E]
                    step(tt(ended[:, :, :], cumb[0:1, :].rearrange("p (o e) -> p o e", o=1).broadcast_to(wide),
                            bidx[:, :, :], ALU.is_le))
                    step(tt(endblk[:, :, :], ended[:, :, :],
                            nblk[0:1, :].rearrange("p (o e) -> p o e", o=1).broadcast_to(wide), ALU.mult))
                    dve.tensor_reduce(tabf[:, 0, :], ended[:, :, :], AX_X, ALU.add)
                    step(dve.tensor_reduce(tabf[:, 1, :], endblk[:, :, :], AX_X, ALU.add))
                    step(tt(tabf[:, 2, :], bidx[:, :, 0], tabf[:, 1, :], ALU.subtract))
                    step(ts(tabf[:, 3, :], tabf[:, 2, :], float(P), None, ALU.mult))
                    step(dve.scalar_tensor_tensor(out=tabf[:, 4, :], in0=tabf[:, 0, :], scalar=float(SLOTS0),
                                                  in1=tabf[:, 3, :], op0=ALU.mult, op1=ALU.add))
                    ts(tab[:, 0, :], tabf[:, 0, :], float(E - 1), None, ALU.min)
                    ts(tab[:, 1, :], tabf[:, 4, :], float(E * SLOTS0 - P), None, ALU.min
                       ).then_inc(tab_ready, 1)
                    step(tt(shift[:, :], cumb[:, :], nblk[:, :], ALU.subtract))
                    step(dve.scalar_tensor_tensor(out=shift[:, :], in0=shift[:, :], scalar=float(P),
                                                  in1=base0[:, :], op0=ALU.mult, op1=ALU.subtract))
                    for k in range(2):
                        for b in range(B):
                            ins = tt(pick[:, k, b], oh[:, k, b],
                                     shift[:, :].rearrange("p (o e) -> p o e", o=1).broadcast_to([P, R, E]),
                                     ALU.mult)
                    step(ins)
                    every = "p k b r -> p (k b r)"
                    step(dve.tensor_reduce(rank_f[:, :, :, :].rearrange(every),
                                           pick[:, :, :, :, :].rearrange("p k b r e -> p (k b r) e"), AX_X,
                                           ALU.add))
                    tt(row0[:, :, :, :].rearrange(every), slot_f[:, :, :, :].rearrange(every),
                       rank_f[:, :, :, :].rearrange(every), ALU.add).then_inc(row0_ready, 1)

            def copy_x(i, s):
                dve.wait_ge(tx_done, i + 1)
                if not isinstance(i, int) or i >= 2:
                    dve.wait_ge(mm1_done, i - 1)
                copy(xgT[:, s, :], bank(0)[:, 0:P]).then_inc(xgT_ready, 1)

            def copy_1(i):
                dve.wait_ge(mm1_done, i + 1)
                if not isinstance(i, int) or i >= 1:
                    dve.wait_ge(tr1_done, i)
                copy(h1p[:, :], bank(1)).then_inc(h1p_ready, 1)

            def copy_2(i):
                dve.wait_ge(mm2_done, i + 1)
                if not isinstance(i, int) or i >= 1:
                    dve.wait_ge(tr2_done, i)
                copy(h2p[:, :], bank(3)).then_inc(h2p_ready, 1)

            def result(i, s):
                e = dve.value_load(tab[0:1, 0, bass.ds(i, 1)], min_val=0, max_val=E - 1)
                dve.wait_ge(mm3_done, i + 1)
                if not isinstance(i, int) or i >= 2:
                    dve.wait_ge(y_out[s], 16 * (i // 2))
                tt(y_sb[:, s, :], bank(5)[:, 0:D], b3_sb[:, bass.ds(e * D, D)], ALU.add
                   ).then_inc(y_ready, 1)

            dve.wait_ge(tab_ready, 1)
            copy_x(0, 0)
            copy_1(0)
            copy_x(1, 1)
            copy_1(1)
            copy_x(2, 0)
            for i in range(NB):
                s, o = i % 2, (i + 1) % 2
                copy_2(i)
                if i + 2 < NB:
                    copy_1(i + 2)
                if i:
                    result(i - 1, o)
                if i + 3 < NB:
                    copy_x(i + 3, o)
            result(NB - 1, (NB - 1) % 2)

            for q in range(B * R):
                b, r = divmod(q, R)
                dve.wait_ge(back_in[q], 32)
                step(tt(back[:, b, r, 0, :], back[:, b, r, 0, :], back[:, b, r, 1, :], ALU.add))
                dve.scalar_tensor_tensor(out=x_sb[:, b, r, :], in0=back[:, b, r, 0, :], scalar=0.5,
                                         in1=x_sb[:, b, r, :], op0=ALU.mult, op1=ALU.add
                                         ).then_inc(x1_ready, 1)
                if q:
                    give_xc = divmod(q - 1, R)
                    dve.wait_ge(xc_done, q)
                    copy(a_sb[:, give_xc[0], give_xc[1], :], bank((q - 1) % 2)[:, 0:D])
                    copy(xcT[:, give_xc[0], give_xc[1], :], bank((q - 1) % 2)[:, D:2 * D]
                         ).then_inc(xc_ready, 1)
            dve.wait_ge(xc_done, B * R)
            copy(a_sb[:, B - 1, R - 1, :], bank((B * R - 1) % 2)[:, 0:D])
            copy(xcT[:, B - 1, R - 1, :], bank((B * R - 1) % 2)[:, D:2 * D]).then_inc(xc_ready, 1)

            dve.wait_ge(lg_done, 1)
            step(copy(lg[:, :, :, :].rearrange("p b r e -> p (b r e)"), bank(2)[:, 0:B * R * E]))
            for b in range(B):
                choose(b)
            step(dve.tensor_reduce(cnt[:, :, :, :].rearrange("p k b e -> p (k b) e"),
                                   oh[:, :, :, :, :].rearrange("p k b r e -> p (k b) e r"), AX_X, ALU.add))
            copy(cntb[:, :, :, :], cnt[:, :, :, :]).then_inc(cnt1_ready, 1)
            tt(dl[:, :, :], top_v[:, :, :, 0], top_v[:, :, :, 1], ALU.subtract).then_inc(dl_ready, 1)
            dve.wait_ge(rank1_done, 1)
            by_kb = rank[:, :, :, :, :].rearrange("p k b r e -> p (k b) r e")
            oh_kb = oh[:, :, :, :, :].rearrange("p k b r e -> p (k b) r e")
            step(copy(by_kb[:, :, 0, :], bank(3)[:, 0:2 * B * E].rearrange("p (q e) -> p q e", e=E)))
            for r in range(1, R):
                step(tt(by_kb[:, :, r, :], by_kb[:, :, r - 1, :], oh_kb[:, :, r - 1, :], ALU.add))
            whole = [P, 2 * B * R, E]
            oh_f = oh[:, :, :, :, :].rearrange("p k b r e -> p (k b r) e")
            pick_f = pick[:, :, :, :, :].rearrange("p k b r e -> p (k b r) e")
            flat3 = lambda t: t[:, :, :, :].rearrange("p k b r -> p (k b r)")
            step(tt(pick_f, oh_f, rank[:, :, :, :, :].rearrange("p k b r e -> p (k b r) e"), ALU.mult))
            step(dve.tensor_reduce(flat3(rank_f), pick_f, AX_X, ALU.add))
            step(tt(pick_f, oh_f, base1[:, :].rearrange("p (o e) -> p o e", o=1).broadcast_to(whole),
                    ALU.mult))
            step(dve.tensor_reduce(flat3(slot_f), pick_f, AX_X, ALU.add))
            step(ts(flat3(keep), flat3(rank_f), float(CAP), None, ALU.is_lt))
            step(tt(flat3(slot_f), flat3(slot_f), flat3(rank_f), ALU.add))
            step(ts(flat3(slot_f), flat3(slot_f), dump[:, 0:1], None, ALU.subtract))
            step(tt(flat3(slot_f), flat3(slot_f), flat3(keep), ALU.mult))
            ts(flat3(slot1), flat3(slot_f), dump[:, 0:1], None, ALU.add).then_inc(slot1_ready, 1)
            dve.wait_ge(th_ready, 1)
            ts(p_sb[:, 0], th[:, :, :], 0.5, 0.5, ALU.mult, ALU.add)
            step(ts(p_sb[:, 1], th[:, :, :], -0.5, 0.5, ALU.mult, ALU.add))

            def copy_t(e):
                dve.wait_ge(tt_done, e + 1)
                if e >= 2:
                    dve.wait_ge(fc_done, (e - 1) * HC)
                copy(tgT[:, e % 2, :], bank(e % 2)[:, 0:CAP]).then_inc(tgT_ready, 1)

            def add_bias(e):
                dve.wait_ge(z_done, e + 1)
                if e >= 2:
                    dve.wait_ge(z_out[e % 2], 32 * (e // 2))
                got = bank(4 + e % 2)
                tt(z_sb[:, e % 2, 0:CT - 1, :], got[:, 0:(CT - 1) * D].rearrange("p (c d) -> p c d", d=D),
                   prb_sb[:, e:e + 1, :].broadcast_to([P, CT - 1, D]), ALU.add)
                tt(z_sb[0:LAST, e % 2, CT - 1, :], got[0:LAST, (CT - 1) * D:CT * D], prb_sb[0:LAST, e, :],
                   ALU.add).then_inc(z_ready, 1)

            dve.wait_ge(l1w_in, 48)
            copy_t(0)
            copy_t(1)
            for e in range(E):
                if e + 2 < E:
                    copy_t(e + 2)
                add_bias(e)

            for q in range(B * R):
                b, r = divmod(q, R)
                dve.wait_ge(back1_in[q], 32)
                step(dve.scalar_tensor_tensor(out=r_sb[:, b, r, :], in0=back[:, b, r, 0, :],
                                              scalar=p_sb[:, 0, b, r:r + 1], in1=x_sb[:, b, r, :],
                                              op0=ALU.mult, op1=ALU.add))
                dve.scalar_tensor_tensor(out=r_sb[:, b, r, :], in0=back[:, b, r, 1, :],
                                         scalar=p_sb[:, 1, b, r:r + 1], in1=r_sb[:, b, r, :],
                                         op0=ALU.mult, op1=ALU.add).then_inc(r_ready, 1)


_INS = ['x', 'cond_1024', 'mask_Bx1x1xS_ff0', 'L0_cond_c_attn_w', 'L0_cond_c_attn_b', 'L0_cond_c_proj_w',
        'L0_cond_c_proj_b', 'L0_cond_uk_w', 'L0_cond_uk_b', 'L0_cond_uv_w', 'L0_cond_uv_b',
        'L0_ffn_expert_tokens', 'L0_ffn_W1', 'L0_ffn_b1', 'L0_ffn_W2', 'L0_ffn_b2', 'L0_ffn_W3', 'L0_ffn_b3',
        'L1_cond_weight', 'L1_ffn_gate_w', 'L1_ffn_c_fc', 'L1_ffn_fc_bias', 'L1_ffn_c_proj',
        'L1_ffn_proj_bias']
_OUTS = [((B, S, D), 'float32')]


def kernel(**inputs):
    import numpy as _np
    import concourse.bacc as _bacc
    from concourse import mybir as _mybir
    from concourse.bass_utils import run_bass_kernel_spmd as _run

    nc = _bacc.Bacc("TRN2", target_bir_lowering=False, num_devices=1)
    arrays, args = {}, []
    for name in _INS:
        a = _np.ascontiguousarray(inputs[name])
        arrays[f"in_{name}_dram"] = a
        args.append(nc.dram_tensor(f"in_{name}_dram", a.shape, _mybir.dt.from_np(a.dtype), kind="ExternalInput").ap())
    for i, (shape, dtype) in enumerate(_OUTS):
        dt = _mybir.dt.from_np(_np.dtype(dtype))
        args.append(nc.dram_tensor(f"out_{i}_dram", shape, dt, kind="ExternalOutput").ap())
    build(nc, *args)
    r = _run(nc, [arrays], core_ids=[0])
    return r.results[0]["out_0_dram"]
```

```python
from contextlib import ExitStack

import concourse.bass as bass
from concourse import mybir

ALU = mybir.AluOpType
ACT = mybir.ActivationFunctionType
F32 = mybir.dt.float32
BF16 = mybir.dt.bfloat16
F16 = mybir.dt.float16
I32 = mybir.dt.int32
U32 = mybir.dt.uint32
AX_X = mybir.AxisListType.X

P = 128
B, S, D = 2, 512, 128
R = S // P
H, HD = 16, 8
G = 4
NG = H // G
KC = S // P
E = 8
HID = 512
HC = HID // P
SM_SCALE = float(HD) ** -0.5
MASKED = -30000.0

Q_PART = (0, 0, 1, 1, 0, 2)
K_PART = (0, 1, 0, 1, 2, 0)
PROD_ROWS = len(Q_PART) * HD
MASK_ROW = PROD_ROWS
MAX_ROW = MASK_ROW + 3
ROWS = MAX_ROW + 3

IMG = 32

SLOTS0 = B * S
NB = (2 * B * S + E * (P - 1)) // P
CAP = int(1.25 * B * S * 2 / E)
CT = -(-CAP // P)
LAST = CAP - (CT - 1) * P
CLEAR_ROWS = 16
N_CLEAR = E * SLOTS0 // P // CLEAR_ROWS + 2
IN_UP = 16.0
W_UP = 128.0
DOWN = 1.0 / (IN_UP * W_UP)
PRODUCTS = ((0, 0), (0, 1), (1, 0))
W_TILES = HC * HC + 2 * HC
W_EARLY = HC * HC + HC
W_RING = 4
LEAD, UNROLL = 3, 4
LOOPS = (NB - LEAD - 4) // UNROLL
REST = LEAD + LOOPS * UNROLL
DUMP1 = E * CAP

ROW_B1, ROW_B2, ROW_FC, ROW_QKV, ROW_PROJ, ROW_UK, ROW_UV, ROW_ET, ROW_IMG = (
    0, E * HC, 2 * E * HC, 3 * E * HC, 3 * E * HC + 3, 3 * E * HC + 4, 3 * E * HC + 5,
    3 * E * HC + 6, 3 * E * HC + 6 + E)
N_ROWS = ROW_IMG + B


def score_units():
    out = []
    for kc in range(KC):
        heads = 1 if kc < 2 else kc if kc == 2 else 4
        out += [(kc, heads, j) for j in range(0, G, heads)]
    return out


UNITS = score_units()
NU = len(UNITS)
P_RING = 8
O_RING = 6
LAG = 2


def build(nc, x, cond, mask, attn_w, attn_b, proj_w, proj_b, uk_w, uk_b, uv_w, uv_b,
          et, W1, b1, W2, b2, W3, b3, l1w, gate_w, c_fc, fc_b, c_proj, pr_b, out):
    ctx = ExitStack()
    with ctx:
        def dram(name, shape, dt):
            return nc.dram_tensor(name, shape, dt).ap()

        def sem(name):
            return ctx.enter_context(nc.semaphore(name))

        q_rows_d = [dram(f"q_rows{b}", (MAX_ROW, H, S), BF16) for b in range(B)]
        k_rows_d = [dram(f"k_rows{b}", (ROWS, H, IMG + S), BF16) for b in range(B)]
        FREE1 = 1 + 2 * B * S
        x0_d = dram("x0_slots", (E * SLOTS0, 2 * D + 2), F16)
        x1_d = dram("x1_slots", (DUMP1 + P, D + 1), F32)
        y0_d = dram("y0_rows", (FREE1, D), F32)
        y1_d = dram("y1_rows", (FREE1 + E * CT * P, D), F32)

        def sb(name, shape, dt=F32, stack=ctx):
            return stack.enter_context(nc.sbuf_tensor(name, shape, dt))

        w2_sb = [[sb(f"w2_sb{k}{q}", [P, E * HID], F16) for q in range(2)] for k in range(HC)]
        zeros = w2_sb[HC - 1][0]
        w1_sb = [[sb(f"w1_sb{m}{q}", [P, E * P], F16) for q in range(2)] for m in range(HC)]
        w_ring = [sb(f"w_ring{n}", [P, E, P]) for n in range(W_RING)]
        x_sb = sb("x_sb", [P, B, R, D])
        sent = sb("sent", [P, B, 2, R, D + 1])
        ident = sb("ident", [P, P])
        identh = sb("identh", [P, P], F16)
        identb = sb("identb", [P, P], BF16)
        tri = sb("tri", [P, P], BF16)
        onesb = sb("onesb", [P, P], BF16)
        cols = sb("cols", [P, N_ROWS])
        gate_sb = sb("gate_sb", [P, E])
        wc_sb = sb("wc_sb", [P, B, P])
        wcT_sb = sb("wcT_sb", [P, B, P])
        iota_e = sb("iota_e", [P, R, E])
        base0 = sb("base0", [P, E])
        tcut = sb("tcut", [1, E, SLOTS0 // P])
        bidx = sb("bidx", [1, NB, E])
        warm = sb("warm", [P, 2])
        dump = sb("dump", [P, 1])
        lg = sb("lg", [P, B, R, E])
        free_row = sb("free_row", [P, E, CT])
        is_free = sb("is_free", [P, CT])
        top_v = sb("top_v", [P, B, R, 8])
        top_i = sb("top_i", [P, B, R, 8], U32)
        top_f = sb("top_f", [P, B, R, 8])
        oh = sb("oh", [P, 2, B, R, E])
        ohsum = sb("ohsum", [P, B, R, E])
        cnt = sb("cnt", [P, 2, B, E])
        cntb = sb("cntb", [P, 2, B, E], BF16)
        rank = sb("rank", [P, 2, B, R, E])
        pick = sb("pick", [P, 2, B, R, E])
        slot_f = sb("slot_f", [P, 2, B, R])
        rank_f = sb("rank_f", [P, 2, B, R])
        keep = sb("keep", [P, 2, B, R])
        slot0 = sb("slot0", [P, 2, B, R], I32)
        slot1 = sb("slot1", [P, 2, B, R], I32)
        p_sb = sb("p_sb", [P, 2, B, R])
        dl = sb("dl", [P, B, R])
        th = sb("th", [P, B, R])
        nbge = sb("nbge", [1, E, SLOTS0 // P])
        nblk = sb("nblk", [1, E])
        cumb = sb("cumb", [1, E])
        ended = sb("ended", [1, NB, E])
        endblk = sb("endblk", [1, NB, E])
        tabf = sb("tabf", [1, 5, NB])
        tab = sb("tab", [1, 2, NB], I32)

        with ExitStack() as at:
            with ExitStack() as pre:
                early = sb("early", [P, 4, H, 32], F32, pre)
                hsel, place, onec, vplace = (early[:, n] for n in range(4))
                k32 = sb("k32", [P, B, IMG + S], F32, pre)
                xT = sb("xT", [P, B, S], F32, pre)
                q32 = sb("q32", [P, B, S], F32, pre)
                part = sb("part", [P, 2 * B, 3, IMG + S], BF16, pre)
                wqkv = sb("wqkv", [P, 3 * D], F32, pre)
                mask_sb = sb("mask_sb", [B, S], F32, pre)
                mres = sb("mres", [B, S], F32, pre)
                mpart = sb("mpart", [B, 3, S], BF16, pre)
                mrowone = sb("mrowone", [H, 3, IMG + S], BF16, pre)
                mrowzero = sb("mrowzero", [H, 3, IMG], BF16, pre)
                vb_bc = sb("vb_bc", [P, D], F32, pre)
                cond_bc = sb("cond_bc", [P, B, D], F32, pre)
                res = sb("res", [P, 2, IMG + S], F32, pre)
                lw_sb, sq_sb, uk_sb, uv_sb, ukT, uvT = (
                    sb(n, [P, P], F32, pre)[:, :] for n in ("lw", "sq", "uk", "uv", "ukT", "uvT"))
            p_ring = sb("p_ring", [P, P_RING, S], F32, at)
            o_sb = sb("o_sb", [P, O_RING, S], F32, at)
            qb = sb("qb", [ROWS, 2, G, S], BF16, at)
            kb = sb("kb", [ROWS, 2, G, IMG + S], BF16, at)
            onT = sb("onT", [P, R, P], F32, at)
            aT = sb("aT", [P, R, P], F32, at)
            pimg = sb("pimg", [P, 2, S], F32, at)
            mrow = sb("mrow", [3 * G, 2, S], BF16, at)
            on_sb = sb("on_sb", [P, 2, H, HD], F32, at)
            mA = sb("mA", [P, B, KC, H], F32, at)
            qa = sb("qa", [MAX_ROW, 2, G, S], BF16, at)
            ka = sb("ka", [MAX_ROW, 2, G, IMG + S], BF16, at)
            rows_sb = sb("rows_sb", [P, D], F32, at)
            proj_sb = sb("proj_sb", [P, D], F32, at)
            nrm = sb("nrm", [P, B, 8], F32, at)
            causal_a = sb("causal_a", [P, P], BF16, at)
            causal_b = sb("causal_b", [P, P], BF16, at)
            hmask = sb("hmask", [P, H], F32, at)
            v_sb = sb("v_sb", [P, B, KC, H, HD + 1], F32, at)
            vimg = sb("vimg", [P, B], F32, at)
            kimg_bd = sb("kimg_bd", [P, B, H], F32, at)
            vimg_bd = sb("vimg_bd", [P, B, H, 32], F32, at)
            simg = sb("simg", [P, B, KC, H], F32, at)
            negm = sb("negm", [P, KC, G], F32, at)
            mr = sb("mr", [P, KC, G], F32, at)
            mp = sb("mp", [P, KC, 3, G], BF16, at)
            rden = sb("rden", [P, H], F32, at)

        w3_sb = [[sb(f"w3_sb{k}{q}", [P, E * P], F16) for q in range(2)] for k in range(HC)]
        b3_sb = sb("b3_sb", [P, E * D])
        fc_sb = sb("fc_sb", [P, E, HID])
        cp_sb = sb("cp_sb", [P, E, HC, D])
        prb_sb = sb("prb_sb", [P, E, D])
        back = sb("back", [P, 2, B, R, D])
        id_all = sb("id_all", [P, NB], I32)
        id_now = sb("id_now", [P, 2], I32)
        id1 = sb("id1", [P, 4, CT], I32)
        xcT = sb("xcT", [P, B, R, P])
        with ExitStack() as f0:
            xg = sb("xg", [P, 2, 2 * D + 2], F16, f0)
            xgT = sb("xgT", [P, 2, 2, P], F16, f0)
            h32 = sb("h32", [P, 2, HID], F32, f0)
            z32 = sb("z32", [P, HID], F32, f0)
            h1 = sb("h1", [P, 2, 2, HID], F16, f0)
            h2 = sb("h2", [P, 2, 2, HID], F16, f0)
            y_sb = sb("y_sb", [P, 2, D], F32, f0)
        tg = sb("tg", [P, 2, CT, D + 1])
        tgT = sb("tgT", [P, 2, 2, CAP], F16)
        hT = sb("hT", [P, 2, 2, HC, CAP], F16)
        z_sb = sb("z_sb", [P, 2, CT, D])
        fc16, cp16 = ([t[:, :].rearrange("p (e n) -> p e n", e=E) for t in w2_sb[k]] for k in range(2))
        h1_32 = w2_sb[2][0][:, :].bitcast(F32)[:, 0:HC * CAP].rearrange("p (c n) -> p c n", c=HC)

        def sems(names):
            return [sem(n) for n in names.split()]

        (x_in, rows_in, wqkv_in, uk_in, cond_in, mask_in, misc_in, b3_in, w_hi, w_lo, l1w_in,
         zero_out) = sems(
            "x_in rows_in wqkv_in uk_in cond_in mask_in misc_in b3_in w_hi w_lo l1w_in "
            "zero_out")
        w_in = [sem(f"w_in{n}") for n in range(W_RING)]
        pool_step, dve_step, act_step, ident_ready, consts, zeroed = sems(
            "pool_step dve_step act_step ident_ready consts zeroed")
        (xT_done, xT_ready, cols_done, cols_ready, img_done, img_ready, qkv_done, qkv_ready, hi_ready,
         mid_ready, parts_ready, v_done, v_ready, simg_done, simg_ready, vimg_done, vimg_ready,
         var_ready, sqrt_ready, wc_ready, wcT_done, wcT_ready, mask_ready, kbd_ready, vplace_ready) = sems(
            "xT_done xT_ready cols_done cols_ready img_done img_ready qkv_done qkv_ready hi_ready "
            "mid_ready parts_ready v_done v_ready simg_done simg_ready vimg_done vimg_ready "
            "var_ready sqrt_ready wc_ready wcT_done wcT_ready mask_ready kbd_ready vplace_ready")
        rows_out = [sem(f"rows_out{n}") for n in range(2 * B)]
        krest_out = [sem(f"krest_out{b}") for b in range(B)]
        a_done, a_used, m_parts, s_done, exp_done, pv_done, o_ready, cnt_ready, slot_ready, tab_ready = sems(
            "a_done a_used m_parts s_done exp_done pv_done o_ready cnt_ready slot_ready tab_ready")
        qka_in = [sem(f"qka_in{n}") for n in range(2)]
        qkb_in = [sem(f"qkb_in{n}") for n in range(2)]
        sent0, tx_done, xgT_ready, mm1_done, gelu1_done, h1_ready, mm2_done, gelu2_done, h2_ready, \
            mm3_done, y_ready = sems(
                "sent0 tx_done xgT_ready mm1_done gelu1_done h1_ready mm2_done gelu2_done h2_ready "
                "mm3_done y_ready")
        hi1_ready, hi2_ready, z_copied, tz_done = sems("hi1_ready hi2_ready z_copied tz_done")
        xg_in = [sem(f"xg_in{n}") for n in range(2)]
        y_out = [sem(f"y_out{n}") for n in range(2)]
        back_in = [sem(f"back_in{n}") for n in range(B)]
        x1_ready, xc_done, xc_ready, xcT_done, xcT_ready, lg_done, cnt1_ready, rank1_done, slot1_ready, dl_ready, \
            th_ready, sent1 = sems(
                "x1_ready xc_done xc_ready xcT_done xcT_ready lg_done cnt1_ready rank1_done slot1_ready dl_ready "
                "th_ready sent1")
        fc_hi, fc_lo, hid_done, hT_hi = sems("fc_hi fc_lo hid_done hT_hi")
        tt_done, tgT_ready, fc_done, hT_ready, z_done, z_ready, r_ready, out_sent = sems(
            "tt_done tgT_ready fc_done hT_ready z_done z_ready r_ready out_sent")
        tg_in = [sem(f"tg_in{n}") for n in range(2)]
        z_out = [sem(f"z_out{n}") for n in range(2)]
        back1_in = [sem(f"back1_in{n}") for n in range(B)]

        def stepper(eng, stepped):
            steps = 0

            def step(ins):
                nonlocal steps
                steps += 1
                ins.then_inc(stepped, 1)
                eng.wait_ge(stepped, steps)

            return step

        groups = B * NG

        def a_pieces(n):
            out = [("score", n, t, hp) for t in range(KC) for hp in range(G // 2)] if n < groups else []
            if 1 <= n <= groups:
                out.insert(4 if n < groups else 0, ("maxT", n - 1))
            return out

        def s_pieces(n):
            return [("s", n, k) for k in range(NU + 1)]

        def chunk_units(kc):
            return [k + 1 for k, u in enumerate(UNITS) if u[0] == kc]

        def b_pieces():
            out = [[] for _ in range(groups + 1)]
            for c in range(groups * KC + 1):
                n, kc = divmod(c, KC)
                if c < groups * KC:
                    units = ([0] if kc == 0 else []) + chunk_units(kc)
                    out[n] += [("s", n, k) for k in units]
                if c:
                    out[n] += [("pv", *divmod(c - 1, KC))]
            out[groups - 1] += out.pop()
            return out

        def tail(b):
            out = [("on", b, 0), ("on", b, 1), ("onT", b, 0), ("on", b, 2), ("onT", b, 1), ("on", b, 3),
                   ("onT", b, 2), ("onT", b, 3)]
            return out + [("aT", b), ("route", b), ("a", b), ("count", b)]

        def merged(one, two):
            at = sorted([(i / len(one), 0, p) for i, p in enumerate(one)]
                        + [((i + 0.5) / len(two), 1, p) for i, p in enumerate(two)], key=lambda q: q[:2])
            return [p for _, _, p in at]

        by_group = b_pieces()
        schedule = []
        for n in range(groups + LAG):
            first = a_pieces(n) if n < groups + 1 else []
            if n == groups - 1:
                first = first + tail(0)
            schedule += merged(first, by_group[n - LAG] if n >= LAG else [])
        schedule += tail(1) + [("total",)]
        a_order = [p for p in schedule if p[0] not in ("s", "pv")]
        a_at = {p: i for i, p in enumerate(a_order)}

        pair = [ctx.enter_context(nc.psum_tensor(f"pair{n}", [P, 2, 512], F32)) for n in range(2)]
        single = [ctx.enter_context(nc.psum_tensor(f"bank{n}", [P, 512], F32)) for n in range(4, 8)]

        def bank(n):
            return pair[n // 2][:, n % 2, :] if n < 4 else single[n - 4][:, :]

        FC_BANKS = (2, 3, 6, 7)
        XC_BANKS = ((0, 1), (4, 5))

        def a_bank(piece):
            return pair[a_at[piece] % 2]

        def s_index(n, k):
            return n * (NU + 1) + k

        def p_index(n, k):
            return n * NU + k - 1

        def chunk_of(w):
            n, k = divmod(w, NU)
            return n * KC + UNITS[k][0]

        def block_of(j, c):
            return UNROLL * j + c, c % 2, UNROLL // 2 * j + c // 2

        def later(count, least):
            return not isinstance(count, int) or count >= least

        def table(eng, row, first, n):
            _, values = nc.values_load_multi_w_load_instructions(
                tab[0:1, row, bass.ds(first, n)], engines=[eng], min_val=0,
                max_val=(E - 1) if row == 0 else E * SLOTS0 - P,
                skip_runtime_bounds_check_because="the table's values are clamped when it is made")
            return values

        def w_tile(n):
            cols_of = lambda c: slice(c * P, (c + 1) * P)
            by_expert = lambda t, at: t[:, :].rearrange("p (e n) -> p e n", e=E)[:, :, at]
            if n < HC * HC:
                k, m = divmod(n, HC)
                return W2[:, cols_of(k), cols_of(m)], [by_expert(t, cols_of(m)) for t in w2_sb[k]]
            k = (n - HC * HC) % HC
            if n < HC * HC + HC:
                return W1[:, :, cols_of(k)], [by_expert(t, cols_of(0)) for t in w1_sb[k]]
            return W3[:, cols_of(k), :], [by_expert(t, cols_of(0)) for t in w3_sb[k]]

        sparse = 9
        high_at = [14 + 7 * n if n < sparse else 73 + 2 * (n - sparse) for n in range(W_EARLY)]
        low_at = [v + (4 if n < sparse else 2) for n, v in enumerate(high_at)]


        block = ctx.enter_context(nc.Block())

        @block.sync
        def _(sp):
            sp.dma_start(x_sb[:, :, :, :], x.rearrange("b (p r) d -> p b r d", r=R)).then_inc(x_in, 16)
            for at_row, n, src in (
                    (ROW_B1, E * HC, b1.rearrange("e (c p) -> (e c) p", p=P)),
                    (ROW_B2, E * HC, b2.rearrange("e (c p) -> (e c) p", p=P)),
                    (ROW_FC, E * HC, fc_b.rearrange("e o (c p) -> (e o c) p", p=P)),
                    (ROW_QKV, 3, attn_b.rearrange("(c p) -> c p", p=P)),
                    (ROW_PROJ, 1, proj_b.rearrange("(c p) -> c p", p=P)),
                    (ROW_UK, 1, uk_b.rearrange("(c p) -> c p", p=P)),
                    (ROW_UV, 1, uv_b.rearrange("(c p) -> c p", p=P)),
                    (ROW_ET, E, et),
                    (ROW_IMG, B, cond)):
                sp.dma_start(rows_sb[at_row:at_row + n, :], src).then_inc(rows_in, 16)

            def store_parts(b):
                for i in range(2):
                    n = 2 * b + i
                    sp.wait_ge(parts_ready, n + 1)
                    rows, which = (k_rows_d[b], K_PART) if i else (q_rows_d[b], Q_PART)
                    width = IMG + S if i else S
                    for c, m in enumerate(which):
                        sp.dma_start(rows[c * HD:(c + 1) * HD].rearrange("d h t -> h d t"),
                                     part[:, n, m, 0:width]).then_inc(rows_out[n], 16)

            sp.wait_ge(consts, 1)
            for b in range(B):
                sp.dma_start(q_rows_d[b][MASK_ROW:MAX_ROW].rearrange("r h t -> h r t"),
                             mrowone[:, :, IMG:]).then_inc(krest_out[b], 16)
                sp.dma_start(k_rows_d[b][MAX_ROW:ROWS].rearrange("r h t -> h r t"),
                             mrowone[:, :, :]).then_inc(krest_out[b], 16)
                sp.dma_start(k_rows_d[b][MASK_ROW:MAX_ROW, :, 0:IMG].rearrange("r h t -> h r t"),
                             mrowzero[:, :, :]).then_inc(krest_out[b], 16)
            sp.wait_ge(mask_ready, 1)
            for b in range(B):
                for m in range(3):
                    sp.dma_start(k_rows_d[b][MASK_ROW + m:MASK_ROW + m + 1, :, IMG:],
                                 mpart[b:b + 1, m:m + 1, :].broadcast_to([1, H, S])
                                 ).then_inc(krest_out[b], 16)

            def rows_stored(b):
                sp.wait_ge(rows_out[2 * b], 16 * len(Q_PART))
                sp.wait_ge(rows_out[2 * b + 1], 16 * len(K_PART))
                sp.wait_ge(krest_out[b], 16 * 6)

            def load_a(n):
                b, g = divmod(n, NG)
                if n >= 2:
                    sp.wait_ge(a_done, a_at[("score", n - 2, KC - 1, G // 2 - 1)] + 1)
                sp.dma_start(qa[:, n % 2], q_rows_d[b][:, g * G:(g + 1) * G, :]).then_inc(qka_in[n % 2], 16)
                sp.dma_start(ka[:, n % 2], k_rows_d[b][0:MAX_ROW, g * G:(g + 1) * G, :]
                             ).then_inc(qka_in[n % 2], 16)

            def load_b(n):
                b, g = divmod(n, NG)
                if n >= 2:
                    sp.wait_ge(s_done, s_index(n - 1, 0))
                sp.dma_start(qb[0:MAX_ROW, n % 2], q_rows_d[b][:, g * G:(g + 1) * G, :]
                             ).then_inc(qkb_in[n % 2], 16)
                sp.dma_start(kb[:, n % 2], k_rows_d[b][:, g * G:(g + 1) * G, :]).then_inc(qkb_in[n % 2], 16)
                sp.wait_ge(a_used, a_at[("maxT", n)] + 1)
                for m in range(3):
                    sp.dma_start(qb[MAX_ROW + m:MAX_ROW + m + 1, n % 2], mrow[m * G:(m + 1) * G, n % 2, :]
                                 ).then_inc(qkb_in[n % 2], 16)

            store_parts(0)
            rows_stored(0)
            load_a(0)
            load_a(1)
            store_parts(1)
            rows_stored(1)
            sp.wait_ge(a_done, 1)
            sp.wait_ge(a_used, 1)
            for n in range(groups):
                if n + 2 < groups:
                    load_a(n + 2)
                load_b(n)

            def load_block(j, c, first):
                i, s, _ = block_of(j, c)
                if later(i, 2):
                    sp.wait_ge(xgT_ready, i - 1)
                sp.dma_start(xg[:, s], x0_d[bass.ds(first, P), :]
                             ).then_inc(xg_in[s], 16)

            def collect(src, signals):
                by_token = src[1:FREE1].rearrange("(k b p r) d -> k b p r d", k=2, b=B, r=R)
                for b in range(B):
                    for k in range(2):
                        sp.dma_start(back[:, k, b], by_token[k, b]).then_inc(signals[b], 16)

            sp.wait_ge(a_done, a_at[("on", B - 1, R - 1)] + 1)
            sp.dma_start(b3_sb[:, :], b3.rearrange("e d -> (e d)").partition_broadcast(P)).then_inc(b3_in, 16)
            sp.wait_ge(tab_ready, 1)
            sp.wait_ge(a_used, len(a_order))
            sp.wait_ge(sent0, 16 * B * R * 2)
            first = table(mybir.EngineType.SP, 1, 0, LEAD)
            for i in range(LEAD):
                load_block(0, i, first[i])
            with sp.Fori(0, LOOPS) as j:
                first = table(mybir.EngineType.SP, 1, UNROLL * j + LEAD, UNROLL)
                for n in range(UNROLL):
                    load_block(j, LEAD + n, first[n])
            first = table(mybir.EngineType.SP, 1, REST, NB - REST)
            for i in range(REST, NB):
                load_block(0, i, first[i - REST])
            for s in range(2):
                sp.wait_ge(y_out[s], 16 * ((NB - s + 1) // 2))
            collect(y0_d, back_in)

            def load_expert(e):
                if e >= 2:
                    sp.wait_ge(tgT_ready, e - 1)
                whole = e * CAP + (CT - 1) * P
                sp.dma_start(tg[:, e % 2, 0:CT - 1], x1_d[e * CAP:whole, :]
                             .rearrange("(c p) d -> p c d", p=P)).then_inc(tg_in[e % 2], 16)
                sp.dma_start(tg[0:LAST, e % 2, CT - 1], x1_d[whole:whole + LAST, :]
                             ).then_inc(tg_in[e % 2], 16)

            sp.wait_ge(sent1, 16 * B * R * 2)
            for e in range(E):
                load_expert(e)
            for s in range(2):
                sp.wait_ge(z_out[s], 16 * CT * (E // 2))
            collect(y1_d, back1_in)
            for b in range(B):
                sp.wait_ge(r_ready, R * (b + 1))
                sp.dma_start(out[b].rearrange("(p r) d -> p r d", r=R), x_sb[:, b]).then_inc(out_sent, 16)
            sp.wait_ge(out_sent, 16 * B)

        @block.gpsimd
        def _(pool):
            step = stepper(pool, pool_step)
            step(pool.memset(ident[:, :], 0.0))
            pool.affine_select(out=ident[:, :], in_=ident[:, :], compare_op=ALU.not_equal, fill=1.0, base=0,
                               pattern=[[-1, P]], channel_multiplier=1).then_inc(ident_ready, 1)
            for t, v in ((identb, 0.0), (identh, 0.0), (causal_a, 0.0), (causal_b, 0.0), (tri, 1.0),
                         (onesb, 1.0), (hmask, 1.0)):
                last = pool.memset(t[:, :], v)
            pool.memset(mrowzero[:, :, :], 0.0)
            pool.memset(mrowone[:, :, :], 1.0)
            step(pool.memset(early[:, 0:3], 0.0))
            pool.affine_select(out=identb[:, :], in_=identb[:, :], compare_op=ALU.not_equal, fill=1.0,
                               base=0, pattern=[[-1, P]], channel_multiplier=1)
            pool.affine_select(out=identh[:, :], in_=identh[:, :], compare_op=ALU.not_equal, fill=1.0,
                               base=0, pattern=[[-1, P]], channel_multiplier=1)
            pool.affine_select(out=causal_a[:, :], in_=causal_a[:, :], compare_op=ALU.is_ge, fill=MASKED,
                               base=0, pattern=[[-1, P]], channel_multiplier=1)
            pool.affine_select(out=causal_b[:, :], in_=causal_b[:, :], compare_op=ALU.is_ge, fill=MASKED,
                               base=0, pattern=[[1, P]], channel_multiplier=-1)
            pool.affine_select(out=tri[:, :], in_=tri[:, :], compare_op=ALU.is_ge, fill=0.0, base=-1,
                               pattern=[[1, P]], channel_multiplier=-1)
            pool.memset(mrowone[:, :, 1:IMG], 0.0)
            step(pool.affine_select(out=hmask[:, :], in_=hmask[:, :], compare_op=ALU.is_ge, fill=0.0,
                                    base=0, pattern=[[-HD, H]], channel_multiplier=1))
            step(pool.affine_select(out=hmask[:, :], in_=hmask[:, :], compare_op=ALU.is_ge, fill=0.0,
                                    base=HD - 1, pattern=[[HD, H]], channel_multiplier=-1))
            pool.tensor_copy(hsel[:, :, 0], hmask[:, :])
            pool.affine_select(out=place[:, :, 0:HD], in_=place[:, :, 0:HD], compare_op=ALU.not_equal,
                               fill=1.0, base=0, pattern=[[-HD, H], [-1, HD]], channel_multiplier=1)
            at_one = onec[:, :, HD].rearrange("p (g j) -> p g j", j=G)
            pool.affine_select(out=at_one, in_=at_one, compare_op=ALU.not_equal, fill=1.0, base=0,
                               pattern=[[0, NG], [-32, G]], channel_multiplier=1)
            any_f = {"allow_small_or_imprecise_dtypes": True}
            pool.iota(iota_e[:, :, :], [[0, R], [1, E]], base=0, channel_multiplier=0, **any_f)
            pool.iota(base0[:, :], [[SLOTS0, E]], base=0, channel_multiplier=0, **any_f)
            pool.iota(tcut[:, :, :], [[0, E], [P, SLOTS0 // P]], base=0, channel_multiplier=0, **any_f)
            pool.iota(bidx[:, :, :], [[1, NB], [0, E]], base=0, channel_multiplier=0, **any_f)
            for b in range(B):
                for k in range(2):
                    pool.iota(sent[:, b, k].bitcast(I32)[:, :, D], [[1, R]], base=1 + (k * B + b) * S,
                              channel_multiplier=R)
            pool.iota(free_row[:, :, :], [[CT * P, E], [P, CT]], base=FREE1, channel_multiplier=1, **any_f)
            pool.iota(dump[:, :], [[0, 1]], base=DUMP1, channel_multiplier=1, **any_f).then_inc(consts, 1)

            def load_weights(n):
                if n >= W_RING:
                    pool.wait_ge(w_lo, n - W_RING + 1)
                pool.dma_start(w_ring[n % W_RING][:, :, :], w_tile(n)[0].rearrange("e p n -> p e n")
                               ).then_inc(w_in[n % W_RING], 16)

            pool.wait_ge(qka_in[1], 32)
            for n in range(W_RING):
                load_weights(n)
            pool.wait_ge(zeroed, 1)
            x0_clear = x0_d.rearrange("(n p w) c -> n p w c", p=P, w=CLEAR_ROWS)
            x1_clear = x1_d[0:DUMP1].rearrange("(p w) d -> p w d", p=P)
            y1_clear = y1_d[1:FREE1].rearrange("(p w) d -> p w d", p=P)

            def zero_rows(n, width):
                return zeros[:, 0:width].rearrange("p (o c) -> p o c", o=1).broadcast_to([P, n, width])

            clears = [(x0_clear[n], zero_rows(CLEAR_ROWS, 2 * D + 2)) for n in range(N_CLEAR - 2)]
            clears += [(x1_clear, zero_rows(DUMP1 // P, 2 * D + 2).bitcast(F32)),
                       (y1_clear, zero_rows(2 * B * S // P, 2 * D).bitcast(F32))]

            for n in range(W_TILES - W_RING):
                load_weights(n + W_RING)
                if n < len(clears):
                    pool.dma_start(*clears[n]).then_inc(zero_out, 16)

            def dispatch(b, k, slots, dst, signal):
                for r in range(R):
                    row = sent[:, b, k, r, :]
                    pool.indirect_dma_start(
                        dst, bass.IndirectOffsetOnAxis(ap=slots[:, k, b, r:r + 1], axis=0),
                        row.bitcast(F16) if dst is x0_d else row, None).then_inc(signal, 16)

            pool.wait_ge(zero_out, 16 * N_CLEAR)
            pool.wait_ge(slot_ready, 1)
            for k in range(2):
                dispatch(0, k, slot0, x0_d, sent0)
            pool.wait_ge(slot_ready, 2)
            for k in range(2):
                dispatch(1, k, slot0, x0_d, sent0)
            for i in range(NB):
                if i < E // 2:
                    two = slice(2 * i, 2 * i + 2)
                    pool.dma_start(fc_sb[:, two, :], c_fc[two].rearrange("e p n -> p e n")).then_inc(l1w_in, 16)
                    pool.dma_start(cp_sb[:, two], c_proj[two].rearrange("e (c p) n -> p e c n", p=P)
                                   ).then_inc(l1w_in, 16)
                if i == E // 2:
                    pool.dma_start(prb_sb[:, :, :].rearrange("p e d -> p (e d)"),
                                   pr_b.rearrange("e o d -> (e o d)").partition_broadcast(P)
                                   ).then_inc(l1w_in, 16)
                if i:
                    pool.wait_ge(y_out[(i - 1) % 2], 16 * ((i - 1) // 2 + 1))
                pool.wait_ge(y_ready, i + 1)
                pool.indirect_dma_start(
                    y0_d, bass.IndirectOffsetOnAxis(ap=id_now[:, i % 2:i % 2 + 1], axis=0),
                    y_sb[:, i % 2, :], None).then_inc(y_out[i % 2], 16)

            for n in range(2 * B):
                k, b = divmod(n, B)
                if n < 2:
                    pool.wait_ge(slot1_ready, n + 1)
                dispatch(b, k, slot1, x1_d, sent1)
            for e in range(E):
                pool.wait_ge(z_ready, e + 1)
                for c in range(CT):
                    k = P if c < CT - 1 else LAST
                    pool.indirect_dma_start(
                        y1_d, bass.IndirectOffsetOnAxis(ap=id1[0:k, e % 4, c:c + 1], axis=0),
                        z_sb[0:k, e % 2, c, :], None).then_inc(z_out[e % 2], 16)

        @block.scalar
        def _(act):
            act.dma_start(wqkv[:, :], attn_w).then_inc(wqkv_in, 16)
            act.dma_start(uk_sb, uk_w).then_inc(uk_in, 16)
            act.dma_start(uv_sb, uv_w).then_inc(uk_in, 16)
            act.dma_start(vb_bc[:, :], attn_b[2 * D:3 * D].partition_broadcast(P)).then_inc(misc_in, 16)
            act.dma_start(lw_sb, l1w.rearrange("a o i c -> (a o) (i c)")).then_inc(cond_in, 16)
            for b in range(B):
                act.dma_start(cond_bc[:, b, :], cond[b].partition_broadcast(P)).then_inc(cond_in, 16)
            act.dma_start(mask_sb[:, :], mask.rearrange("b i j s -> (b i j) s")).then_inc(mask_in, 16)
            act.dma_start(proj_sb[:, :], proj_w).then_inc(misc_in, 16)
            act.dma_start(gate_sb[:, :], gate_w).then_inc(misc_in, 16)
            act.wait_ge(var_ready, 1)
            act.activation(nrm[:, :, 2], nrm[:, :, 1], ACT.Sqrt).then_inc(sqrt_ready, 1)
            for n in range(2 * B):
                b, i = divmod(n, 2)
                w = IMG + S if i else S
                src = k32[:, b, :] if i else q32[:, b, :]
                act.wait_ge(qkv_ready, n + 1)
                act.copy(part[:, n, 0, 0:w], src).then_inc(hi_ready, 1)
                act.wait_ge(mid_ready, n + 1)
                act.copy(part[:, n, 1, 0:w], res[:, i, 0:w]).then_inc(act_step, 1)

            def high_part(n):
                act.wait_ge(w_in[n % W_RING], 16 * (n // W_RING + 1))
                if n == (HC - 1) * HC:
                    act.wait_ge(zero_out, 16 * N_CLEAR)
                act.activation(w_tile(n)[1][0], w_ring[n % W_RING][:, :, :], ACT.Copy, scale=W_UP
                               ).then_inc(w_hi, 1)

            act.wait_ge(ident_ready, 1)
            act.activation(warm[:, 0:1], ident[:, 0:1], ACT.Exp)
            act.wait_ge(parts_ready, 2 * B)
            for piece in schedule:
                if piece[0] != "s":
                    continue
                _, n, k = piece
                v = s_index(n, k)
                if v in high_at:
                    high_part(high_at.index(v))
                act.wait_ge(s_done, v + 1)
                if k == 0:
                    if n >= 2:
                        act.wait_ge(pv_done, (n - 2) * KC + 1)
                    act.activation(pimg[:, n % 2, :], bank(4 + v % 3), ACT.Exp).then_inc(exp_done, 1)
                    continue
                w = p_index(n, k)
                if w >= P_RING:
                    act.wait_ge(pv_done, chunk_of(w - P_RING) + 1)
                kc, heads, _ = UNITS[k - 1]
                width = heads * (S - kc * P)
                act.activation(p_ring[:, w % P_RING, 0:width], bank(4 + v % 3)[:, 0:width], ACT.Exp
                               ).then_inc(exp_done, 1)

            act.wait_ge(pv_done, groups * KC)
            act.wait_ge(a_done, a_at[("on", B - 1, R - 1)] + 1)
            for n in range(W_EARLY, W_TILES):
                high_part(n)

            def hidden_units(i, e, got, to, bias_row, done):
                for c in range(HC):
                    ins = act.activation(to[:, c * P:(c + 1) * P], got[:, c * P:(c + 1) * P], ACT.Gelu,
                                         bias=cols[:, bass.ds(e * HC + (bias_row + c), 1)], scale=DOWN)
                ins.then_inc(done, 1)

            def gelu1(j, c, e):
                i, s, _ = block_of(j, c)
                act.wait_ge(mm1_done, i + 1)
                if later(i, 1):
                    act.wait_ge(h1_ready, i)
                hidden_units(i, e, bank(1 + s), h32[:, 0], ROW_B1, gelu1_done)

            def gelu2(j, c, e):
                i, s, _ = block_of(j, c)
                act.wait_ge(tz_done, i + 1)
                if later(i, 1):
                    act.wait_ge(h2_ready, i)
                hidden_units(i, e, bank(4), h32[:, 1], ROW_B2, gelu2_done)

            act.activation(warm[:, 1:2], ident[:, 0:1], ACT.Gelu)
            act.wait_ge(tab_ready, 1)
            act.wait_ge(a_used, len(a_order))
            of = table(mybir.EngineType.Activation, 0, 0, LEAD + 2)
            gelu1(0, 0, of[0])
            gelu1(0, 1, of[1])
            for i in range(LEAD):
                gelu1(0, i + 2, of[i + 2])
                gelu2(0, i, of[i])
            with act.Fori(0, LOOPS) as j:
                of = table(mybir.EngineType.Activation, 0, UNROLL * j + LEAD, UNROLL + 2)
                for n in range(UNROLL):
                    gelu1(j, LEAD + n + 2, of[n + 2])
                    gelu2(j, LEAD + n, of[n])
            of = table(mybir.EngineType.Activation, 0, REST, NB - REST)
            for i in range(REST, NB):
                if i + 2 < NB:
                    gelu1(0, i + 2, of[i + 2 - REST])
                gelu2(0, i, of[i - REST])

            for b in range(B):
                act.wait_ge(xcT_done, b + 1)
                act.copy(xcT[:, b].rearrange("p r n -> p (r n)"), bank(XC_BANKS[b][1])).then_inc(xcT_ready, 1)
            act.wait_ge(dl_ready, 1)
            act.activation(th[:, :, :], dl[:, :, :], ACT.Tanh, scale=0.5).then_inc(th_ready, 1)
            act.wait_ge(l1w_in, 16 * (E + 1))
            for e in range(E):
                act.activation(fc16[0][:, e], fc_sb[:, e], ACT.Copy, scale=W_UP)
                act.activation(cp16[0][:, e], cp_sb[:, e].rearrange("p c d -> p (c d)"), ACT.Copy, scale=W_UP
                               ).then_inc(fc_hi, 1)
            for e in range(E):
                for c in range(HC):
                    act.wait_ge(fc_done, e * HC + c + 1)
                    if e and c % 2 == 0:
                        act.wait_ge(hT_ready, 2 * e - 1 + c // 2)
                    act.activation(h1_32[:, c, :], bank(FC_BANKS[c])[:, 0:CAP], ACT.Gelu,
                                   bias=cols[:, ROW_FC + e * HC + c:ROW_FC + e * HC + c + 1], scale=DOWN
                                   ).then_inc(hid_done, 1)
                    if c % 2:
                        act.wait_ge(hid_done, e * HC + c + 1)
                        if e >= 2:
                            act.wait_ge(z_done, e - 1)
                        act.activation(hT[:, e % 2, 0, c - 1:c + 1, :], h1_32[:, c - 1:c + 1, :], ACT.Copy,
                                       scale=IN_UP).then_inc(hT_hi, 1)

        @block.tensor
        def _(pe):
            mm, tr = pe.matmul, pe.transpose
            pe.wait_ge(ident_ready, 1)
            pe.wait_ge(x_in, 16)
            for b in range(B):
                for r in range(R):
                    ins = tr(bank(b)[:, r * P:(r + 1) * P], x_sb[:, b, r, :], ident[:, :])
                ins.then_inc(xT_done, 1)
            pe.wait_ge(rows_in, 16 * 9)
            pe.wait_ge(uk_in, 32)
            tr(bank(2)[:, 0:N_ROWS], rows_sb[0:N_ROWS, :], ident[0:N_ROWS, 0:N_ROWS])
            tr(bank(2)[:, P:2 * P], uk_sb, ident[:, :])
            tr(bank(2)[:, 2 * P:3 * P], uv_sb, ident[:, :]).then_inc(cols_done, 1)
            pe.wait_ge(xT_ready, 1)
            pe.wait_ge(wqkv_in, 16)
            mm(bank(4), wqkv[:, 0:D], xT[:, 0, :], start=True, stop=True).then_inc(qkv_done, 1)
            mm(bank(5), wqkv[:, D:2 * D], xT[:, 0, :], start=True, stop=True).then_inc(qkv_done, 1)
            pe.wait_ge(cols_ready, 1)
            mm(bank(3)[:, 0:B], ukT, cols[:, ROW_IMG:ROW_IMG + B], start=True, stop=True)
            mm(bank(3)[:, B:2 * B], uvT, cols[:, ROW_IMG:ROW_IMG + B], start=True, stop=True
               ).then_inc(img_done, 1)
            pe.wait_ge(xT_ready, 2)
            mm(bank(6), wqkv[:, 0:D], xT[:, 1, :], start=True, stop=True).then_inc(qkv_done, 1)
            mm(bank(7), wqkv[:, D:2 * D], xT[:, 1, :], start=True, stop=True).then_inc(qkv_done, 1)
            for b in range(B):
                for kc in range(KC):
                    ins = mm(bank(b)[:, kc * P:(kc + 1) * P], xT[:, b, kc * P:(kc + 1) * P],
                             wqkv[:, 2 * D:3 * D], start=True, stop=True)
                ins.then_inc(v_done, 1)
            pe.wait_ge(consts, 1)
            for b in range(B):
                pe.wait_ge(vplace_ready, b + 1)
                for g in range(NG):
                    ins = mm(bank(3)[:, g * P:(g + 1) * P],
                             hsel[:, g * G:(g + 1) * G, :].rearrange("p h c -> p (h c)"),
                             vplace[:, g * G:(g + 1) * G, :].rearrange("p h c -> p (h c)"),
                             start=True, stop=True)
                ins.then_inc(vimg_done, 1)
            pe.wait_ge(kbd_ready, 1)
            for b in range(B):
                pe.wait_ge(qkv_ready, 2 * b + 1)
                for t in range(KC):
                    at_c = (b * KC + t) * H
                    ins = mm(bank(2)[:, at_c:at_c + H], q32[:, b, t * P:(t + 1) * P], kimg_bd[:, b, :],
                             start=True, stop=True)
            ins.then_inc(simg_done, 1)
            pe.wait_ge(wc_ready, 1)
            pe.wait_ge(vimg_ready, B)
            for b in range(B):
                ins = tr(bank(3)[:, b * P:(b + 1) * P], wc_sb[:, b, :], ident[:, :])
            ins.then_inc(wcT_done, 1)
            pe.wait_ge(v_ready, B)
            pe.wait_ge(simg_ready, 1)
            pe.wait_ge(wcT_ready, 1)
            pe.wait_ge(qkv_ready, 2 * B)

            def score(n, t, hp):
                b, g = divmod(n, NG)
                pe.wait_ge(qka_in[n % 2], 32 * (n // 2 + 1))
                n_keys = (t + 1) * P
                for i in range(2):
                    j = 2 * hp + i
                    to = a_bank(("score", n, t, hp))[:, i, :]
                    mm(to[:, 0:n_keys], qa[:, n % 2, j, t * P:(t + 1) * P],
                       ka[:, n % 2, j, IMG:IMG + n_keys], start=True, stop=False)
                    ins = mm(to[:, t * P:n_keys], identb[:, :], causal_a[:, :], start=False, stop=True)
                return ins

            def second_scores(n, k):
                v = s_index(n, k)
                to = bank(4 + v % 3)
                if v >= 3:
                    pe.wait_ge(exp_done, v - 2)
                if k == 0:
                    pe.wait_ge(qkb_in[n % 2], 80 * (n // 2 + 1))
                    for j in range(G):
                        ins = mm(to[32 * j:32 * (j + 1), :], kb[:, n % 2, j, 0:IMG], qb[:, n % 2, j, :],
                                 start=True, stop=True, tile_position=(0, 32 * j))
                    return ins
                kc, heads, j0 = UNITS[k - 1]
                width = S - kc * P
                for i in range(heads):
                    mm(to[:, i * width:(i + 1) * width],
                       kb[:, n % 2, j0 + i, IMG + kc * P:IMG + (kc + 1) * P], qb[:, n % 2, j0 + i, kc * P:],
                       start=True, stop=False, skip_group_check=True)
                    ins = mm(to[:, i * width:i * width + P], identb[:, :], causal_b[:, :],
                             start=False, stop=True, skip_group_check=True)
                return ins

            def values(n, kc):
                b, g = divmod(n, NG)
                pe.wait_ge(exp_done, s_index(n, chunk_units(kc)[-1]) + 1)
                if kc == 0:
                    if n:
                        pe.wait_ge(o_ready, n)
                    mm(bank(7), vimg_bd[:, b, g * G:(g + 1) * G, :].rearrange("p h c -> p (h c)"),
                       pimg[:, n % 2, :], start=True, stop=False, skip_group_check=True)
                width = S - kc * P
                for k in chunk_units(kc):
                    _, heads, j0 = UNITS[k - 1]
                    w = p_index(n, k)
                    for i in range(heads):
                        j = j0 + i
                        ins = mm(bank(7)[32 * j:32 * j + HD + 1, kc * P:], v_sb[:, b, kc, g * G + j, :],
                                 p_ring[:, w % P_RING, i * width:(i + 1) * width], start=False,
                                 stop=(kc == KC - 1), tile_position=(0, 32 * j), skip_group_check=True)
                return ins

            for piece in schedule:
                kind, *arg = piece
                if kind == "s":
                    second_scores(*arg).then_inc(s_done, 1)
                    continue
                if kind == "pv":
                    values(*arg).then_inc(pv_done, 1)
                    continue
                if a_at[piece] >= 2:
                    pe.wait_ge(a_used, a_at[piece] - 1)
                to = a_bank(piece)[:, 0, :]
                if kind == "score":
                    ins = score(*arg)
                elif kind == "maxT":
                    pe.wait_ge(m_parts, arg[0] + 1)
                    to = to.bitcast(BF16)
                    for t in range(KC):
                        ins = tr(to[0:3 * G, t * P:(t + 1) * P], mp[:, t, :, :].rearrange("p m h -> p (m h)"),
                                 identb[:, :])
                elif kind == "on":
                    b, r = arg
                    pe.wait_ge(o_ready, (b + 1) * NG)
                    for g in range(NG):
                        ins = tr(to[:, g * P:(g + 1) * P], o_sb[:, (b * NG + g) % O_RING, r::R], ident[:, :])
                elif kind == "onT":
                    b, r = arg
                    pe.wait_ge(a_used, a_at[("on", b, r)] + 1)
                    ins = tr(to[:, 0:P], on_sb[:, r % 2].rearrange("p h d -> p (h d)"), ident[:, :])
                elif kind == "aT":
                    b, = arg
                    pe.wait_ge(misc_in, 48)
                    pe.wait_ge(a_used, a_at[("onT", b, R - 1)] + 1)
                    ins = mm(to, proj_sb[:, :], onT[:, :, :].rearrange("p r q -> p (r q)"), start=True, stop=True)
                elif kind == "a":
                    b, = arg
                    pe.wait_ge(a_used, a_at[("aT", b)] + 1)
                    for r in range(R):
                        ins = tr(to[:, r * P:(r + 1) * P], aT[:, r, :], ident[:, :])
                elif kind == "route":
                    b, = arg
                    pe.wait_ge(a_used, a_at[("aT", b)] + 1)
                    for r in range(R):
                        ins = mm(to[:, r * E:(r + 1) * E], aT[:, r, :], cols[:, ROW_ET:ROW_ET + E],
                                 start=True, stop=True)
                elif kind == "count":
                    b, = arg
                    pe.wait_ge(cnt_ready, b + 1)
                    ins = mm(to[:, 0:E], tri[:, :], cntb[:, 0, b, :], start=True, stop=(b == 0))
                    for b_ in range(b):
                        ins = mm(to[:, 0:E], onesb[:, :], cntb[:, 0, b_, :], start=False, stop=(b_ == b - 1))
                else:
                    for b in range(B):
                        ins = mm(to[:, 0:E], onesb[:, :], cntb[:, 0, b, :], start=(b == 0), stop=(b == B - 1))
                ins.then_inc(a_done, 1)

            def transpose_x(j, c):
                i, s, turn = block_of(j, c)
                pe.wait_ge(xg_in[s], 16 * (turn + 1))
                if later(i, 1):
                    pe.wait_ge(xgT_ready, i)
                to = bank(0).bitcast(F16)
                for q in range(2):
                    ins = tr(to[:, q * P:(q + 1) * P], xg[:, s, q * D:(q + 1) * D], identh[:, :])
                ins.then_inc(tx_done, 1)

            def first_layer(j, c, e):
                i, s, _ = block_of(j, c)
                pe.wait_ge(xgT_ready, i + 1)
                if later(i, 2):
                    pe.wait_ge(gelu1_done, i - 1)
                for m in range(HC):
                    for n, (wq, xq) in enumerate(PRODUCTS):
                        ins = mm(bank(1 + s)[:, m * P:(m + 1) * P], w1_sb[m][wq][:, bass.ds(e * P, P)],
                                 xgT[:, s, xq, :], start=(n == 0), stop=(n == len(PRODUCTS) - 1))
                ins.then_inc(mm1_done, 1)

            def second_layer(j, c, e):
                i, s, _ = block_of(j, c)
                pe.wait_ge(h1_ready, i + 1)
                if later(i, 1):
                    pe.wait_ge(z_copied, i)
                for k in range(HC):
                    for n, (wq, hq) in enumerate(PRODUCTS):
                        ins = mm(bank(3), h1[:, s, hq, k * P:(k + 1) * P], w2_sb[k][wq][:, bass.ds(e * HID, HID)],
                                 start=(k == 0 and n == 0), stop=(k == HC - 1 and n == len(PRODUCTS) - 1))
                ins.then_inc(mm2_done, 1)

            def transpose_z(j, c):
                i, _, _ = block_of(j, c)
                pe.wait_ge(z_copied, i + 1)
                if later(i, 1):
                    pe.wait_ge(gelu2_done, i)
                for m in range(HC):
                    ins = tr(bank(4)[:, m * P:(m + 1) * P], z32[:, m * P:(m + 1) * P], ident[:, :])
                ins.then_inc(tz_done, 1)

            def third_layer(j, c, e):
                i, s, _ = block_of(j, c)
                pe.wait_ge(h2_ready, i + 1)
                if later(i, 1):
                    pe.wait_ge(y_ready, i)
                for k in range(HC):
                    for n, (wq, hq) in enumerate(PRODUCTS):
                        ins = mm(bank(5)[:, 0:D], h2[:, s, hq, k * P:(k + 1) * P],
                                 w3_sb[k][wq][:, bass.ds(e * P, P)], start=(k == 0 and n == 0),
                                 stop=(k == HC - 1 and n == len(PRODUCTS) - 1))
                ins.then_inc(mm3_done, 1)

            pe.wait_ge(tab_ready, 1)
            pe.wait_ge(a_used, len(a_order))
            pe.wait_ge(w_lo, W_EARLY)
            of = table(mybir.EngineType.PE, 0, 0, LEAD + 2)
            transpose_x(0, 0)
            transpose_x(0, 1)
            first_layer(0, 0, of[0])
            transpose_x(0, 2)
            first_layer(0, 1, of[1])
            for i in range(LEAD):
                second_layer(0, i, of[i])
                first_layer(0, i + 2, of[i + 2])
                transpose_x(0, i + 3)
                transpose_z(0, i)
                if i == 0:
                    pe.wait_ge(w_lo, W_TILES)
                if i:
                    third_layer(0, i - 1, of[i - 1])
            with pe.Fori(0, LOOPS) as j:
                of = table(mybir.EngineType.PE, 0, UNROLL * j + (LEAD - 1), UNROLL + 3)
                for n in range(UNROLL):
                    second_layer(j, LEAD + n, of[n + 1])
                    first_layer(j, LEAD + n + 2, of[n + 3])
                    transpose_x(j, LEAD + n + 3)
                    transpose_z(j, LEAD + n)
                    third_layer(j, LEAD + n - 1, of[n])
            of = table(mybir.EngineType.PE, 0, REST - 1, NB - REST + 1)
            for i in range(REST, NB):
                second_layer(0, i, of[i + 1 - REST])
                if i + 2 < NB:
                    first_layer(0, i + 2, of[i + 3 - REST])
                if i + 3 < NB:
                    transpose_x(0, i + 3)
                transpose_z(0, i)
                third_layer(0, i - 1, of[i - REST])
            third_layer(0, NB - 1, of[NB - REST])

            def logits(b):
                pe.wait_ge(xcT_ready, b + 1)
                for r in range(R):
                    ins = mm(bank(2 + b)[:, r * E:(r + 1) * E], xcT[:, b, r, :], gate_sb[:, :], start=True,
                             stop=True)
                ins.then_inc(lg_done, 1)

            for b in range(B):
                for r in range(R):
                    pe.wait_ge(x1_ready, b * R + r + 1)
                    ins = mm(bank(XC_BANKS[b][1])[:, r * D:(r + 1) * D], x_sb[:, b, r, :], wcT_sb[:, b, :],
                             start=True, stop=True)
                ins.then_inc(xcT_done, 1)
                for r in range(R):
                    ins = mm(bank(XC_BANKS[b][0])[:, r * D:(r + 1) * D], wcT_sb[:, b, :], x_sb[:, b, r, :],
                             start=True, stop=True)
                ins.then_inc(xc_done, 1)
                logits(b)
            c1 = cntb[:, :, :, :].rearrange("p k b e -> p (k b) e")
            for n in range(2 * B):
                if n < 2:
                    pe.wait_ge(cnt1_ready, n + 1)
                to = bank(6 if n == 0 else 7)[:, n * E:(n + 1) * E]
                ins = mm(to, tri[:, :], c1[:, n, :], start=True, stop=(n == 0))
                for before in range(n):
                    ins = mm(to, onesb[:, :], c1[:, before, :], start=False, stop=(before == n - 1))
                if n in (0, 2 * B - 1):
                    ins.then_inc(rank1_done, 1)

            def transpose_t(e):
                pe.wait_ge(tg_in[e % 2], 32 * (e // 2 + 1))
                if e >= 2:
                    pe.wait_ge(tgT_ready, e - 1)
                for c in range(CT):
                    k = P if c < CT - 1 else LAST
                    ins = tr(bank(e % 2)[:, c * P:c * P + k], tg[0:k, e % 2, c, 0:D], ident[0:k, 0:k])
                ins.then_inc(tt_done, 1)

            def hidden(e):
                pe.wait_ge(tgT_ready, e + 1)
                for c in range(HC):
                    n = e * HC + c
                    if e:
                        pe.wait_ge(hid_done, n - HC + 1)
                    for i, (wq, xq) in enumerate(PRODUCTS):
                        ins = mm(bank(FC_BANKS[c])[:, 0:CAP], fc16[wq][:, e, c * P:(c + 1) * P],
                                 tgT[:, e % 2, xq, :], start=(i == 0), stop=(i == len(PRODUCTS) - 1))
                    ins.then_inc(fc_done, 1)

            def project(e):
                pe.wait_ge(hT_ready, (e + 1) * 2)
                if e >= 2:
                    pe.wait_ge(z_ready, e - 1)
                for t in range(CT):
                    k = P if t < CT - 1 else LAST
                    for c in range(HC):
                        for i, (wq, hq) in enumerate(PRODUCTS):
                            ins = mm(bank(4 + e % 2)[0:k, t * P:t * P + D],
                                     hT[:, e % 2, hq, c, t * P:t * P + k], cp16[wq][:, e, c * D:(c + 1) * D],
                                     start=(c == 0 and i == 0), stop=(c == HC - 1 and i == len(PRODUCTS) - 1))
                ins.then_inc(z_done, 1)

            pe.wait_ge(fc_lo, E)
            transpose_t(0)
            transpose_t(1)
            hidden(0)
            for e in range(E):
                if e + 2 < E:
                    transpose_t(e + 2)
                if e + 1 < E:
                    hidden(e + 1)
                project(e)

        @block.vector
        def _(dve):
            step = stepper(dve, dve_step)
            tt, ts, copy = dve.tensor_tensor, dve.tensor_scalar, dve.tensor_copy
            dve.memset(zeros[:, :], 0.0).then_inc(zeroed, 1)
            dve.memset(v_sb[:, :, :, :, HD:HD + 1].rearrange("p b k h i -> p (b k h) i"), 1.0)

            dve.wait_ge(cond_in, 48)
            for b in range(B):
                step(dve.scalar_tensor_tensor(out=wc_sb[:, b, :], in0=lw_sb, scalar=float(D) ** -0.5,
                                              in1=cond_bc[:, b, :], op0=ALU.mult, op1=ALU.mult))
                step(dve.tensor_tensor_reduce(out=sq_sb, in0=wc_sb[:, b, :], in1=wc_sb[:, b, :], scale=1.0,
                                              scalar=0.0, op0=ALU.mult, op1=ALU.add,
                                              accum_out=nrm[:, b, 0:1]))
            ts(nrm[:, :, 1], nrm[:, :, 0], 1e-8, None, ALU.add).then_inc(var_ready, 1)
            dve.wait_ge(mask_in, 16)
            step(copy(mpart[:, 0, :], mask_sb[:, :]))
            step(tt(mres[:, :], mask_sb[:, :], mpart[:, 0, :], ALU.subtract))
            step(copy(mpart[:, 1, :], mres[:, :]))
            tt(mpart[:, 2, :], mres[:, :], mpart[:, 1, :], ALU.subtract).then_inc(mask_ready, 1)

            for b in range(B):
                dve.wait_ge(xT_done, b + 1)
                copy(xT[:, b, :].rearrange("d (p r) -> d r p", r=R),
                     bank(b).rearrange("d (r p) -> d r p", r=R)).then_inc(xT_ready, 1)
            dve.wait_ge(cols_done, 1)
            copy(cols[:, :], bank(2)[:, 0:N_ROWS])
            copy(ukT, bank(2)[:, P:2 * P])
            copy(uvT, bank(2)[:, 2 * P:3 * P]).then_inc(cols_ready, 1)
            dve.wait_ge(cols_ready, 1)

            def qkv(n):
                b, i = divmod(n, 2)
                dve.wait_ge(qkv_done, n + 1)
                if i == 0:
                    ts(q32[:, b, :], bank(4 + n), cols[:, ROW_QKV:ROW_QKV + 1], SM_SCALE, ALU.add, ALU.mult
                       ).then_inc(qkv_ready, 1)
                else:
                    ts(k32[:, b, IMG:], bank(4 + n), cols[:, ROW_QKV + 1:ROW_QKV + 2], None, ALU.add
                       ).then_inc(qkv_ready, 1)

            def residue(n):
                b, i = divmod(n, 2)
                w = IMG + S if i else S
                src = k32[:, b, :] if i else q32[:, b, :]
                dve.wait_ge(hi_ready, n + 1)
                tt(res[:, i, 0:w], src, part[:, n, 0, 0:w], ALU.subtract).then_inc(mid_ready, 1)

            def last_part(n):
                b, i = divmod(n, 2)
                w = IMG + S if i else S
                dve.wait_ge(act_step, n + 1)
                tt(part[:, n, 2, 0:w], res[:, i, 0:w], part[:, n, 1, 0:w], ALU.subtract
                   ).then_inc(parts_ready, 1)

            qkv(0)
            dve.wait_ge(img_done, 1)
            dve.memset(k32[:, :, 0:IMG], 0.0)
            step(ts(vimg[:, :], bank(3)[:, B:2 * B], cols[:, ROW_UV:ROW_UV + 1], None, ALU.add))
            step(ts(k32[:, :, 0], bank(3)[:, 0:B], cols[:, ROW_UK:ROW_UK + 1], None, ALU.add))
            qkv(1)
            residue(0)
            dve.wait_ge(consts, 1)
            for b in range(B):
                ins = ts(kimg_bd[:, b, :], hmask[:, :], k32[:, b, 0:1], None, ALU.mult)
            ins.then_inc(kbd_ready, 1)
            last_part(0)
            residue(1)
            ts(vplace, place, vimg[:, 0:1], None, ALU.mult).then_inc(vplace_ready, 1)
            qkv(2)
            last_part(1)
            qkv(3)
            for b in range(B):
                dve.wait_ge(v_done, b + 1)
                tt(v_sb[:, b, :, :, 0:HD], bank(b).rearrange("p (k h d) -> p k h d", k=KC, h=H),
                   vb_bc[:, :].rearrange("p (o h d) -> p o h d", o=1, h=H).broadcast_to([P, KC, H, HD]),
                   ALU.add).then_inc(v_ready, 1)
            dve.wait_ge(vimg_done, 1)
            tt(vimg_bd[:, 0], bank(3).rearrange("p (h c) -> p h c", c=32), onec, ALU.add
               ).then_inc(vimg_ready, 1)
            ts(vplace, place, vimg[:, 1:2], None, ALU.mult).then_inc(vplace_ready, 1)
            residue(2)
            dve.wait_ge(sqrt_ready, 1)
            step(dve.reciprocal(nrm[:, :, 3], nrm[:, :, 2]))
            step(tt(nrm[:, :, 4], nrm[:, :, 3], nrm[:, :, 3], ALU.mult))
            step(tt(nrm[:, :, 5], nrm[:, :, 4], nrm[:, :, 1], ALU.mult))
            step(ts(nrm[:, :, 6], nrm[:, :, 5], -0.5, 1.5, ALU.mult, ALU.add))
            step(tt(nrm[:, :, 7], nrm[:, :, 6], nrm[:, :, 3], ALU.mult))
            last_part(2)
            residue(3)
            for b in range(B):
                ins = ts(wc_sb[:, b, :], wc_sb[:, b, :], nrm[:, b, 7:8], None, ALU.mult)
            ins.then_inc(wc_ready, 1)
            last_part(3)
            dve.wait_ge(vimg_done, 2)
            tt(vimg_bd[:, 1], bank(3).rearrange("p (h c) -> p h c", c=32), onec, ALU.add
               ).then_inc(vimg_ready, 1)
            dve.wait_ge(simg_done, 1)
            copy(simg[:, :, :, :].rearrange("p b t h -> p (b t h)"), bank(2)[:, 0:B * KC * H]
                 ).then_inc(simg_ready, 1)
            dve.wait_ge(wcT_done, 1)
            copy(wcT_sb[:, :, :].rearrange("p b i -> p (b i)"), bank(3)[:, 0:B * P]).then_inc(wcT_ready, 1)
            dve.wait_ge(simg_ready, 1)

            def low_part(n):
                dve.wait_ge(w_hi, n + 1)
                _, (hi, lo) = w_tile(n)
                dve.scalar_tensor_tensor(out=lo, in0=w_ring[n % W_RING][:, :, :], scalar=W_UP, in1=hi,
                                         op0=ALU.mult, op1=ALU.subtract).then_inc(w_lo, 1)

            def maxima(n, first, last):
                b, g = divmod(n, NG)
                mine = slice(g * G, (g + 1) * G)
                if first == 0:
                    dve.wait_ge(a_used, a_at[("score", n, KC - 1, G // 2 - 1)] + 1)
                    if n:
                        dve.wait_ge(a_done, a_at[("maxT", n - 1)] + 1)
                for at_step in range(first, last):
                    if at_step == 0:
                        step(tt(mr[:, :, :], mA[:, b, :, mine], simg[:, b, :, mine], ALU.max))
                    elif at_step == 1:
                        step(ts(negm[:, :, :], mr[:, :, :], -1.0, None, ALU.mult))
                    elif at_step == 2:
                        step(copy(mp[:, :, 0, :], negm[:, :, :]))
                    elif at_step == 3:
                        step(tt(mr[:, :, :], negm[:, :, :], mp[:, :, 0, :], ALU.subtract))
                    elif at_step == 4:
                        step(copy(mp[:, :, 1, :], mr[:, :, :]))
                    else:
                        tt(mp[:, :, 2, :], mr[:, :, :], mp[:, :, 1, :], ALU.subtract).then_inc(m_parts, 1)

            def choose(b):
                for r in range(R):
                    ins = dve.max(top_v[:, b, r, :], lg[:, b, r, :])
                step(ins)
                for r in range(R):
                    ins = dve.max_index(top_i[:, b, r, :], top_v[:, b, r, :], lg[:, b, r, :])
                step(ins)
                step(copy(top_f[:, b, :, 0:2], top_i[:, b, :, 0:2]))
                for k in range(2):
                    ins = tt(oh[:, k, b], iota_e[:, :, :], top_f[:, b, :, k:k + 1].broadcast_to([P, R, E]),
                             ALU.is_equal)
                step(ins)

            for piece in schedule:
                kind, *arg = piece
                if kind == "s":
                    if s_index(*arg) in low_at:
                        low_part(low_at.index(s_index(*arg)))
                    continue
                if kind == "pv":
                    n, kc = arg
                    if kc == KC - 1:
                        dve.wait_ge(pv_done, (n + 1) * KC)
                        if n >= O_RING:
                            dve.wait_ge(a_done, a_at[("on", (n - O_RING) // NG, R - 1)] + 1)
                        copy(o_sb[:, n % O_RING, :], bank(7)).then_inc(o_ready, 1)
                    continue
                dve.wait_ge(a_done, a_at[piece] + 1)
                got = a_bank(piece)
                flat = got[:, 0, :]
                if kind == "score":
                    n, t, hp = arg
                    b, g = divmod(n, NG)
                    dve.tensor_reduce(mA[:, b, t, g * G + 2 * hp:g * G + 2 * hp + 2],
                                      got[:, :, 0:(t + 1) * P], AX_X, ALU.max).then_inc(a_used, 1)
                    if n and t == 0:
                        maxima(n - 1, 3 * hp, 3 * hp + 3)
                    if (n, t, hp) == (groups - 1, KC - 1, G // 2 - 1):
                        maxima(n, 0, 6)
                elif kind == "maxT":
                    n, = arg
                    if n >= 2:
                        dve.wait_ge(qkb_in[n % 2], 80 * (n // 2))
                    copy(mrow[:, n % 2, :], flat.bitcast(BF16)[0:3 * G, 0:S]).then_inc(a_used, 1)
                elif kind == "on":
                    b, r = arg
                    view = flat.rearrange("p (h c) -> p h c", c=32)
                    dve.wait_ge(a_used, a_at[piece])
                    step(dve.reciprocal(rden[:, :], view[:, :, HD]))
                    tt(on_sb[:, r % 2], view[:, :, 0:HD],
                       rden[:, :].rearrange("p (h o) -> p h o", o=1).broadcast_to([P, H, HD]), ALU.mult
                       ).then_inc(a_used, 1)
                elif kind == "onT":
                    b, r = arg
                    copy(onT[:, r, :], flat[:, 0:P]).then_inc(a_used, 1)
                elif kind == "aT":
                    b, = arg
                    ts(aT[:, :, :].rearrange("p r q -> p (r q)"), flat, cols[:, ROW_PROJ:ROW_PROJ + 1], None,
                       ALU.add).then_inc(a_used, 1)
                elif kind == "a":
                    b, = arg
                    parts, again = (sent[:, b, k].bitcast(F16) for k in range(2))
                    got_a = flat.rearrange("p (r d) -> p r d", r=R)
                    step(ts(parts[:, :, 0:D], got_a, IN_UP, None, ALU.mult))
                    dve.scalar_tensor_tensor(out=parts[:, :, D:2 * D], in0=got_a, scalar=IN_UP,
                                             in1=parts[:, :, 0:D], op0=ALU.mult, op1=ALU.subtract
                                             ).then_inc(a_used, 1)
                    dve.wait_ge(a_used, a_at[piece] + 1)
                    copy(again[:, :, 0:2 * D], parts[:, :, 0:2 * D])
                elif kind == "route":
                    b, = arg
                    copy(lg[:, b].rearrange("p r e -> p (r e)"), flat[:, 0:R * E]).then_inc(a_used, 1)
                    dve.wait_ge(a_used, a_at[piece] + 1)
                    choose(b)
                    step(tt(ohsum[:, b], oh[:, 0, b], oh[:, 1, b], ALU.add))
                    step(dve.tensor_reduce(cnt[:, 0, b, :], ohsum[:, b].rearrange("p r e -> p e r"), AX_X,
                                           ALU.add))
                    copy(cntb[:, 0, b, :], cnt[:, 0, b, :]).then_inc(cnt_ready, 1)
                elif kind == "count":
                    b, = arg
                    tt(rank[:, 0, b, 0, :], flat[:, 0:E], base0[:, :], ALU.add).then_inc(a_used, 1)
                    dve.wait_ge(a_used, a_at[piece] + 1)
                    for r in range(1, R):
                        step(tt(rank[:, 0, b, r, :], rank[:, 0, b, r - 1, :], ohsum[:, b, r - 1, :], ALU.add))
                    for k in range(2):
                        ins = tt(pick[:, k, b], oh[:, k, b], rank[:, 0, b], ALU.mult)
                    step(ins)
                    step(dve.tensor_reduce(slot_f[:, :, b, :], pick[:, :, b], AX_X, ALU.add))
                    copy(slot0[:, :, b, :], slot_f[:, :, b, :]).then_inc(slot_ready, 1)
                else:
                    tot = flat[0:1, 0:E]
                    tt(nbge[:, :, :], tcut[:, :, :],
                       tot.rearrange("p (e o) -> p e o", o=1).broadcast_to([1, E, SLOTS0 // P]), ALU.is_lt
                       ).then_inc(a_used, 1)
                    dve.wait_ge(a_used, a_at[piece] + 1)
                    step(dve.tensor_reduce(nblk[:, :], nbge[:, :, :], AX_X, ALU.add))
                    step(dve.tensor_tensor_scan(cumb[:, :], nblk[:, :], nblk[:, :], 0.0, ALU.add, ALU.bypass))
                    wide = [1, NB, E]
                    step(tt(ended[:, :, :], cumb[0:1, :].rearrange("p (o e) -> p o e", o=1).broadcast_to(wide),
                            bidx[:, :, :], ALU.is_le))
                    step(tt(endblk[:, :, :], ended[:, :, :],
                            nblk[0:1, :].rearrange("p (o e) -> p o e", o=1).broadcast_to(wide), ALU.mult))
                    dve.tensor_reduce(tabf[:, 0, :], ended[:, :, :], AX_X, ALU.add)
                    step(dve.tensor_reduce(tabf[:, 1, :], endblk[:, :, :], AX_X, ALU.add))
                    step(tt(tabf[:, 2, :], bidx[:, :, 0], tabf[:, 1, :], ALU.subtract))
                    step(ts(tabf[:, 3, :], tabf[:, 2, :], float(P), None, ALU.mult))
                    step(dve.scalar_tensor_tensor(out=tabf[:, 4, :], in0=tabf[:, 0, :], scalar=float(SLOTS0),
                                                  in1=tabf[:, 3, :], op0=ALU.mult, op1=ALU.add))
                    ts(tab[:, 0, :], tabf[:, 0, :], float(E - 1), None, ALU.min)
                    ts(tab[:, 1, :], tabf[:, 4, :], float(E * SLOTS0 - P), None, ALU.min
                       ).then_inc(tab_ready, 1)

            def copy_x(j, c):
                i, s, _ = block_of(j, c)
                dve.wait_ge(tx_done, i + 1)
                if later(i, 2):
                    dve.wait_ge(mm1_done, i - 1)
                copy(id_all[:, bass.ds(i, 1)], xg[:, s, 2 * D:].bitcast(I32))
                copy(xgT[:, s].rearrange("p q n -> p (q n)"), bank(0).bitcast(F16)[:, 0:2 * P]
                     ).then_inc(xgT_ready, 1)

            def copy_z(j, c):
                i, _, _ = block_of(j, c)
                dve.wait_ge(mm2_done, i + 1)
                if later(i, 1):
                    dve.wait_ge(tz_done, i)
                copy(z32[:, :], bank(3)).then_inc(z_copied, 1)

            def split_1(j, c):
                i, s, _ = block_of(j, c)
                dve.wait_ge(gelu1_done, i + 1)
                if later(i, 2):
                    dve.wait_ge(mm2_done, i - 1)
                ts(h1[:, s, 0, :], h32[:, 0], IN_UP, None, ALU.mult).then_inc(hi1_ready, 1)
                dve.wait_ge(hi1_ready, i + 1)
                dve.scalar_tensor_tensor(out=h1[:, s, 1, :], in0=h32[:, 0], scalar=IN_UP, in1=h1[:, s, 0, :],
                                         op0=ALU.mult, op1=ALU.subtract).then_inc(h1_ready, 1)

            def split_2(j, c):
                i, s, _ = block_of(j, c)
                dve.wait_ge(gelu2_done, i + 1)
                if later(i, 2):
                    dve.wait_ge(mm3_done, i - 1)
                ts(h2[:, s, 0, :], h32[:, 1], IN_UP, None, ALU.mult).then_inc(hi2_ready, 1)
                dve.wait_ge(hi2_ready, i + 1)
                dve.scalar_tensor_tensor(out=h2[:, s, 1, :], in0=h32[:, 1], scalar=IN_UP, in1=h2[:, s, 0, :],
                                         op0=ALU.mult, op1=ALU.subtract).then_inc(h2_ready, 1)

            def result(j, c, e):
                i, s, turn = block_of(j, c)
                dve.wait_ge(mm3_done, i + 1)
                if later(i, 2):
                    dve.wait_ge(y_out[s], 16 * turn)
                dve.wait_ge(xgT_ready, i + 1)
                copy(id_now[:, s:s + 1], id_all[:, bass.ds(i, 1)])
                dve.scalar_tensor_tensor(out=y_sb[:, s, :], in0=bank(5)[:, 0:D], scalar=DOWN,
                                         in1=b3_sb[:, bass.ds(e * D, D)], op0=ALU.mult, op1=ALU.add
                                         ).then_inc(y_ready, 1)

            for n in range(W_EARLY, W_TILES):
                low_part(n)
            dve.wait_ge(tab_ready, 1)
            dve.wait_ge(b3_in, 16)
            of = table(mybir.EngineType.DVE, 0, 0, LEAD)
            copy_x(0, 0)
            copy_x(0, 1)
            split_1(0, 0)
            copy_x(0, 2)
            split_1(0, 1)
            for i in range(LEAD):
                copy_z(0, i)
                copy_x(0, i + 3)
                split_1(0, i + 2)
                if i:
                    result(0, i - 1, of[i - 1])
                split_2(0, i)
            with dve.Fori(0, LOOPS) as j:
                of = table(mybir.EngineType.DVE, 0, UNROLL * j + (LEAD - 1), UNROLL)
                for n in range(UNROLL):
                    copy_z(j, LEAD + n)
                    copy_x(j, LEAD + n + 3)
                    split_1(j, LEAD + n + 2)
                    result(j, LEAD + n - 1, of[n])
                    split_2(j, LEAD + n)
            of = table(mybir.EngineType.DVE, 0, REST - 1, NB - REST + 1)
            for i in range(REST, NB):
                copy_z(0, i)
                if i + 3 < NB:
                    copy_x(0, i + 3)
                if i + 2 < NB:
                    split_1(0, i + 2)
                result(0, i - 1, of[i - REST])
                split_2(0, i)
            result(0, NB - 1, of[NB - REST])

            for b in range(B):
                dve.wait_ge(back_in[b], 32)
                step(tt(back[:, 0, b], back[:, 0, b], back[:, 1, b], ALU.add))
                for r in range(R):
                    dve.scalar_tensor_tensor(out=x_sb[:, b, r, :], in0=back[:, 0, b, r, :], scalar=0.5,
                                             in1=x_sb[:, b, r, :], op0=ALU.mult, op1=ALU.add
                                             ).then_inc(x1_ready, 1)
            dve.memset(tg[:, :, CT - 1, :], 0.0)

            def copy_xc(b):
                dve.wait_ge(xc_done, b + 1)
                for k in range(2):
                    ins = copy(sent[:, b, k, :, 0:D], bank(XC_BANKS[b][0]).rearrange("p (r d) -> p r d", d=D))
                ins.then_inc(xc_ready, 1)

            def choices(b):
                dve.wait_ge(lg_done, b + 1)
                step(copy(lg[:, b].rearrange("p r e -> p (r e)"), bank(2 + b)[:, 0:R * E]))
                choose(b)
                step(dve.tensor_reduce(cnt[:, :, b, :], oh[:, :, b].rearrange("p k r e -> p k e r"), AX_X,
                                       ALU.add))
                copy(cntb[:, :, b, :], cnt[:, :, b, :]).then_inc(cnt1_ready, 1)

            def slots(first, last, got):
                n = last - first
                sets = "p k b r e -> p (k b) r e"
                rank_s = rank[:, :, :, :, :].rearrange(sets)[:, first:last]
                oh_s = oh[:, :, :, :, :].rearrange(sets)[:, first:last]
                step(copy(rank_s[:, :, 0, :], got.rearrange("p (q e) -> p q e", e=E)))
                for r in range(1, R):
                    step(tt(rank_s[:, :, r, :], rank_s[:, :, r - 1, :], oh_s[:, :, r - 1, :], ALU.add))
                flat4 = lambda t: t.rearrange("p q r e -> p (q r) e")
                flat3 = lambda t: t[:, :, :, :].rearrange("p k b r -> p (k b r)")[:, first * R:last * R]
                pick_f = flat4(pick[:, :, :, :, :].rearrange(sets)[:, first:last])
                step(tt(pick_f, flat4(oh_s), flat4(rank_s), ALU.mult))
                step(dve.tensor_reduce(flat3(rank_f), pick_f, AX_X, ALU.add))
                ts(flat3(keep), flat3(rank_f), float(CAP), None, ALU.is_lt)
                for q in range(first, last):
                    ins = dve.scalar_tensor_tensor(out=slot_f[:, q // B, q % B, :], in0=top_f[:, q % B, :, q // B],
                                                   scalar=float(CAP), in1=rank_f[:, q // B, q % B, :],
                                                   op0=ALU.mult, op1=ALU.add)
                step(ins)
                step(dve.scalar_tensor_tensor(out=flat3(slot_f), in0=flat3(slot_f), scalar=dump[:, 0:1],
                                              in1=flat3(keep), op0=ALU.subtract, op1=ALU.mult))
                ts(flat3(slot1), flat3(slot_f), dump[:, 0:1], None, ALU.add).then_inc(slot1_ready, 1)

            choices(0)
            copy_xc(0)
            dve.wait_ge(rank1_done, 1)
            slots(0, 1, bank(6)[:, 0:E])
            choices(1)
            copy_xc(1)
            dve.wait_ge(rank1_done, 2)
            slots(1, 2 * B, bank(7)[:, E:2 * B * E])
            tt(dl[:, :, :], top_v[:, :, :, 0], top_v[:, :, :, 1], ALU.subtract).then_inc(dl_ready, 1)
            dve.wait_ge(th_ready, 1)
            ts(p_sb[:, 0], th[:, :, :], 0.5, 0.5, ALU.mult, ALU.add)
            step(ts(p_sb[:, 1], th[:, :, :], -0.5, 0.5, ALU.mult, ALU.add))

            def copy_t(e):
                dve.wait_ge(tt_done, e + 1)
                if e >= 2:
                    dve.wait_ge(fc_done, (e - 1) * HC)
                if e >= 4:
                    dve.wait_ge(z_out[e % 2], 16 * CT * (e // 2 - 1))
                ids = tg[:, e % 2].bitcast(I32)
                step(ts(is_free[:, :], ids[:, :, D], 0.0, None, ALU.is_equal))
                step(tt(is_free[:, :], is_free[:, :], free_row[:, e, :], ALU.mult))
                tt(id1[:, e % 4, :], is_free[:, :], ids[:, :, D], ALU.add)
                step(ts(tgT[:, e % 2, 0, :], bank(e % 2)[:, 0:CAP], IN_UP, None, ALU.mult))
                dve.scalar_tensor_tensor(out=tgT[:, e % 2, 1, :], in0=bank(e % 2)[:, 0:CAP], scalar=IN_UP,
                                         in1=tgT[:, e % 2, 0, :], op0=ALU.mult, op1=ALU.subtract
                                         ).then_inc(tgT_ready, 1)

            def split_h(e):
                for half in range(2):
                    mine = slice(2 * half, 2 * half + 2)
                    dve.wait_ge(hT_hi, 2 * e + half + 1)
                    dve.scalar_tensor_tensor(out=hT[:, e % 2, 1, mine, :], in0=h1_32[:, mine, :], scalar=IN_UP,
                                             in1=hT[:, e % 2, 0, mine, :], op0=ALU.mult, op1=ALU.subtract
                                             ).then_inc(hT_ready, 1)

            def add_bias(e):
                dve.wait_ge(z_done, e + 1)
                if e >= 2:
                    dve.wait_ge(z_out[e % 2], 16 * CT * (e // 2))
                got = bank(4 + e % 2)
                dve.scalar_tensor_tensor(out=z_sb[:, e % 2, 0:CT - 1, :],
                                         in0=got[:, 0:(CT - 1) * D].rearrange("p (c d) -> p c d", d=D),
                                         scalar=DOWN, in1=prb_sb[:, e:e + 1, :].broadcast_to([P, CT - 1, D]),
                                         op0=ALU.mult, op1=ALU.add)
                dve.scalar_tensor_tensor(out=z_sb[0:LAST, e % 2, CT - 1, :],
                                         in0=got[0:LAST, (CT - 1) * D:CT * D], scalar=DOWN,
                                         in1=prb_sb[0:LAST, e, :], op0=ALU.mult, op1=ALU.add
                                         ).then_inc(z_ready, 1)

            dve.wait_ge(l1w_in, 16 * (E + 1))
            for e in range(E):
                dve.wait_ge(fc_hi, e + 1)
                for raw, (hi, lo) in ((fc_sb[:, e], fc16), (cp_sb[:, e].rearrange("p c d -> p (c d)"), cp16)):
                    ins = dve.scalar_tensor_tensor(out=lo[:, e], in0=raw, scalar=W_UP, in1=hi[:, e],
                                                   op0=ALU.mult, op1=ALU.subtract)
                ins.then_inc(fc_lo, 1)
            copy_t(0)
            copy_t(1)
            split_h(0)
            for e in range(E):
                if e + 2 < E:
                    copy_t(e + 2)
                if e + 1 < E:
                    split_h(e + 1)
                add_bias(e)

            for q in range(B * R):
                b, r = divmod(q, R)
                if r == 0:
                    dve.wait_ge(back1_in[b], 32)
                step(dve.scalar_tensor_tensor(out=x_sb[:, b, r, :], in0=back[:, 0, b, r, :],
                                              scalar=p_sb[:, 0, b, r:r + 1], in1=x_sb[:, b, r, :],
                                              op0=ALU.mult, op1=ALU.add))
                dve.scalar_tensor_tensor(out=x_sb[:, b, r, :], in0=back[:, 1, b, r, :],
                                         scalar=p_sb[:, 1, b, r:r + 1], in1=x_sb[:, b, r, :],
                                         op0=ALU.mult, op1=ALU.add).then_inc(r_ready, 1)


_INS = ['x', 'cond_1024', 'mask_Bx1x1xS_ff0', 'L0_cond_c_attn_w', 'L0_cond_c_attn_b', 'L0_cond_c_proj_w',
        'L0_cond_c_proj_b', 'L0_cond_uk_w', 'L0_cond_uk_b', 'L0_cond_uv_w', 'L0_cond_uv_b',
        'L0_ffn_expert_tokens', 'L0_ffn_W1', 'L0_ffn_b1', 'L0_ffn_W2', 'L0_ffn_b2', 'L0_ffn_W3', 'L0_ffn_b3',
        'L1_cond_weight', 'L1_ffn_gate_w', 'L1_ffn_c_fc', 'L1_ffn_fc_bias', 'L1_ffn_c_proj',
        'L1_ffn_proj_bias']
_OUTS = [((B, S, D), 'float32')]


def kernel(**inputs):
    import numpy as _np
    import concourse.bacc as _bacc
    from concourse import mybir as _mybir
    from concourse.bass_utils import run_bass_kernel_spmd as _run

    nc = _bacc.Bacc("TRN2", target_bir_lowering=False, num_devices=1)
    arrays, args = {}, []
    for name in _INS:
        a = _np.ascontiguousarray(inputs[name])
        arrays[f"in_{name}_dram"] = a
        args.append(nc.dram_tensor(f"in_{name}_dram", a.shape, _mybir.dt.from_np(a.dtype), kind="ExternalInput").ap())
    for i, (shape, dtype) in enumerate(_OUTS):
        dt = _mybir.dt.from_np(_np.dtype(dtype))
        args.append(nc.dram_tensor(f"out_{i}_dram", shape, dt, kind="ExternalOutput").ap())
    build(nc, *args)
    r = _run(nc, [arrays], core_ids=[0])
    return r.results[0]["out_0_dram"]
```

```python
from contextlib import ExitStack

import concourse.bass as bass
from concourse import mybir

ALU = mybir.AluOpType
ACT = mybir.ActivationFunctionType
F32 = mybir.dt.float32
BF16 = mybir.dt.bfloat16
F16 = mybir.dt.float16
I32 = mybir.dt.int32
U32 = mybir.dt.uint32
AX_X = mybir.AxisListType.X

P = 128
B, S, D = 2, 512, 128
R = S // P
H, HD = 16, 8
G = 4
NG = H // G
KC = S // P
E = 8
HID = 512
HC = HID // P
SM_SCALE = float(HD) ** -0.5
MASKED = -30000.0

Q_PART = (0, 0, 1, 1, 0, 2)
K_PART = (0, 1, 0, 1, 2, 0)
PROD_ROWS = len(Q_PART) * HD
MASK_ROW = PROD_ROWS
MAX_ROW = MASK_ROW + 3
ROWS = MAX_ROW + 3

IMG = 32

LEAD = 3
SLOTS0 = B * S
NB = (2 * B * S + E * (P - 1) + LEAD) // P
CAP = int(1.25 * B * S * 2 / E)
CT = -(-CAP // P)
LAST = CAP - (CT - 1) * P
CLEAR_ROWS = 16
N_CLEAR = E * SLOTS0 // P // CLEAR_ROWS + 2
IN_UP = 16.0
W_UP = 128.0
DOWN = 1.0 / (IN_UP * W_UP)
PRODUCTS = ((0, 0), (0, 1), (1, 0))
W_TILES = HC * HC + 2 * HC
W_EARLY = HC * HC + HC
W_RING = 4
UNROLL = 4
LOOPS = (NB - LEAD - 4) // UNROLL
REST = LEAD + LOOPS * UNROLL
DUMP1 = E * CAP
EARLY = 2
PREPARED = 5
W3_POOL = 2

ROW_B1, ROW_B2, ROW_FC, ROW_QKV, ROW_PROJ, ROW_UK, ROW_UV, ROW_ET, ROW_IMG = (
    0, E * HC, 2 * E * HC, 3 * E * HC, 3 * E * HC + 3, 3 * E * HC + 4, 3 * E * HC + 5,
    3 * E * HC + 6, 3 * E * HC + 6 + E)
N_ROWS = ROW_IMG + B


def score_units():
    out = []
    for kc in range(KC):
        heads = 1 if kc < 2 else kc if kc == 2 else 4
        out += [(kc, heads, j) for j in range(0, G, heads)]
    return out


UNITS = score_units()
NU = len(UNITS)
P_RING = 8
O_RING = 6
LAG = 2


def build(nc, x, cond, mask, attn_w, attn_b, proj_w, proj_b, uk_w, uk_b, uv_w, uv_b,
          et, W1, b1, W2, b2, W3, b3, l1w, gate_w, c_fc, fc_b, c_proj, pr_b, out):
    ctx = ExitStack()
    with ctx:
        def dram(name, shape, dt):
            return nc.dram_tensor(name, shape, dt).ap()

        def sem(name):
            return ctx.enter_context(nc.semaphore(name))

        q_rows_d = [dram(f"q_rows{b}", (MAX_ROW, H, S), BF16) for b in range(B)]
        k_rows_d = [dram(f"k_rows{b}", (ROWS, H, IMG + S), BF16) for b in range(B)]
        FREE1 = 1 + 2 * B * S
        x0_d = dram("x0_slots", (E * SLOTS0, 2 * D + 2), F16)
        x1_d = dram("x1_slots", (DUMP1 + 2 * B * S, D + 1), F32)
        y0_d = dram("y0_rows", (FREE1, D), F32)
        y1_d = dram("y1_rows", (FREE1 + E * CT * P, D), F32)

        def sb(name, shape, dt=F32, stack=ctx):
            return stack.enter_context(nc.sbuf_tensor(name, shape, dt))

        w2_sb = [[sb(f"w2_sb{k}{q}", [P, E * HID], F16) for q in range(2)] for k in range(HC)]
        zeros = w2_sb[HC - 1][0]
        w1_sb = [[sb(f"w1_sb{m}{q}", [P, E * P], F16) for q in range(2)] for m in range(HC)]
        w_ring = [sb(f"w_ring{n}", [P, E, P]) for n in range(W_RING)]
        x_sb = sb("x_sb", [P, B, R, D])
        sent = sb("sent", [P, B, 2, R, D + 1])
        ident = sb("ident", [P, P])
        identh = sb("identh", [P, P], F16)
        identb = sb("identb", [P, P], BF16)
        tri = sb("tri", [P, P], BF16)
        onesb = sb("onesb", [P, P], BF16)
        cols = sb("cols", [P, N_ROWS])
        gate_sb = sb("gate_sb", [P, E])
        wc_sb = sb("wc_sb", [P, B, P])
        wcT_sb = sb("wcT_sb", [P, B, P])
        iota_e = sb("iota_e", [P, R, E])
        base0 = sb("base0", [P, E])
        tcut = sb("tcut", [1, E, SLOTS0 // P])
        bidx = sb("bidx", [1, NB, E])
        warm = sb("warm", [P, 2])
        dump = sb("dump", [P, 2 * B * R])
        rank_d = sb("rank_d", [P, 2, B, R])
        lg = sb("lg", [P, B, R, E])
        free_row = sb("free_row", [P, E, CT])
        is_free = sb("is_free", [P, CT])
        top_v = sb("top_v", [P, B, R, 8])
        top_i = sb("top_i", [P, B, R, 8], U32)
        top_f = sb("top_f", [P, B, R, 8])
        oh = sb("oh", [P, 2, B, R, E])
        ohsum = sb("ohsum", [P, B, R, E])
        cnt = sb("cnt", [P, 2, B, E])
        cntb = sb("cntb", [P, 2, B, E], BF16)
        rank = sb("rank", [P, 2, B, R, E])
        pick = sb("pick", [P, 2, B, R, E])
        slot_f = sb("slot_f", [P, 2, B, R])
        rank_f = sb("rank_f", [P, 2, B, R])
        keep = sb("keep", [P, 2, B, R])
        slot0 = sb("slot0", [P, 2, B, R], I32)
        slot1 = sb("slot1", [P, 2, B, R], I32)
        p_sb = sb("p_sb", [P, 2, B, R])
        dl = sb("dl", [P, B, R])
        th = sb("th", [P, B, R])
        sel = sb("sel", [P, B, R, E])
        slot_no = sb("slot_no", [P, CAP], F16)
        nbge = sb("nbge", [1, E, SLOTS0 // P])
        nblk = sb("nblk", [1, E])
        cumb = sb("cumb", [1, E])
        ended = sb("ended", [1, NB, E])
        endblk = sb("endblk", [1, NB, E])
        tabf = sb("tabf", [1, 5, NB])
        tab = sb("tab", [1, 2, NB], I32)

        with ExitStack() as at:
            with ExitStack() as pre:
                early = sb("early", [P, 4, H, 32], F32, pre)
                hsel, place, onec, vplace = (early[:, n] for n in range(4))
                k32 = sb("k32", [P, B, IMG + S], F32, pre)
                xT = sb("xT", [P, B, S], F32, pre)
                q32 = sb("q32", [P, B, S], F32, pre)
                part = sb("part", [P, 2 * B, 3, IMG + S], BF16, pre)
                wqkv = sb("wqkv", [P, 3 * D], F32, pre)
                mask_sb = sb("mask_sb", [B, S], F32, pre)
                mres = sb("mres", [B, S], F32, pre)
                mpart = sb("mpart", [B, 3, S], BF16, pre)
                mrowone = sb("mrowone", [H, 3, IMG + S], BF16, pre)
                mrowzero = sb("mrowzero", [H, 3, IMG], BF16, pre)
                vb_bc = sb("vb_bc", [P, D], F32, pre)
                cond_bc = sb("cond_bc", [P, B, D], F32, pre)
                res = sb("res", [P, 2, IMG + S], F32, pre)
                lw_sb, sq_sb, uk_sb, uv_sb, ukT, uvT = (
                    sb(n, [P, P], F32, pre)[:, :] for n in ("lw", "sq", "uk", "uv", "ukT", "uvT"))
            p_ring = sb("p_ring", [P, P_RING, S], F32, at)
            o_sb = sb("o_sb", [P, O_RING, S], F32, at)
            qb = sb("qb", [ROWS, 2, G, S], BF16, at)
            kb = sb("kb", [ROWS, 2, G, IMG + S], BF16, at)
            onT = sb("onT", [P, R, P], F32, at)
            aT = sb("aT", [P, R, P], F32, at)
            pimg = sb("pimg", [P, 2, S], F32, at)
            mrow = sb("mrow", [3 * G, 2, S], BF16, at)
            on_sb = sb("on_sb", [P, 2, H, HD], F32, at)
            mA = sb("mA", [P, B, KC, H], F32, at)
            qa = sb("qa", [MAX_ROW, 2, G, S], BF16, at)
            ka = sb("ka", [MAX_ROW, 2, G, IMG + S], BF16, at)
            rows_sb = sb("rows_sb", [P, D], F32, at)
            proj_sb = sb("proj_sb", [P, D], F32, at)
            nrm = sb("nrm", [P, B, 8], F32, at)
            causal_a = sb("causal_a", [P, P], BF16, at)
            causal_b = sb("causal_b", [P, P], BF16, at)
            hmask = sb("hmask", [P, H], F32, at)
            v_sb = sb("v_sb", [P, B, KC, H, HD + 1], F32, at)
            vimg = sb("vimg", [P, B], F32, at)
            kimg_bd = sb("kimg_bd", [P, B, H], F32, at)
            vimg_bd = sb("vimg_bd", [P, B, H, 32], F32, at)
            simg = sb("simg", [P, B, KC, H], F32, at)
            negm = sb("negm", [P, KC, G], F32, at)
            mr = sb("mr", [P, KC, G], F32, at)
            mp = sb("mp", [P, KC, 3, G], BF16, at)
            rden = sb("rden", [P, H], F32, at)

        w3_sb = [[sb(f"w3_sb{k}{q}", [P, E * P], F16) for q in range(2)] for k in range(HC)]
        b3_sb = sb("b3_sb", [P, E * D])
        fc_sb = sb("fc_sb", [P, E, HID])
        cp_sb = sb("cp_sb", [P, E, HC, D])
        prb_sb = sb("prb_sb", [P, E, D])
        back = sb("back", [P, 2, B, R, D])
        early0 = back[:, :, :, :, :].rearrange("p k b r d -> p (k b r d)").bitcast(F16)
        onehot0 = early0[:, 0:LEAD * B * R * P].rearrange("p (i q n) -> p i q n", i=LEAD, q=B * R)
        xg_lead = early0[:, LEAD * B * R * P:LEAD * (B * R * P + 2 * D + 2)].rearrange("p (i n) -> p i n", i=LEAD)
        id_all = sb("id_all", [P, NB], I32)
        id_now = sb("id_now", [P, 2], I32)
        id1 = sb("id1", [P, E, CT], I32)
        xcT = sb("xcT", [P, B, R, P])
        with ExitStack() as f0:
            xg = sb("xg", [P, 2, 2 * D + 2], F16, f0)
            xgT = sb("xgT", [P, 2, 2, P], F16, f0)
            h32 = sb("h32", [P, 2, HID], F32, f0)
            z32 = sb("z32", [P, HID], F32, f0)
            h1 = sb("h1", [P, 2, 2, HID], F16, f0)
            h2 = sb("h2", [P, 2, 2, HID], F16, f0)
            y_sb = sb("y_sb", [P, 2, D], F32, f0)
        tg = sb("tg", [P, 2, CT, D + 1])
        tgT = sb("tgT", [P, 2, 2, CAP], F16)
        hT = sb("hT", [P, 2, 2, HC, CAP], F16)
        z_sb = [sb(f"z_sb{n}", [P, CT, D]) for n in range(2)]
        z_sb += [w1_sb[n][1][:, :].bitcast(F32)[:, 0:CT * D].rearrange("p (c d) -> p c d", c=CT) for n in range(2)]
        fc16, cp16 = ([t[:, :].rearrange("p (e n) -> p e n", e=E) for t in w2_sb[k]] for k in range(2))
        onehot = [t[:, 0:B * R * CAP].rearrange("p (q n) -> p q n", q=B * R)
                  for t in (w2_sb[2][1], w2_sb[3][1])]
        xc16 = [w2_sb[3][0][:, q * B * R * D:(q + 1) * B * R * D].rearrange("p (b n) -> p b n", b=B)
                for q in range(2)]
        tg_early = [w1_sb[e][0][:, :].bitcast(F32)[:, 0:CT * (D + 1)].rearrange("p (c d) -> p c d", c=CT)
                    for e in range(EARLY)]
        h1_32 = w2_sb[2][0][:, :].bitcast(F32)[:, 0:HC * CAP].rearrange("p (c n) -> p c n", c=HC)

        def sems(names):
            return [sem(n) for n in names.split()]

        (x_in, rows_in, wqkv_in, uk_in, cond_in, mask_in, misc_in, b3_in, w_up, w_hi, w_lo, w_lo_pool, l1w_in,
         zero_out) = sems(
            "x_in rows_in wqkv_in uk_in cond_in mask_in misc_in b3_in w_up w_hi w_lo w_lo_pool l1w_in "
            "zero_out")
        w_in = [sem(f"w_in{n}") for n in range(W_RING)]
        pool_step, dve_step, act_step, ident_ready, consts, zeroed = sems(
            "pool_step dve_step act_step ident_ready consts zeroed")
        (xT_done, xT_ready, cols_done, cols_ready, img_done, qkv_done, qkv_ready, hi_ready,
         mid_ready, parts_ready, v_done, v_ready, simg_done, simg_ready, vimg_done, vimg_ready,
         var_ready, sqrt_ready, wc_ready, wcT_done, wcT_ready, mask_ready, kbd_ready, vplace_ready) = sems(
            "xT_done xT_ready cols_done cols_ready img_done qkv_done qkv_ready hi_ready "
            "mid_ready parts_ready v_done v_ready simg_done simg_ready vimg_done vimg_ready "
            "var_ready sqrt_ready wc_ready wcT_done wcT_ready mask_ready kbd_ready vplace_ready")
        rows_out = [sem(f"rows_out{n}") for n in range(2 * B)]
        krest_out = [sem(f"krest_out{b}") for b in range(B)]
        a_done, a_used, m_parts, s_done, exp_done, pv_done, o_ready, cnt_ready, slot_ready, tab_ready = sems(
            "a_done a_used m_parts s_done exp_done pv_done o_ready cnt_ready slot_ready tab_ready")
        qka_in = [sem(f"qka_in{n}") for n in range(2)]
        qkb_in = [sem(f"qkb_in{n}") for n in range(2)]
        sent0, tx_done, xgT_ready, mm1_done, gelu1_done, h1_ready, mm2_done, gelu2_done, h2_ready, \
            mm3_done, y_ready = sems(
                "sent0 tx_done xgT_ready mm1_done gelu1_done h1_ready mm2_done gelu2_done h2_ready "
                "mm3_done y_ready")
        hi1_ready, hi2_ready, z_copied, tz_done = sems("hi1_ready hi2_ready z_copied tz_done")
        xg_in = [sem(f"xg_in{n}") for n in range(2)]
        lead_in, marked, id_copied = sems("lead_in marked id_copied")
        y_out = [sem(f"y_out{n}") for n in range(2)]
        back_in = [sem(f"back_in{n}") for n in range(B)]
        x1_ready, xc_done, xc_ready, xcT_done, xcT_ready, lg_done, cnt1_ready, rank1_done, slot1_ready, dl_ready, \
            th_ready, sent1 = sems(
                "x1_ready xc_done xc_ready xcT_done xcT_ready lg_done cnt1_ready rank1_done slot1_ready dl_ready "
                "th_ready sent1")
        fc_hi, fc_lo, hid_done, hT_hi = sems("fc_hi fc_lo hid_done hT_hi")
        xc_hi, xc_lo, onehot_ready, early_done, tgT_hi, early_in, id_ready, p_ready, weighted = sems(
            "xc_hi xc_lo onehot_ready early_done tgT_hi early_in id_ready p_ready weighted")
        tt_done, tgT_ready, fc_done, hT_ready, z_done, z_ready, r_ready, out_sent = sems(
            "tt_done tgT_ready fc_done hT_ready z_done z_ready r_ready out_sent")
        tg_in = [sem(f"tg_in{n}") for n in range(2)]
        z_out = [sem(f"z_out{n}") for n in range(4)]
        back1_in = [sem(f"back1_in{n}") for n in range(B)]

        def stepper(eng, stepped):
            steps = 0

            def step(ins):
                nonlocal steps
                steps += 1
                ins.then_inc(stepped, 1)
                eng.wait_ge(stepped, steps)

            return step

        groups = B * NG

        def a_pieces(n):
            out = [("score", n, t, hp) for t in range(KC) for hp in range(G // 2)] if n < groups else []
            if 1 <= n <= groups:
                out.insert(4 if n < groups else 0, ("maxT", n - 1))
            return out

        def chunk_units(kc):
            return [k + 1 for k, u in enumerate(UNITS) if u[0] == kc]

        def b_pieces():
            out = [[] for _ in range(groups + 1)]
            for c in range(groups * KC + 1):
                n, kc = divmod(c, KC)
                if c < groups * KC:
                    units = ([0] if kc == 0 else []) + chunk_units(kc)
                    out[n] += [("s", n, k) for k in units]
                if c:
                    out[n] += [("pv", *divmod(c - 1, KC))]
            out[groups - 1] += out.pop()
            return out

        def tail(b):
            out = [("on", b, 0), ("on", b, 1), ("onT", b, 0), ("on", b, 2), ("onT", b, 1), ("on", b, 3),
                   ("onT", b, 2), ("onT", b, 3)]
            return out + [("aT", b), ("route", b), ("a", b), ("count", b)]

        def merged(one, two):
            at = sorted([(i / len(one), 0, p) for i, p in enumerate(one)]
                        + [((i + 0.5) / len(two), 1, p) for i, p in enumerate(two)], key=lambda q: q[:2])
            return [p for _, _, p in at]

        by_group = b_pieces()
        schedule = []
        for n in range(groups + LAG):
            first = a_pieces(n) if n < groups + 1 else []
            if n == groups - 1:
                first = first + tail(0)
            schedule += merged(first, by_group[n - LAG] if n >= LAG else [])
        schedule += tail(1) + [("total",)]
        a_order = [p for p in schedule if p[0] not in ("s", "pv")]
        a_at = {p: i for i, p in enumerate(a_order)}

        pair = [ctx.enter_context(nc.psum_tensor(f"pair{n}", [P, 2, 512], F32)) for n in range(2)]
        single = [ctx.enter_context(nc.psum_tensor(f"bank{n}", [P, 512], F32)) for n in range(4, 8)]

        def bank(n):
            return pair[n // 2][:, n % 2, :] if n < 4 else single[n - 4][:, :]

        FC_BANKS = (2, 3, 6, 7)
        XC_BANKS = ((0, 1), (4, 5))

        def a_bank(piece):
            return pair[a_at[piece] % 2]

        def s_index(n, k):
            return n * (NU + 1) + k

        def p_index(n, k):
            return n * NU + k - 1

        def chunk_of(w):
            n, k = divmod(w, NU)
            return n * KC + UNITS[k][0]

        def block_of(j, c):
            return UNROLL * j + c, c % 2, UNROLL // 2 * j + c // 2

        def later(count, least):
            return not isinstance(count, int) or count >= least

        def table(eng, row, first, n):
            _, values = nc.values_load_multi_w_load_instructions(
                tab[0:1, row, bass.ds(first, n)], engines=[eng], min_val=0,
                max_val=(E - 1) if row == 0 else E * SLOTS0 - P,
                skip_runtime_bounds_check_because="the table's values are clamped when it is made")
            return values

        def w_tile(n):
            cols_of = lambda c: slice(c * P, (c + 1) * P)
            by_expert = lambda t, at: t[:, :].rearrange("p (e n) -> p e n", e=E)[:, :, at]
            if n < HC * HC:
                k, m = divmod(n, HC)
                return W2[:, cols_of(k), cols_of(m)], [by_expert(t, cols_of(m)) for t in w2_sb[k]]
            k = (n - HC * HC) % HC
            if n < HC * HC + HC:
                return W1[:, :, cols_of(k)], [by_expert(t, cols_of(0)) for t in w1_sb[k]]
            return W3[:, cols_of(k), :], [by_expert(t, cols_of(0)) for t in w3_sb[k]]

        sparse = 9
        high_at = [14 + 7 * n if n < sparse else 73 + 2 * (n - sparse) for n in range(W_EARLY)]
        low_at = [v + (4 if n < sparse else 2) for n, v in enumerate(high_at)]


        block = ctx.enter_context(nc.Block())

        @block.sync
        def _(sp):
            sp.dma_start(x_sb[:, :, :, :], x.rearrange("b (p r) d -> p b r d", r=R)).then_inc(x_in, 16)
            for at_row, n, src in (
                    (ROW_B1, E * HC, b1.rearrange("e (c p) -> (e c) p", p=P)),
                    (ROW_B2, E * HC, b2.rearrange("e (c p) -> (e c) p", p=P)),
                    (ROW_FC, E * HC, fc_b.rearrange("e o (c p) -> (e o c) p", p=P)),
                    (ROW_QKV, 3, attn_b.rearrange("(c p) -> c p", p=P)),
                    (ROW_PROJ, 1, proj_b.rearrange("(c p) -> c p", p=P)),
                    (ROW_UK, 1, uk_b.rearrange("(c p) -> c p", p=P)),
                    (ROW_UV, 1, uv_b.rearrange("(c p) -> c p", p=P)),
                    (ROW_ET, E, et),
                    (ROW_IMG, B, cond)):
                sp.dma_start(rows_sb[at_row:at_row + n, :], src).then_inc(rows_in, 16)

            def store_parts(b):
                for i in range(2):
                    n = 2 * b + i
                    sp.wait_ge(parts_ready, n + 1)
                    rows, which = (k_rows_d[b], K_PART) if i else (q_rows_d[b], Q_PART)
                    width = IMG + S if i else S
                    for c, m in enumerate(which):
                        sp.dma_start(rows[c * HD:(c + 1) * HD].rearrange("d h t -> h d t"),
                                     part[:, n, m, 0:width]).then_inc(rows_out[n], 16)

            sp.wait_ge(consts, 1)
            for b in range(B):
                sp.dma_start(q_rows_d[b][MASK_ROW:MAX_ROW].rearrange("r h t -> h r t"),
                             mrowone[:, :, IMG:]).then_inc(krest_out[b], 16)
                sp.dma_start(k_rows_d[b][MAX_ROW:ROWS].rearrange("r h t -> h r t"),
                             mrowone[:, :, :]).then_inc(krest_out[b], 16)
                sp.dma_start(k_rows_d[b][MASK_ROW:MAX_ROW, :, 0:IMG].rearrange("r h t -> h r t"),
                             mrowzero[:, :, :]).then_inc(krest_out[b], 16)
            sp.wait_ge(mask_ready, 1)
            for b in range(B):
                for m in range(3):
                    sp.dma_start(k_rows_d[b][MASK_ROW + m:MASK_ROW + m + 1, :, IMG:],
                                 mpart[b:b + 1, m:m + 1, :].broadcast_to([1, H, S])
                                 ).then_inc(krest_out[b], 16)

            def rows_stored(b):
                sp.wait_ge(rows_out[2 * b], 16 * len(Q_PART))
                sp.wait_ge(rows_out[2 * b + 1], 16 * len(K_PART))
                sp.wait_ge(krest_out[b], 16 * 6)

            def load_a(n):
                b, g = divmod(n, NG)
                if n >= 2:
                    sp.wait_ge(a_done, a_at[("score", n - 2, KC - 1, G // 2 - 1)] + 1)
                sp.dma_start(qa[:, n % 2], q_rows_d[b][:, g * G:(g + 1) * G, :]).then_inc(qka_in[n % 2], 16)
                sp.dma_start(ka[:, n % 2], k_rows_d[b][0:MAX_ROW, g * G:(g + 1) * G, :]
                             ).then_inc(qka_in[n % 2], 16)

            def load_b(n):
                b, g = divmod(n, NG)
                if n >= 2:
                    sp.wait_ge(s_done, s_index(n - 1, 0))
                sp.dma_start(qb[0:MAX_ROW, n % 2], q_rows_d[b][:, g * G:(g + 1) * G, :]
                             ).then_inc(qkb_in[n % 2], 16)
                sp.dma_start(kb[:, n % 2], k_rows_d[b][:, g * G:(g + 1) * G, :]).then_inc(qkb_in[n % 2], 16)
                sp.wait_ge(a_used, a_at[("maxT", n)] + 1)
                for m in range(3):
                    sp.dma_start(qb[MAX_ROW + m:MAX_ROW + m + 1, n % 2], mrow[m * G:(m + 1) * G, n % 2, :]
                                 ).then_inc(qkb_in[n % 2], 16)

            store_parts(0)
            rows_stored(0)
            load_a(0)
            load_a(1)
            store_parts(1)
            rows_stored(1)
            sp.wait_ge(a_done, 1)
            sp.wait_ge(a_used, 1)
            for n in range(groups):
                if n + 2 < groups:
                    load_a(n + 2)
                load_b(n)

            def load_block(j, c, first):
                i, s, _ = block_of(j, c)
                sp.wait_ge(xgT_ready, i - 1)
                sp.dma_start(xg[:, s], x0_d[bass.ds(first, P), :]
                             ).then_inc(xg_in[s], 16)

            def collect(src, signals):
                by_token = src[1:FREE1].rearrange("(k b p r) d -> k b p r d", k=2, b=B, r=R)
                for b in range(B):
                    for k in range(2):
                        sp.dma_start(back[:, k, b], by_token[k, b]).then_inc(signals[b], 16)

            sp.wait_ge(a_done, a_at[("on", B - 1, R - 1)] + 1)
            sp.dma_start(b3_sb[:, :], b3.rearrange("e d -> (e d)").partition_broadcast(P)).then_inc(b3_in, 16)
            sp.wait_ge(tab_ready, 1)
            sp.wait_ge(a_used, len(a_order))
            sp.wait_ge(sent0, 16 * B * R * 2)
            for i in range(LEAD):
                sp.dma_start(xg_lead[:, i, :], x0_d[i * SLOTS0:i * SLOTS0 + P, :]).then_inc(lead_in, 16)
            with sp.Fori(0, LOOPS) as j:
                first = table(mybir.EngineType.SP, 1, UNROLL * j + LEAD, UNROLL)
                for n in range(UNROLL):
                    load_block(j, LEAD + n, first[n])
            first = table(mybir.EngineType.SP, 1, REST, NB - REST)
            for i in range(REST, NB):
                load_block(0, i, first[i - REST])
            for s in range(2):
                sp.wait_ge(y_out[s], 16 * ((NB - s + 1) // 2))
            collect(y0_d, back_in)

            def load_expert(e, to, signal):
                if e >= EARLY + 2:
                    sp.wait_ge(tgT_ready, e - 1)
                whole = e * CAP + (CT - 1) * P
                sp.dma_start(to[:, 0:CT - 1], x1_d[e * CAP:whole, :]
                             .rearrange("(c p) d -> p c d", p=P)).then_inc(signal, 16)
                sp.dma_start(to[0:LAST, CT - 1], x1_d[whole:whole + LAST, :]).then_inc(signal, 16)

            sp.wait_ge(sent1, 16 * B * R * 2)
            for e in (EARLY, EARLY + 1, *range(EARLY), *range(EARLY + 2, E)):
                if e < EARLY:
                    load_expert(e, tg_early[e], early_in)
                else:
                    load_expert(e, tg[:, e % 2], tg_in[e % 2])
            for s in range(4):
                sp.wait_ge(z_out[s], 16 * CT * (E // 4))
            collect(y1_d, back1_in)
            for b in range(B):
                sp.wait_ge(r_ready, b + 1)
                sp.dma_start(out[b].rearrange("(p r) d -> p r d", r=R), x_sb[:, b]).then_inc(out_sent, 16)
            sp.wait_ge(out_sent, 16 * B)

        @block.gpsimd
        def _(pool):
            step = stepper(pool, pool_step)
            step(pool.memset(ident[:, :], 0.0))
            pool.affine_select(out=ident[:, :], in_=ident[:, :], compare_op=ALU.not_equal, fill=1.0, base=0,
                               pattern=[[-1, P]], channel_multiplier=1).then_inc(ident_ready, 1)
            for t, v in ((identb, 0.0), (identh, 0.0), (causal_a, 0.0), (causal_b, 0.0), (tri, 1.0),
                         (onesb, 1.0), (hmask, 1.0)):
                last = pool.memset(t[:, :], v)
            pool.memset(mrowzero[:, :, :], 0.0)
            pool.memset(mrowone[:, :, :], 1.0)
            step(pool.memset(early[:, 0:3], 0.0))
            pool.affine_select(out=identb[:, :], in_=identb[:, :], compare_op=ALU.not_equal, fill=1.0,
                               base=0, pattern=[[-1, P]], channel_multiplier=1)
            pool.affine_select(out=identh[:, :], in_=identh[:, :], compare_op=ALU.not_equal, fill=1.0,
                               base=0, pattern=[[-1, P]], channel_multiplier=1)
            pool.affine_select(out=causal_a[:, :], in_=causal_a[:, :], compare_op=ALU.is_ge, fill=MASKED,
                               base=0, pattern=[[-1, P]], channel_multiplier=1)
            pool.affine_select(out=causal_b[:, :], in_=causal_b[:, :], compare_op=ALU.is_ge, fill=MASKED,
                               base=0, pattern=[[1, P]], channel_multiplier=-1)
            pool.affine_select(out=tri[:, :], in_=tri[:, :], compare_op=ALU.is_ge, fill=0.0, base=-1,
                               pattern=[[1, P]], channel_multiplier=-1)
            pool.memset(mrowone[:, :, 1:IMG], 0.0)
            step(pool.affine_select(out=hmask[:, :], in_=hmask[:, :], compare_op=ALU.is_ge, fill=0.0,
                                    base=0, pattern=[[-HD, H]], channel_multiplier=1))
            step(pool.affine_select(out=hmask[:, :], in_=hmask[:, :], compare_op=ALU.is_ge, fill=0.0,
                                    base=HD - 1, pattern=[[HD, H]], channel_multiplier=-1))
            pool.tensor_copy(hsel[:, :, 0], hmask[:, :])
            pool.affine_select(out=place[:, :, 0:HD], in_=place[:, :, 0:HD], compare_op=ALU.not_equal,
                               fill=1.0, base=0, pattern=[[-HD, H], [-1, HD]], channel_multiplier=1)
            at_one = onec[:, :, HD].rearrange("p (g j) -> p g j", j=G)
            pool.affine_select(out=at_one, in_=at_one, compare_op=ALU.not_equal, fill=1.0, base=0,
                               pattern=[[0, NG], [-32, G]], channel_multiplier=1)
            any_f = {"allow_small_or_imprecise_dtypes": True}
            pool.iota(slot_no[:, :], [[1, CAP]], base=1, channel_multiplier=0, **any_f)
            pool.iota(iota_e[:, :, :], [[0, R], [1, E]], base=0, channel_multiplier=0, **any_f)
            pool.iota(base0[:, :], [[SLOTS0, E]], base=0, channel_multiplier=0, **any_f)
            step(pool.iota(tcut[:, :, :], [[0, E], [P, SLOTS0 // P]], base=0, channel_multiplier=0, **any_f))
            pool.memset(tcut[:, 0:LEAD, 0], float(2 * B * S))
            pool.iota(tab[:, 0, 0:LEAD], [[1, LEAD]], base=0, channel_multiplier=0)
            pool.iota(tab[:, 1, 0:LEAD], [[SLOTS0, LEAD]], base=0, channel_multiplier=0)
            pool.iota(bidx[:, :, :], [[1, NB], [0, E]], base=-LEAD, channel_multiplier=0, **any_f)
            for b in range(B):
                for k in range(2):
                    pool.iota(sent[:, b, k].bitcast(I32)[:, :, D], [[1, R]], base=1 + (k * B + b) * S,
                              channel_multiplier=R)
            pool.iota(free_row[:, :, :], [[CT * P, E], [P, CT]], base=FREE1, channel_multiplier=1, **any_f)
            pool.iota(dump[:, :], [[P, 2 * B * R]], base=DUMP1, channel_multiplier=1, **any_f).then_inc(consts, 1)

            def load_weights(n):
                if n >= W_RING:
                    pool.wait_ge(w_lo, n - W_RING + 1)
                pool.dma_start(w_ring[n % W_RING][:, :, :], w_tile(n)[0].rearrange("e p n -> p e n")
                               ).then_inc(w_in[n % W_RING], 16)

            pool.wait_ge(qka_in[1], 32)
            for n in range(W_RING):
                load_weights(n)
            pool.wait_ge(zeroed, 1)
            x0_clear = x0_d.rearrange("(n p w) c -> n p w c", p=P, w=CLEAR_ROWS)
            x1_clear = x1_d[0:DUMP1].rearrange("(p w) d -> p w d", p=P)
            y1_clear = y1_d[1:FREE1].rearrange("(p w) d -> p w d", p=P)

            def zero_rows(n, width):
                return zeros[:, 0:width].rearrange("p (o c) -> p o c", o=1).broadcast_to([P, n, width])

            clears = [(x0_clear[n], zero_rows(CLEAR_ROWS, 2 * D + 2)) for n in range(N_CLEAR - 2)]
            clears += [(x1_clear, zero_rows(DUMP1 // P, 2 * D + 2).bitcast(F32)),
                       (y1_clear, zero_rows(2 * B * S // P, 2 * D).bitcast(F32))]

            for n in range(W_TILES - W_RING):
                load_weights(n + W_RING)
                if n < len(clears):
                    pool.dma_start(*clears[n]).then_inc(zero_out, 16)

            def dispatch(b, k, slots, dst, signal):
                for r in range(R):
                    row = sent[:, b, k, r, :]
                    pool.indirect_dma_start(
                        dst, bass.IndirectOffsetOnAxis(ap=slots[:, k, b, r:r + 1], axis=0),
                        row.bitcast(F16) if dst is x0_d else row, None).then_inc(signal, 16)

            pool.wait_ge(zero_out, 16 * N_CLEAR)
            pool.wait_ge(slot_ready, 1)
            for k in range(2):
                dispatch(0, k, slot0, x0_d, sent0)
            pool.wait_ge(slot_ready, 2)
            for k in range(2):
                dispatch(1, k, slot0, x0_d, sent0)
            for n in range(W_TILES - W3_POOL, W_TILES):
                pool.wait_ge(w_hi, n + 1)
                hi, lo = w_tile(n)[1]
                pool.tensor_tensor(lo, w_ring[n % W_RING][:, :, :], hi, ALU.subtract).then_inc(w_lo_pool, 1)
            for i in range(NB):
                if i < E // 2:
                    two = slice(2 * i, 2 * i + 2)
                    pool.dma_start(fc_sb[:, two, :], c_fc[two].rearrange("e p n -> p e n")).then_inc(l1w_in, 16)
                    pool.dma_start(cp_sb[:, two], c_proj[two].rearrange("e (c p) n -> p e c n", p=P)
                                   ).then_inc(l1w_in, 16)
                if i == E // 2:
                    pool.dma_start(prb_sb[:, :, :].rearrange("p e d -> p (e d)"),
                                   pr_b.rearrange("e o d -> (e o d)").partition_broadcast(P)
                                   ).then_inc(l1w_in, 16)
                if i:
                    pool.wait_ge(y_out[(i - 1) % 2], 16 * ((i - 1) // 2 + 1))
                if i == 0:
                    pool.wait_ge(lead_in, 16 * LEAD)
                pool.wait_ge(y_ready, i + 1)
                ids = id_now[:, i % 2:i % 2 + 1] if i >= LEAD - 1 else xg_lead[:, i, 2 * D:].bitcast(I32)
                pool.indirect_dma_start(
                    y0_d, bass.IndirectOffsetOnAxis(ap=ids, axis=0),
                    y_sb[:, i % 2, :], None).then_inc(y_out[i % 2], 16)

            for n in range(2 * B):
                k, b = divmod(n, B)
                if n < 2:
                    pool.wait_ge(xc_ready, 2 * (n + 1))
                    pool.wait_ge(slot1_ready, n + 1)
                dispatch(b, k, slot1, x1_d, sent1)
            for e in range(E):
                pool.wait_ge(z_ready, e + 1)
                if e < EARLY:
                    pool.wait_ge(id_ready, e + 1)
                for c in range(CT):
                    k = P if c < CT - 1 else LAST
                    pool.indirect_dma_start(
                        y1_d, bass.IndirectOffsetOnAxis(ap=id1[0:k, e, c:c + 1], axis=0),
                        z_sb[e % 4][0:k, c, :], None).then_inc(z_out[e % 4], 16)

        @block.scalar
        def _(act):
            act.dma_start(wqkv[:, :], attn_w).then_inc(wqkv_in, 16)
            act.dma_start(uk_sb, uk_w).then_inc(uk_in, 16)
            act.dma_start(uv_sb, uv_w).then_inc(uk_in, 16)
            act.dma_start(vb_bc[:, :], attn_b[2 * D:3 * D].partition_broadcast(P)).then_inc(misc_in, 16)
            act.dma_start(lw_sb, l1w.rearrange("a o i c -> (a o) (i c)")).then_inc(cond_in, 16)
            for b in range(B):
                act.dma_start(cond_bc[:, b, :], cond[b].partition_broadcast(P)).then_inc(cond_in, 16)
            act.dma_start(mask_sb[:, :], mask.rearrange("b i j s -> (b i j) s")).then_inc(mask_in, 16)
            act.dma_start(proj_sb[:, :], proj_w).then_inc(misc_in, 16)
            act.dma_start(gate_sb[:, :], gate_w).then_inc(misc_in, 16)
            act.wait_ge(var_ready, 1)
            act.activation(nrm[:, :, 2], nrm[:, :, 1], ACT.Sqrt).then_inc(sqrt_ready, 1)
            for n in range(2 * B):
                b, i = divmod(n, 2)
                w = IMG + S if i else S
                src = k32[:, b, :] if i else q32[:, b, :]
                act.wait_ge(qkv_ready, n + 1)
                act.copy(part[:, n, 0, 0:w], src).then_inc(hi_ready, 1)
                act.wait_ge(mid_ready, n + 1)
                act.copy(part[:, n, 1, 0:w], res[:, i, 0:w]).then_inc(act_step, 1)

            def high_part(n):
                act.wait_ge(w_in[n % W_RING], 16 * (n // W_RING + 1))
                if n == (HC - 1) * HC:
                    act.wait_ge(zero_out, 16 * N_CLEAR)
                tile, hi = w_ring[n % W_RING][:, :, :], w_tile(n)[1][0]
                if n >= W_TILES - W3_POOL:
                    act.activation(tile, tile, ACT.Copy, scale=W_UP).then_inc(w_up, 1)
                    act.wait_ge(w_up, n - (W_TILES - W3_POOL) + 1)
                    act.copy(hi, tile).then_inc(w_hi, 1)
                else:
                    act.activation(hi, tile, ACT.Copy, scale=W_UP).then_inc(w_hi, 1)

            act.wait_ge(ident_ready, 1)
            act.activation(warm[:, 0:1], ident[:, 0:1], ACT.Exp)
            act.wait_ge(parts_ready, 2 * B)
            for piece in schedule:
                if piece[0] != "s":
                    continue
                _, n, k = piece
                v = s_index(n, k)
                if v in high_at:
                    high_part(high_at.index(v))
                act.wait_ge(s_done, v + 1)
                if k == 0:
                    if n >= 2:
                        act.wait_ge(pv_done, (n - 2) * KC + 1)
                    act.activation(pimg[:, n % 2, :], bank(4 + v % 3), ACT.Exp).then_inc(exp_done, 1)
                    continue
                w = p_index(n, k)
                if w >= P_RING:
                    act.wait_ge(pv_done, chunk_of(w - P_RING) + 1)
                kc, heads, _ = UNITS[k - 1]
                width = heads * (S - kc * P)
                act.activation(p_ring[:, w % P_RING, 0:width], bank(4 + v % 3)[:, 0:width], ACT.Exp
                               ).then_inc(exp_done, 1)

            act.wait_ge(pv_done, groups * KC)
            act.wait_ge(a_done, a_at[("on", B - 1, R - 1)] + 1)
            for n in range(W_EARLY, W_TILES):
                high_part(n)

            def hidden_units(i, e, got, to, bias_row, done):
                for c in range(HC):
                    ins = act.activation(to[:, c * P:(c + 1) * P], got[:, c * P:(c + 1) * P], ACT.Gelu,
                                         bias=cols[:, bass.ds(e * HC + (bias_row + c), 1)], scale=DOWN)
                ins.then_inc(done, 1)

            def gelu1(j, c, e):
                i, s, _ = block_of(j, c)
                act.wait_ge(mm1_done, i + 1)
                if later(i, 1):
                    act.wait_ge(h1_ready, i)
                hidden_units(i, e, bank(1 + s), h32[:, 0], ROW_B1, gelu1_done)

            def gelu2(j, c, e):
                i, s, _ = block_of(j, c)
                act.wait_ge(tz_done, i + 1)
                if later(i, 1):
                    act.wait_ge(h2_ready, i)
                hidden_units(i, e, bank(4), h32[:, 1], ROW_B2, gelu2_done)

            act.activation(warm[:, 1:2], ident[:, 0:1], ACT.Gelu)
            act.wait_ge(a_used, len(a_order))
            gelu1(0, 0, 0)
            gelu1(0, 1, 1)
            act.wait_ge(tab_ready, 1)
            of = table(mybir.EngineType.Activation, 0, 0, LEAD + 2)
            for i in range(LEAD):
                gelu1(0, i + 2, of[i + 2])
                gelu2(0, i, of[i])
            with act.Fori(0, LOOPS) as j:
                of = table(mybir.EngineType.Activation, 0, UNROLL * j + LEAD, UNROLL + 2)
                for n in range(UNROLL):
                    gelu1(j, LEAD + n + 2, of[n + 2])
                    gelu2(j, LEAD + n, of[n])
            of = table(mybir.EngineType.Activation, 0, REST, NB - REST)
            for i in range(REST, NB):
                if i + 2 < NB:
                    gelu1(0, i + 2, of[i + 2 - REST])
                gelu2(0, i, of[i - REST])

            act.wait_ge(l1w_in, 16 * (E + 1))
            for e in range(E):
                act.activation(fc16[0][:, e], fc_sb[:, e], ACT.Copy, scale=W_UP)
                act.activation(cp16[0][:, e], cp_sb[:, e].rearrange("p c d -> p (c d)"), ACT.Copy, scale=W_UP
                               ).then_inc(fc_hi, 1)
            for b in range(B):
                act.wait_ge(xcT_done, b + 1)
                act.copy(xcT[:, b].rearrange("p r n -> p (r n)"), bank(XC_BANKS[b][1])).then_inc(xcT_ready, 1)
                act.wait_ge(xc_done, b + 1)
                for k in range(2):
                    act.copy(sent[:, b, k, :, 0:D],
                             bank(XC_BANKS[b][0]).rearrange("p (r d) -> p r d", d=D)
                             ).then_inc(xc_ready, 1)
                act.activation(xc16[0][:, b], bank(XC_BANKS[b][0]), ACT.Copy, scale=IN_UP).then_inc(xc_hi, 1)
            for e in range(EARLY):
                act.wait_ge(early_done, 2 * e + 1)
                if e >= 2:
                    act.wait_ge(fc_done, (e - 1) * HC)
                act.copy(tgT[:, e % 2, 0, :], bank(0)[:, 0:CAP]).then_inc(tgT_hi, 1)
            act.wait_ge(dl_ready, 1)
            act.activation(th[:, :, :], dl[:, :, :], ACT.Tanh, scale=0.5).then_inc(th_ready, 1)
            for e in range(E):
                for c in range(HC):
                    act.wait_ge(fc_done, e * HC + c + 1)
                    if e and c % 2 == 0:
                        act.wait_ge(hT_ready, 2 * e - 1 + c // 2)
                    act.activation(h1_32[:, c, :], bank(FC_BANKS[c])[:, 0:CAP], ACT.Gelu,
                                   bias=cols[:, ROW_FC + e * HC + c:ROW_FC + e * HC + c + 1], scale=DOWN
                                   ).then_inc(hid_done, 1)
                    if c % 2:
                        act.wait_ge(hid_done, e * HC + c + 1)
                        if e >= 2:
                            act.wait_ge(z_done, e - 1)
                        act.activation(hT[:, e % 2, 0, c - 1:c + 1, :], h1_32[:, c - 1:c + 1, :], ACT.Copy,
                                       scale=IN_UP).then_inc(hT_hi, 1)
            act.wait_ge(p_ready, 1)
            for b in range(B):
                act.wait_ge(back1_in[b], 32)
                for r in range(R):
                    ins = act.activation(back[:, 1, b, r, :], back[:, 1, b, r, :], ACT.Copy,
                                         scale=p_sb[:, 1, b, r:r + 1])
                ins.then_inc(weighted, 1)

        @block.tensor
        def _(pe):
            mm, tr = pe.matmul, pe.transpose
            pe.wait_ge(ident_ready, 1)
            pe.wait_ge(x_in, 16)
            for b in range(B):
                for r in range(R):
                    ins = tr(bank(b)[:, r * P:(r + 1) * P], x_sb[:, b, r, :], ident[:, :])
                ins.then_inc(xT_done, 1)
            pe.wait_ge(rows_in, 16 * 9)
            pe.wait_ge(uk_in, 32)
            tr(bank(2)[:, 0:N_ROWS], rows_sb[0:N_ROWS, :], ident[0:N_ROWS, 0:N_ROWS])
            tr(bank(2)[:, P:2 * P], uk_sb, ident[:, :])
            tr(bank(2)[:, 2 * P:3 * P], uv_sb, ident[:, :]).then_inc(cols_done, 1)
            pe.wait_ge(xT_ready, 1)
            pe.wait_ge(wqkv_in, 16)
            mm(bank(4), wqkv[:, 0:D], xT[:, 0, :], start=True, stop=True).then_inc(qkv_done, 1)
            mm(bank(5), wqkv[:, D:2 * D], xT[:, 0, :], start=True, stop=True).then_inc(qkv_done, 1)
            pe.wait_ge(cols_ready, 1)
            mm(bank(3)[:, 0:B], ukT, cols[:, ROW_IMG:ROW_IMG + B], start=True, stop=True)
            mm(bank(3)[:, B:2 * B], uvT, cols[:, ROW_IMG:ROW_IMG + B], start=True, stop=True
               ).then_inc(img_done, 1)
            pe.wait_ge(xT_ready, 2)
            mm(bank(6), wqkv[:, 0:D], xT[:, 1, :], start=True, stop=True).then_inc(qkv_done, 1)
            mm(bank(7), wqkv[:, D:2 * D], xT[:, 1, :], start=True, stop=True).then_inc(qkv_done, 1)
            for b in range(B):
                for kc in range(KC):
                    ins = mm(bank(b)[:, kc * P:(kc + 1) * P], xT[:, b, kc * P:(kc + 1) * P],
                             wqkv[:, 2 * D:3 * D], start=True, stop=True)
                ins.then_inc(v_done, 1)
            pe.wait_ge(consts, 1)
            for b in range(B):
                pe.wait_ge(vplace_ready, b + 1)
                for g in range(NG):
                    ins = mm(bank(3)[:, g * P:(g + 1) * P],
                             hsel[:, g * G:(g + 1) * G, :].rearrange("p h c -> p (h c)"),
                             vplace[:, g * G:(g + 1) * G, :].rearrange("p h c -> p (h c)"),
                             start=True, stop=True)
                ins.then_inc(vimg_done, 1)
            pe.wait_ge(kbd_ready, 1)
            for b in range(B):
                pe.wait_ge(qkv_ready, 2 * b + 1)
                for t in range(KC):
                    at_c = (b * KC + t) * H
                    ins = mm(bank(2)[:, at_c:at_c + H], q32[:, b, t * P:(t + 1) * P], kimg_bd[:, b, :],
                             start=True, stop=True)
            ins.then_inc(simg_done, 1)
            pe.wait_ge(wc_ready, 1)
            pe.wait_ge(vimg_ready, B)
            for b in range(B):
                ins = tr(bank(3)[:, b * P:(b + 1) * P], wc_sb[:, b, :], ident[:, :])
            ins.then_inc(wcT_done, 1)
            pe.wait_ge(v_ready, B)
            pe.wait_ge(simg_ready, 1)
            pe.wait_ge(wcT_ready, 1)
            pe.wait_ge(qkv_ready, 2 * B)

            def score(n, t, hp):
                b, g = divmod(n, NG)
                pe.wait_ge(qka_in[n % 2], 32 * (n // 2 + 1))
                n_keys = (t + 1) * P
                for i in range(2):
                    j = 2 * hp + i
                    to = a_bank(("score", n, t, hp))[:, i, :]
                    mm(to[:, 0:n_keys], qa[:, n % 2, j, t * P:(t + 1) * P],
                       ka[:, n % 2, j, IMG:IMG + n_keys], start=True, stop=False)
                    ins = mm(to[:, t * P:n_keys], identb[:, :], causal_a[:, :], start=False, stop=True)
                return ins

            def second_scores(n, k):
                v = s_index(n, k)
                to = bank(4 + v % 3)
                if v >= 3:
                    pe.wait_ge(exp_done, v - 2)
                if k == 0:
                    pe.wait_ge(qkb_in[n % 2], 80 * (n // 2 + 1))
                    for j in range(G):
                        ins = mm(to[32 * j:32 * (j + 1), :], kb[:, n % 2, j, 0:IMG], qb[:, n % 2, j, :],
                                 start=True, stop=True, tile_position=(0, 32 * j))
                    return ins
                kc, heads, j0 = UNITS[k - 1]
                width = S - kc * P
                for i in range(heads):
                    mm(to[:, i * width:(i + 1) * width],
                       kb[:, n % 2, j0 + i, IMG + kc * P:IMG + (kc + 1) * P], qb[:, n % 2, j0 + i, kc * P:],
                       start=True, stop=False, skip_group_check=True)
                    ins = mm(to[:, i * width:i * width + P], identb[:, :], causal_b[:, :],
                             start=False, stop=True, skip_group_check=True)
                return ins

            def values(n, kc):
                b, g = divmod(n, NG)
                pe.wait_ge(exp_done, s_index(n, chunk_units(kc)[-1]) + 1)
                if kc == 0:
                    if n:
                        pe.wait_ge(o_ready, n)
                    mm(bank(7), vimg_bd[:, b, g * G:(g + 1) * G, :].rearrange("p h c -> p (h c)"),
                       pimg[:, n % 2, :], start=True, stop=False, skip_group_check=True)
                width = S - kc * P
                for k in chunk_units(kc):
                    _, heads, j0 = UNITS[k - 1]
                    w = p_index(n, k)
                    for i in range(heads):
                        j = j0 + i
                        ins = mm(bank(7)[32 * j:32 * j + HD + 1, kc * P:], v_sb[:, b, kc, g * G + j, :],
                                 p_ring[:, w % P_RING, i * width:(i + 1) * width], start=False,
                                 stop=(kc == KC - 1), tile_position=(0, 32 * j), skip_group_check=True)
                return ins

            for piece in schedule:
                kind, *arg = piece
                if kind == "s":
                    second_scores(*arg).then_inc(s_done, 1)
                    continue
                if kind == "pv":
                    values(*arg).then_inc(pv_done, 1)
                    continue
                if a_at[piece] >= 2:
                    pe.wait_ge(a_used, a_at[piece] - 1)
                to = a_bank(piece)[:, 0, :]
                if kind == "score":
                    ins = score(*arg)
                elif kind == "maxT":
                    pe.wait_ge(m_parts, arg[0] + 1)
                    to = to.bitcast(BF16)
                    for t in range(KC):
                        ins = tr(to[0:3 * G, t * P:(t + 1) * P], mp[:, t, :, :].rearrange("p m h -> p (m h)"),
                                 identb[:, :])
                elif kind == "on":
                    b, r = arg
                    pe.wait_ge(o_ready, (b + 1) * NG)
                    for g in range(NG):
                        ins = tr(to[:, g * P:(g + 1) * P], o_sb[:, (b * NG + g) % O_RING, r::R], ident[:, :])
                elif kind == "onT":
                    b, r = arg
                    pe.wait_ge(a_used, a_at[("on", b, r)] + 1)
                    ins = tr(to[:, 0:P], on_sb[:, r % 2].rearrange("p h d -> p (h d)"), ident[:, :])
                elif kind == "aT":
                    b, = arg
                    pe.wait_ge(misc_in, 48)
                    pe.wait_ge(a_used, a_at[("onT", b, R - 1)] + 1)
                    ins = mm(to, proj_sb[:, :], onT[:, :, :].rearrange("p r q -> p (r q)"), start=True, stop=True)
                elif kind == "a":
                    b, = arg
                    pe.wait_ge(a_used, a_at[("aT", b)] + 1)
                    for r in range(R):
                        ins = tr(to[:, r * P:(r + 1) * P], aT[:, r, :], ident[:, :])
                elif kind == "route":
                    b, = arg
                    pe.wait_ge(a_used, a_at[("aT", b)] + 1)
                    for r in range(R):
                        ins = mm(to[:, r * E:(r + 1) * E], aT[:, r, :], cols[:, ROW_ET:ROW_ET + E],
                                 start=True, stop=True)
                elif kind == "count":
                    b, = arg
                    pe.wait_ge(cnt_ready, b + 1)
                    ins = mm(to[:, 0:E], tri[:, :], cntb[:, 0, b, :], start=True, stop=(b == 0))
                    for b_ in range(b):
                        ins = mm(to[:, 0:E], onesb[:, :], cntb[:, 0, b_, :], start=False, stop=(b_ == b - 1))
                else:
                    for b in range(B):
                        ins = mm(to[:, 0:E], onesb[:, :], cntb[:, 0, b, :], start=(b == 0), stop=(b == B - 1))
                ins.then_inc(a_done, 1)

            def gather_x(i):
                if i:
                    pe.wait_ge(xgT_ready, i)
                for part in range(2):
                    for q in range(B * R):
                        pe.wait_ge(marked, i * B * R + q + 1)
                        b, r = divmod(q, R)
                        ins = mm(bank(0)[:, part * P:(part + 1) * P],
                                 sent[:, b, 0].bitcast(F16)[:, r, part * D:(part + 1) * D],
                                 onehot0[:, i, q, :], start=(q == 0), stop=(q == B * R - 1))
                ins.then_inc(tx_done, 1)

            def transpose_x(j, c):
                i, s, turn = block_of(j, c)
                pe.wait_ge(xg_in[s], 16 * (turn + 1 - (LEAD + 1 - s) // 2))
                pe.wait_ge(xgT_ready, i)
                to = bank(0).bitcast(F16)
                for q in range(2):
                    ins = tr(to[:, q * P:(q + 1) * P], xg[:, s, q * D:(q + 1) * D], identh[:, :])
                ins.then_inc(tx_done, 1)

            def first_layer(j, c, e):
                i, s, _ = block_of(j, c)
                pe.wait_ge(xgT_ready, i + 1)
                if later(i, 2):
                    pe.wait_ge(gelu1_done, i - 1)
                for m in range(HC):
                    for n, (wq, xq) in enumerate(PRODUCTS):
                        ins = mm(bank(1 + s)[:, m * P:(m + 1) * P], w1_sb[m][wq][:, bass.ds(e * P, P)],
                                 xgT[:, s, xq, :], start=(n == 0), stop=(n == len(PRODUCTS) - 1))
                ins.then_inc(mm1_done, 1)

            def second_layer(j, c, e):
                i, s, _ = block_of(j, c)
                pe.wait_ge(h1_ready, i + 1)
                if later(i, 1):
                    pe.wait_ge(z_copied, i)
                for k in range(HC):
                    for n, (wq, hq) in enumerate(PRODUCTS):
                        ins = mm(bank(3), h1[:, s, hq, k * P:(k + 1) * P], w2_sb[k][wq][:, bass.ds(e * HID, HID)],
                                 start=(k == 0 and n == 0), stop=(k == HC - 1 and n == len(PRODUCTS) - 1))
                ins.then_inc(mm2_done, 1)

            def transpose_z(j, c):
                i, _, _ = block_of(j, c)
                pe.wait_ge(z_copied, i + 1)
                if later(i, 1):
                    pe.wait_ge(gelu2_done, i)
                for m in range(HC):
                    ins = tr(bank(4)[:, m * P:(m + 1) * P], z32[:, m * P:(m + 1) * P], ident[:, :])
                ins.then_inc(tz_done, 1)

            def third_layer(j, c, e):
                i, s, _ = block_of(j, c)
                pe.wait_ge(h2_ready, i + 1)
                if later(i, 1):
                    pe.wait_ge(y_ready, i)
                for k in range(HC):
                    for n, (wq, hq) in enumerate(PRODUCTS):
                        ins = mm(bank(5)[:, 0:D], h2[:, s, hq, k * P:(k + 1) * P],
                                 w3_sb[k][wq][:, bass.ds(e * P, P)], start=(k == 0 and n == 0),
                                 stop=(k == HC - 1 and n == len(PRODUCTS) - 1))
                ins.then_inc(mm3_done, 1)

            pe.wait_ge(a_used, len(a_order))
            pe.wait_ge(w_lo, W_EARLY)
            gather_x(0)
            gather_x(1)
            first_layer(0, 0, 0)
            gather_x(2)
            first_layer(0, 1, 1)
            pe.wait_ge(tab_ready, 1)
            of = table(mybir.EngineType.PE, 0, 0, LEAD + 2)
            for i in range(LEAD):
                second_layer(0, i, of[i])
                first_layer(0, i + 2, of[i + 2])
                transpose_x(0, i + 3)
                transpose_z(0, i)
                if i == 0:
                    pe.wait_ge(w_lo, W_TILES - W3_POOL)
                    pe.wait_ge(w_lo_pool, W3_POOL)
                if i:
                    third_layer(0, i - 1, of[i - 1])
            with pe.Fori(0, LOOPS) as j:
                of = table(mybir.EngineType.PE, 0, UNROLL * j + (LEAD - 1), UNROLL + 3)
                for n in range(UNROLL):
                    second_layer(j, LEAD + n, of[n + 1])
                    first_layer(j, LEAD + n + 2, of[n + 3])
                    transpose_x(j, LEAD + n + 3)
                    transpose_z(j, LEAD + n)
                    third_layer(j, LEAD + n - 1, of[n])
            of = table(mybir.EngineType.PE, 0, REST - 1, NB - REST + 1)
            for i in range(REST, NB):
                second_layer(0, i, of[i + 1 - REST])
                if i + 2 < NB:
                    first_layer(0, i + 2, of[i + 3 - REST])
                if i + 3 < NB:
                    transpose_x(0, i + 3)
                transpose_z(0, i)
                third_layer(0, i - 1, of[i - REST])
            third_layer(0, NB - 1, of[NB - REST])

            def logits(b):
                pe.wait_ge(xcT_ready, b + 1)
                for r in range(R):
                    ins = mm(bank(2 + b)[:, r * E:(r + 1) * E], xcT[:, b, r, :], gate_sb[:, :], start=True,
                             stop=True)
                ins.then_inc(lg_done, 1)

            for b in range(B):
                for r in range(R):
                    pe.wait_ge(x1_ready, b * R + r + 1)
                    ins = mm(bank(XC_BANKS[b][1])[:, r * D:(r + 1) * D], x_sb[:, b, r, :], wcT_sb[:, b, :],
                             start=True, stop=True)
                ins.then_inc(xcT_done, 1)
                for r in range(R):
                    ins = mm(bank(XC_BANKS[b][0])[:, r * D:(r + 1) * D], wcT_sb[:, b, :], x_sb[:, b, r, :],
                             start=True, stop=True)
                ins.then_inc(xc_done, 1)
                logits(b)
            c1 = cntb[:, :, :, :].rearrange("p k b e -> p (k b) e")
            for n in range(2 * B):
                if n < 2:
                    pe.wait_ge(cnt1_ready, n + 1)
                to = bank(6 if n == 0 else 7)[:, n * E:(n + 1) * E]
                ins = mm(to, tri[:, :], c1[:, n, :], start=True, stop=(n == 0))
                for before in range(n):
                    ins = mm(to, onesb[:, :], c1[:, before, :], start=False, stop=(before == n - 1))
                if n in (0, 2 * B - 1):
                    ins.then_inc(rank1_done, 1)

            def gather(e):
                for part, (parts_made, bank_read) in enumerate(((xc_hi, tgT_hi), (xc_lo, tgT_ready))):
                    pe.wait_ge(parts_made, B)
                    if e:
                        pe.wait_ge(bank_read, e)
                    for q in range(B * R):
                        pe.wait_ge(onehot_ready, e * B * R + q + 1)
                        b, r = divmod(q, R)
                        ins = mm(bank(part)[:, 0:CAP], xc16[part][:, b, r * D:(r + 1) * D], onehot[e % 2][:, q, :],
                                 start=(q == 0), stop=(q == B * R - 1))
                    ins.then_inc(early_done, 1)

            def transpose_t(e):
                pe.wait_ge(tg_in[e % 2], 32 * ((e - EARLY) // 2 + 1))
                pe.wait_ge(tgT_ready, max(e - 1, EARLY))
                for c in range(CT):
                    k = P if c < CT - 1 else LAST
                    ins = tr(bank(e % 2)[:, c * P:c * P + k], tg[0:k, e % 2, c, 0:D], ident[0:k, 0:k])
                ins.then_inc(tt_done, 1)

            def hidden(e):
                pe.wait_ge(fc_lo, e + 1)
                pe.wait_ge(tgT_ready, e + 1)
                for c in range(HC):
                    n = e * HC + c
                    if e:
                        pe.wait_ge(hid_done, n - HC + 1)
                    for i, (wq, xq) in enumerate(PRODUCTS):
                        ins = mm(bank(FC_BANKS[c])[:, 0:CAP], fc16[wq][:, e, c * P:(c + 1) * P],
                                 tgT[:, e % 2, xq, :], start=(i == 0), stop=(i == len(PRODUCTS) - 1))
                    ins.then_inc(fc_done, 1)

            def project(e):
                pe.wait_ge(hT_ready, (e + 1) * 2)
                if e >= 2:
                    pe.wait_ge(z_ready, e - 1)
                for t in range(CT):
                    k = P if t < CT - 1 else LAST
                    for c in range(HC):
                        for i, (wq, hq) in enumerate(PRODUCTS):
                            ins = mm(bank(4 + e % 2)[0:k, t * P:t * P + D],
                                     hT[:, e % 2, hq, c, t * P:t * P + k], cp16[wq][:, e, c * D:(c + 1) * D],
                                     start=(c == 0 and i == 0), stop=(c == HC - 1 and i == len(PRODUCTS) - 1))
                ins.then_inc(z_done, 1)

            gather(0)
            for e in range(EARLY):
                if e + 1 < EARLY:
                    gather(e + 1)
                hidden(e)
                if e:
                    project(e - 1)
            transpose_t(EARLY)
            for e in range(EARLY - 1, E):
                if e + 2 < E:
                    transpose_t(e + 2)
                if e + 1 < E:
                    hidden(e + 1)
                project(e)

        @block.vector
        def _(dve):
            step = stepper(dve, dve_step)
            tt, ts, copy = dve.tensor_tensor, dve.tensor_scalar, dve.tensor_copy
            dve.memset(zeros[:, :], 0.0).then_inc(zeroed, 1)
            dve.memset(v_sb[:, :, :, :, HD:HD + 1].rearrange("p b k h i -> p (b k h) i"), 1.0)

            dve.wait_ge(cond_in, 48)
            for b in range(B):
                step(dve.scalar_tensor_tensor(out=wc_sb[:, b, :], in0=lw_sb, scalar=float(D) ** -0.5,
                                              in1=cond_bc[:, b, :], op0=ALU.mult, op1=ALU.mult))
                step(dve.tensor_tensor_reduce(out=sq_sb, in0=wc_sb[:, b, :], in1=wc_sb[:, b, :], scale=1.0,
                                              scalar=0.0, op0=ALU.mult, op1=ALU.add,
                                              accum_out=nrm[:, b, 0:1]))
            ts(nrm[:, :, 1], nrm[:, :, 0], 1e-8, None, ALU.add).then_inc(var_ready, 1)
            dve.wait_ge(mask_in, 16)
            step(copy(mpart[:, 0, :], mask_sb[:, :]))
            step(tt(mres[:, :], mask_sb[:, :], mpart[:, 0, :], ALU.subtract))
            step(copy(mpart[:, 1, :], mres[:, :]))
            tt(mpart[:, 2, :], mres[:, :], mpart[:, 1, :], ALU.subtract).then_inc(mask_ready, 1)

            for b in range(B):
                dve.wait_ge(xT_done, b + 1)
                copy(xT[:, b, :].rearrange("d (p r) -> d r p", r=R),
                     bank(b).rearrange("d (r p) -> d r p", r=R)).then_inc(xT_ready, 1)
            dve.wait_ge(cols_done, 1)
            copy(cols[:, :], bank(2)[:, 0:N_ROWS])
            copy(ukT, bank(2)[:, P:2 * P])
            copy(uvT, bank(2)[:, 2 * P:3 * P]).then_inc(cols_ready, 1)
            dve.wait_ge(cols_ready, 1)

            def qkv(n):
                b, i = divmod(n, 2)
                dve.wait_ge(qkv_done, n + 1)
                if i == 0:
                    ts(q32[:, b, :], bank(4 + n), cols[:, ROW_QKV:ROW_QKV + 1], SM_SCALE, ALU.add, ALU.mult
                       ).then_inc(qkv_ready, 1)
                else:
                    ts(k32[:, b, IMG:], bank(4 + n), cols[:, ROW_QKV + 1:ROW_QKV + 2], None, ALU.add
                       ).then_inc(qkv_ready, 1)

            def residue(n):
                b, i = divmod(n, 2)
                w = IMG + S if i else S
                src = k32[:, b, :] if i else q32[:, b, :]
                dve.wait_ge(hi_ready, n + 1)
                tt(res[:, i, 0:w], src, part[:, n, 0, 0:w], ALU.subtract).then_inc(mid_ready, 1)

            def last_part(n):
                b, i = divmod(n, 2)
                w = IMG + S if i else S
                dve.wait_ge(act_step, n + 1)
                tt(part[:, n, 2, 0:w], res[:, i, 0:w], part[:, n, 1, 0:w], ALU.subtract
                   ).then_inc(parts_ready, 1)

            qkv(0)
            dve.wait_ge(img_done, 1)
            dve.memset(k32[:, :, 0:IMG], 0.0)
            step(ts(vimg[:, :], bank(3)[:, B:2 * B], cols[:, ROW_UV:ROW_UV + 1], None, ALU.add))
            step(ts(k32[:, :, 0], bank(3)[:, 0:B], cols[:, ROW_UK:ROW_UK + 1], None, ALU.add))
            qkv(1)
            residue(0)
            dve.wait_ge(consts, 1)
            for b in range(B):
                ins = ts(kimg_bd[:, b, :], hmask[:, :], k32[:, b, 0:1], None, ALU.mult)
            ins.then_inc(kbd_ready, 1)
            last_part(0)
            residue(1)
            ts(vplace, place, vimg[:, 0:1], None, ALU.mult).then_inc(vplace_ready, 1)
            qkv(2)
            last_part(1)
            qkv(3)
            for b in range(B):
                dve.wait_ge(v_done, b + 1)
                tt(v_sb[:, b, :, :, 0:HD], bank(b).rearrange("p (k h d) -> p k h d", k=KC, h=H),
                   vb_bc[:, :].rearrange("p (o h d) -> p o h d", o=1, h=H).broadcast_to([P, KC, H, HD]),
                   ALU.add).then_inc(v_ready, 1)
            dve.wait_ge(vimg_done, 1)
            tt(vimg_bd[:, 0], bank(3).rearrange("p (h c) -> p h c", c=32), onec, ALU.add
               ).then_inc(vimg_ready, 1)
            ts(vplace, place, vimg[:, 1:2], None, ALU.mult).then_inc(vplace_ready, 1)
            residue(2)
            dve.wait_ge(sqrt_ready, 1)
            step(dve.reciprocal(nrm[:, :, 3], nrm[:, :, 2]))
            step(tt(nrm[:, :, 4], nrm[:, :, 3], nrm[:, :, 3], ALU.mult))
            step(tt(nrm[:, :, 5], nrm[:, :, 4], nrm[:, :, 1], ALU.mult))
            step(ts(nrm[:, :, 6], nrm[:, :, 5], -0.5, 1.5, ALU.mult, ALU.add))
            step(tt(nrm[:, :, 7], nrm[:, :, 6], nrm[:, :, 3], ALU.mult))
            last_part(2)
            residue(3)
            for b in range(B):
                ins = ts(wc_sb[:, b, :], wc_sb[:, b, :], nrm[:, b, 7:8], None, ALU.mult)
            ins.then_inc(wc_ready, 1)
            last_part(3)
            dve.wait_ge(vimg_done, 2)
            tt(vimg_bd[:, 1], bank(3).rearrange("p (h c) -> p h c", c=32), onec, ALU.add
               ).then_inc(vimg_ready, 1)
            dve.wait_ge(simg_done, 1)
            copy(simg[:, :, :, :].rearrange("p b t h -> p (b t h)"), bank(2)[:, 0:B * KC * H]
                 ).then_inc(simg_ready, 1)
            dve.wait_ge(wcT_done, 1)
            copy(wcT_sb[:, :, :].rearrange("p b i -> p (b i)"), bank(3)[:, 0:B * P]).then_inc(wcT_ready, 1)
            dve.wait_ge(simg_ready, 1)

            def low_part(n):
                dve.wait_ge(w_hi, n + 1)
                _, (hi, lo) = w_tile(n)
                dve.scalar_tensor_tensor(out=lo, in0=w_ring[n % W_RING][:, :, :], scalar=W_UP, in1=hi,
                                         op0=ALU.mult, op1=ALU.subtract).then_inc(w_lo, 1)

            def maxima(n, first, last):
                b, g = divmod(n, NG)
                mine = slice(g * G, (g + 1) * G)
                if first == 0:
                    dve.wait_ge(a_used, a_at[("score", n, KC - 1, G // 2 - 1)] + 1)
                    if n:
                        dve.wait_ge(a_done, a_at[("maxT", n - 1)] + 1)
                for at_step in range(first, last):
                    if at_step == 0:
                        step(tt(mr[:, :, :], mA[:, b, :, mine], simg[:, b, :, mine], ALU.max))
                    elif at_step == 1:
                        step(ts(negm[:, :, :], mr[:, :, :], -1.0, None, ALU.mult))
                    elif at_step == 2:
                        step(copy(mp[:, :, 0, :], negm[:, :, :]))
                    elif at_step == 3:
                        step(tt(mr[:, :, :], negm[:, :, :], mp[:, :, 0, :], ALU.subtract))
                    elif at_step == 4:
                        step(copy(mp[:, :, 1, :], mr[:, :, :]))
                    else:
                        tt(mp[:, :, 2, :], mr[:, :, :], mp[:, :, 1, :], ALU.subtract).then_inc(m_parts, 1)

            def choose(b):
                for r in range(R):
                    ins = dve.max(top_v[:, b, r, :], lg[:, b, r, :])
                step(ins)
                for r in range(R):
                    ins = dve.max_index(top_i[:, b, r, :], top_v[:, b, r, :], lg[:, b, r, :])
                step(ins)
                step(copy(top_f[:, b, :, 0:2], top_i[:, b, :, 0:2]))
                for k in range(2):
                    ins = tt(oh[:, k, b], iota_e[:, :, :], top_f[:, b, :, k:k + 1].broadcast_to([P, R, E]),
                             ALU.is_equal)
                step(ins)

            for piece in schedule:
                kind, *arg = piece
                if kind == "s":
                    if s_index(*arg) in low_at:
                        low_part(low_at.index(s_index(*arg)))
                    continue
                if kind == "pv":
                    n, kc = arg
                    if kc == KC - 1:
                        dve.wait_ge(pv_done, (n + 1) * KC)
                        if n >= O_RING:
                            dve.wait_ge(a_done, a_at[("on", (n - O_RING) // NG, R - 1)] + 1)
                        copy(o_sb[:, n % O_RING, :], bank(7)).then_inc(o_ready, 1)
                    continue
                dve.wait_ge(a_done, a_at[piece] + 1)
                got = a_bank(piece)
                flat = got[:, 0, :]
                if kind == "score":
                    n, t, hp = arg
                    b, g = divmod(n, NG)
                    dve.tensor_reduce(mA[:, b, t, g * G + 2 * hp:g * G + 2 * hp + 2],
                                      got[:, :, 0:(t + 1) * P], AX_X, ALU.max).then_inc(a_used, 1)
                    if n and t == 0:
                        maxima(n - 1, 3 * hp, 3 * hp + 3)
                    if (n, t, hp) == (groups - 1, KC - 1, G // 2 - 1):
                        maxima(n, 0, 6)
                elif kind == "maxT":
                    n, = arg
                    if n >= 2:
                        dve.wait_ge(qkb_in[n % 2], 80 * (n // 2))
                    copy(mrow[:, n % 2, :], flat.bitcast(BF16)[0:3 * G, 0:S]).then_inc(a_used, 1)
                elif kind == "on":
                    b, r = arg
                    view = flat.rearrange("p (h c) -> p h c", c=32)
                    dve.wait_ge(a_used, a_at[piece])
                    step(dve.reciprocal(rden[:, :], view[:, :, HD]))
                    tt(on_sb[:, r % 2], view[:, :, 0:HD],
                       rden[:, :].rearrange("p (h o) -> p h o", o=1).broadcast_to([P, H, HD]), ALU.mult
                       ).then_inc(a_used, 1)
                elif kind == "onT":
                    b, r = arg
                    copy(onT[:, r, :], flat[:, 0:P]).then_inc(a_used, 1)
                elif kind == "aT":
                    b, = arg
                    ts(aT[:, :, :].rearrange("p r q -> p (r q)"), flat, cols[:, ROW_PROJ:ROW_PROJ + 1], None,
                       ALU.add).then_inc(a_used, 1)
                elif kind == "a":
                    b, = arg
                    parts, again = (sent[:, b, k].bitcast(F16) for k in range(2))
                    got_a = flat.rearrange("p (r d) -> p r d", r=R)
                    step(ts(parts[:, :, 0:D], got_a, IN_UP, None, ALU.mult))
                    dve.scalar_tensor_tensor(out=parts[:, :, D:2 * D], in0=got_a, scalar=IN_UP,
                                             in1=parts[:, :, 0:D], op0=ALU.mult, op1=ALU.subtract
                                             ).then_inc(a_used, 1)
                    dve.wait_ge(a_used, a_at[piece] + 1)
                    copy(again[:, :, 0:2 * D], parts[:, :, 0:2 * D])
                elif kind == "route":
                    b, = arg
                    copy(lg[:, b].rearrange("p r e -> p (r e)"), flat[:, 0:R * E]).then_inc(a_used, 1)
                    dve.wait_ge(a_used, a_at[piece] + 1)
                    choose(b)
                    step(tt(ohsum[:, b], oh[:, 0, b], oh[:, 1, b], ALU.add))
                    step(dve.tensor_reduce(cnt[:, 0, b, :], ohsum[:, b].rearrange("p r e -> p e r"), AX_X,
                                           ALU.add))
                    copy(cntb[:, 0, b, :], cnt[:, 0, b, :]).then_inc(cnt_ready, 1)
                elif kind == "count":
                    b, = arg
                    tt(rank[:, 0, b, 0, :], flat[:, 0:E], base0[:, :], ALU.add).then_inc(a_used, 1)
                    dve.wait_ge(a_used, a_at[piece] + 1)
                    for r in range(1, R):
                        step(tt(rank[:, 0, b, r, :], rank[:, 0, b, r - 1, :], ohsum[:, b, r - 1, :], ALU.add))
                    for k in range(2):
                        ins = tt(pick[:, k, b], oh[:, k, b], rank[:, 0, b], ALU.mult)
                    step(ins)
                    step(dve.tensor_reduce(slot_f[:, :, b, :], pick[:, :, b], AX_X, ALU.add))
                    copy(slot0[:, :, b, :], slot_f[:, :, b, :]).then_inc(slot_ready, 1)
                else:
                    tot = flat[0:1, 0:E]
                    tt(nbge[:, :, :], tcut[:, :, :],
                       tot.rearrange("p (e o) -> p e o", o=1).broadcast_to([1, E, SLOTS0 // P]), ALU.is_lt
                       ).then_inc(a_used, 1)
                    dve.wait_ge(a_used, a_at[piece] + 1)

            def block_table():
                step(dve.tensor_reduce(nblk[:, :], nbge[:, :, :], AX_X, ALU.add))
                step(dve.tensor_tensor_scan(cumb[:, :], nblk[:, :], nblk[:, :], 0.0, ALU.add, ALU.bypass))
                wide = [1, NB, E]
                step(tt(ended[:, :, :], cumb[0:1, :].rearrange("p (o e) -> p o e", o=1).broadcast_to(wide),
                        bidx[:, :, :], ALU.is_le))
                step(tt(endblk[:, :, :], ended[:, :, :],
                        nblk[0:1, :].rearrange("p (o e) -> p o e", o=1).broadcast_to(wide), ALU.mult))
                dve.tensor_reduce(tabf[:, 0, :], ended[:, :, :], AX_X, ALU.add)
                step(dve.tensor_reduce(tabf[:, 1, :], endblk[:, :, :], AX_X, ALU.add))
                step(tt(tabf[:, 2, :], bidx[:, :, 0], tabf[:, 1, :], ALU.subtract))
                step(dve.scalar_tensor_tensor(out=tabf[:, 2, :], in0=tabf[:, 0, :], scalar=float(LEAD),
                                              in1=tabf[:, 2, :], op0=ALU.is_lt, op1=ALU.add))
                step(ts(tabf[:, 3, :], tabf[:, 2, :], float(P), None, ALU.mult))
                step(dve.scalar_tensor_tensor(out=tabf[:, 4, :], in0=tabf[:, 0, :], scalar=float(SLOTS0),
                                              in1=tabf[:, 3, :], op0=ALU.mult, op1=ALU.add))
                ts(tab[:, 0, LEAD:], tabf[:, 0, LEAD:], float(E - 1), None, ALU.min)
                ts(tab[:, 1, LEAD:], tabf[:, 4, LEAD:], float(E * SLOTS0 - P), None, ALU.min
                   ).then_inc(tab_ready, 1)

            def mark_x(i):
                for q in range(B * R):
                    b, r = divmod(q, R)
                    ts(onehot0[:, i, q, :], slot_no[:, 0:P], sel[:, b, r, i:i + 1], None, ALU.is_equal
                       ).then_inc(marked, 1)

            def copy_lead(i):
                dve.wait_ge(tx_done, i + 1)
                if i >= 2:
                    dve.wait_ge(mm1_done, i - 1)
                copy(xgT[:, i % 2].rearrange("p q n -> p (q n)"), bank(0)[:, 0:2 * P]).then_inc(xgT_ready, 1)

            def copy_x(j, c):
                i, s, _ = block_of(j, c)
                dve.wait_ge(tx_done, i + 1)
                dve.wait_ge(mm1_done, i - 1)
                copy(id_all[:, bass.ds(i, 1)], xg[:, s, 2 * D:].bitcast(I32))
                copy(xgT[:, s].rearrange("p q n -> p (q n)"), bank(0).bitcast(F16)[:, 0:2 * P]
                     ).then_inc(xgT_ready, 1)

            def copy_z(j, c):
                i, _, _ = block_of(j, c)
                dve.wait_ge(mm2_done, i + 1)
                if later(i, 1):
                    dve.wait_ge(tz_done, i)
                copy(z32[:, :], bank(3)).then_inc(z_copied, 1)

            def split_1(j, c):
                i, s, _ = block_of(j, c)
                dve.wait_ge(gelu1_done, i + 1)
                if later(i, 2):
                    dve.wait_ge(mm2_done, i - 1)
                ts(h1[:, s, 0, :], h32[:, 0], IN_UP, None, ALU.mult).then_inc(hi1_ready, 1)
                dve.wait_ge(hi1_ready, i + 1)
                dve.scalar_tensor_tensor(out=h1[:, s, 1, :], in0=h32[:, 0], scalar=IN_UP, in1=h1[:, s, 0, :],
                                         op0=ALU.mult, op1=ALU.subtract).then_inc(h1_ready, 1)

            def split_2(j, c):
                i, s, _ = block_of(j, c)
                dve.wait_ge(gelu2_done, i + 1)
                if later(i, 2):
                    dve.wait_ge(mm3_done, i - 1)
                ts(h2[:, s, 0, :], h32[:, 1], IN_UP, None, ALU.mult).then_inc(hi2_ready, 1)
                dve.wait_ge(hi2_ready, i + 1)
                dve.scalar_tensor_tensor(out=h2[:, s, 1, :], in0=h32[:, 1], scalar=IN_UP, in1=h2[:, s, 0, :],
                                         op0=ALU.mult, op1=ALU.subtract).then_inc(h2_ready, 1)

            def result(j, c, e):
                i, s, turn = block_of(j, c)
                dve.wait_ge(mm3_done, i + 1)
                if later(i, 2):
                    dve.wait_ge(y_out[s], 16 * turn)
                if later(i, LEAD - 1):
                    dve.wait_ge(xgT_ready, i + 1)
                    copy(id_now[:, s:s + 1], id_all[:, bass.ds(i, 1)])
                dve.scalar_tensor_tensor(out=y_sb[:, s, :], in0=bank(5)[:, 0:D], scalar=DOWN,
                                         in1=b3_sb[:, bass.ds(e * D, D)], op0=ALU.mult, op1=ALU.add
                                         ).then_inc(y_ready, 1)

            for b in range(B):
                ins = dve.scalar_tensor_tensor(out=sel[:, b], in0=rank[:, 0, b], scalar=1.0, in1=ohsum[:, b],
                                               op0=ALU.add, op1=ALU.mult)
            step(ins)
            by_row = sel[:, :, :, :].rearrange("p b r e -> p (b r) e")
            step(tt(by_row, by_row, base0[:, :].rearrange("p (o e) -> p o e", o=1).broadcast_to([P, B * R, E]),
                    ALU.subtract))
            mark_x(0)
            mark_x(1)
            copy_lead(0)
            mark_x(2)
            copy_lead(1)
            block_table()
            split_1(0, 0)
            copy_lead(2)
            low_part(W_EARLY)
            split_1(0, 1)
            for n in range(W_EARLY + 1, W_TILES - W3_POOL):
                low_part(n)
            dve.wait_ge(b3_in, 16)
            for i in range(LEAD):
                copy_z(0, i)
                copy_x(0, i + 3)
                split_1(0, i + 2)
                if i:
                    result(0, i - 1, i - 1)
                split_2(0, i)
            dve.wait_ge(lead_in, 16 * LEAD)
            copy(id_all[:, LEAD - 1:LEAD], xg_lead[:, LEAD - 1, 2 * D:].bitcast(I32)).then_inc(id_copied, 1)
            dve.wait_ge(id_copied, 1)
            with dve.Fori(0, LOOPS) as j:
                of = table(mybir.EngineType.DVE, 0, UNROLL * j + (LEAD - 1), UNROLL)
                for n in range(UNROLL):
                    copy_z(j, LEAD + n)
                    copy_x(j, LEAD + n + 3)
                    split_1(j, LEAD + n + 2)
                    result(j, LEAD + n - 1, of[n])
                    split_2(j, LEAD + n)
            of = table(mybir.EngineType.DVE, 0, REST - 1, NB - REST + 1)
            for i in range(REST, NB):
                copy_z(0, i)
                if i + 3 < NB:
                    copy_x(0, i + 3)
                if i + 2 < NB:
                    split_1(0, i + 2)
                result(0, i - 1, of[i - REST])
                split_2(0, i)
            result(0, NB - 1, of[NB - REST])

            def split_weights(e):
                dve.wait_ge(fc_hi, e + 1)
                for raw, (hi, lo) in ((fc_sb[:, e], fc16), (cp_sb[:, e].rearrange("p c d -> p (c d)"), cp16)):
                    ins = dve.scalar_tensor_tensor(out=lo[:, e], in0=raw, scalar=W_UP, in1=hi[:, e],
                                                   op0=ALU.mult, op1=ALU.subtract)
                ins.then_inc(fc_lo, 1)

            dve.wait_ge(l1w_in, 16 * (E + 1))
            for e in range(PREPARED):
                split_weights(e)

            for b in range(B):
                dve.wait_ge(back_in[b], 32)
                step(tt(back[:, 0, b], back[:, 0, b], back[:, 1, b], ALU.add))
                for r in range(R):
                    dve.scalar_tensor_tensor(out=x_sb[:, b, r, :], in0=back[:, 0, b, r, :], scalar=0.5,
                                             in1=x_sb[:, b, r, :], op0=ALU.mult, op1=ALU.add
                                             ).then_inc(x1_ready, 1)
            dve.memset(tg[:, :, CT - 1, :], 0.0)
            for e in range(EARLY):
                dve.memset(tg_early[e][:, CT - 1, :], 0.0)

            def choices(b):
                dve.wait_ge(lg_done, b + 1)
                step(copy(lg[:, b].rearrange("p r e -> p (r e)"), bank(2 + b)[:, 0:R * E]))
                choose(b)
                step(dve.tensor_reduce(cnt[:, :, b, :], oh[:, :, b].rearrange("p k r e -> p k e r"), AX_X,
                                       ALU.add))
                copy(cntb[:, :, b, :], cnt[:, :, b, :]).then_inc(cnt1_ready, 1)

            def slots(first, last, got):
                n = last - first
                sets = "p k b r e -> p (k b) r e"
                rank_s = rank[:, :, :, :, :].rearrange(sets)[:, first:last]
                oh_s = oh[:, :, :, :, :].rearrange(sets)[:, first:last]
                step(copy(rank_s[:, :, 0, :], got.rearrange("p (q e) -> p q e", e=E)))
                for r in range(1, R):
                    step(tt(rank_s[:, :, r, :], rank_s[:, :, r - 1, :], oh_s[:, :, r - 1, :], ALU.add))
                flat4 = lambda t: t.rearrange("p q r e -> p (q r) e")
                flat3 = lambda t: t[:, :, :, :].rearrange("p k b r -> p (k b r)")[:, first * R:last * R]
                pick_f = flat4(pick[:, :, :, :, :].rearrange(sets)[:, first:last])
                step(tt(pick_f, flat4(oh_s), flat4(rank_s), ALU.mult))
                step(dve.tensor_reduce(flat3(rank_f), pick_f, AX_X, ALU.add))
                mine = dump[:, first * R:last * R]
                ts(flat3(keep), flat3(rank_f), float(CAP), None, ALU.is_lt)
                step(tt(flat3(rank_d), flat3(rank_f), mine, ALU.subtract))
                for q in range(first, last):
                    ins = dve.scalar_tensor_tensor(out=slot_f[:, q // B, q % B, :], in0=top_f[:, q % B, :, q // B],
                                                   scalar=float(CAP), in1=rank_d[:, q // B, q % B, :],
                                                   op0=ALU.mult, op1=ALU.add)
                step(ins)
                step(tt(flat3(slot_f), flat3(slot_f), flat3(keep), ALU.mult))
                tt(flat3(slot1), flat3(slot_f), mine, ALU.add).then_inc(slot1_ready, 1)

            choices(0)
            dve.wait_ge(rank1_done, 1)
            slots(0, 1, bank(6)[:, 0:E])
            choices(1)
            dve.wait_ge(rank1_done, 2)
            slots(1, 2 * B, bank(7)[:, E:2 * B * E])
            tt(ohsum[:, :, :, :], oh[:, 0], oh[:, 1], ALU.add)
            step(tt(sel[:, :, :, :], pick[:, 0], pick[:, 1], ALU.add))
            step(tt(sel[:, :, :, :], sel[:, :, :, :], ohsum[:, :, :, :], ALU.add))

            def mark(e):
                if e >= 2:
                    dve.wait_ge(early_done, 2 * (e - 1))
                for q in range(B * R):
                    b, r = divmod(q, R)
                    ts(onehot[e % 2][:, q, :], slot_no[:, :], sel[:, b, r, e:e + 1], None, ALU.is_equal
                       ).then_inc(onehot_ready, 1)

            def copy_low(e):
                dve.wait_ge(early_done, 2 * e + 2)
                dve.wait_ge(tgT_hi, e + 1)
                if e >= 2:
                    dve.wait_ge(fc_done, (e - 1) * HC)
                copy(tgT[:, e % 2, 1, :], bank(1)[:, 0:CAP]).then_inc(tgT_ready, 1)

            def result_rows(e, ids):
                step(ts(is_free[:, :], ids, 0.0, None, ALU.is_equal))
                step(tt(is_free[:, :], is_free[:, :], free_row[:, e, :], ALU.mult))
                return tt(id1[:, e, :], is_free[:, :], ids, ALU.add)

            def copy_t(e):
                dve.wait_ge(tt_done, e - EARLY + 1)
                if e >= 2:
                    dve.wait_ge(fc_done, (e - 1) * HC)
                result_rows(e, tg[:, e % 2].bitcast(I32)[:, :, D])
                step(ts(tgT[:, e % 2, 0, :], bank(e % 2)[:, 0:CAP], IN_UP, None, ALU.mult))
                dve.scalar_tensor_tensor(out=tgT[:, e % 2, 1, :], in0=bank(e % 2)[:, 0:CAP], scalar=IN_UP,
                                         in1=tgT[:, e % 2, 0, :], op0=ALU.mult, op1=ALU.subtract
                                         ).then_inc(tgT_ready, 1)

            def split_h(e):
                for half in range(2):
                    mine = slice(2 * half, 2 * half + 2)
                    dve.wait_ge(hT_hi, 2 * e + half + 1)
                    dve.scalar_tensor_tensor(out=hT[:, e % 2, 1, mine, :], in0=h1_32[:, mine, :], scalar=IN_UP,
                                             in1=hT[:, e % 2, 0, mine, :], op0=ALU.mult, op1=ALU.subtract
                                             ).then_inc(hT_ready, 1)

            def add_bias(e):
                dve.wait_ge(z_done, e + 1)
                if e >= 4:
                    dve.wait_ge(z_out[e % 4], 16 * CT * (e // 4))
                got = bank(4 + e % 2)
                dve.scalar_tensor_tensor(out=z_sb[e % 4][:, 0:CT - 1, :],
                                         in0=got[:, 0:(CT - 1) * D].rearrange("p (c d) -> p c d", d=D),
                                         scalar=DOWN, in1=prb_sb[:, e:e + 1, :].broadcast_to([P, CT - 1, D]),
                                         op0=ALU.mult, op1=ALU.add)
                dve.scalar_tensor_tensor(out=z_sb[e % 4][0:LAST, CT - 1, :],
                                         in0=got[0:LAST, (CT - 1) * D:CT * D], scalar=DOWN,
                                         in1=prb_sb[0:LAST, e, :], op0=ALU.mult, op1=ALU.add
                                         ).then_inc(z_ready, 1)

            tt(dl[:, :, :], top_v[:, :, :, 0], top_v[:, :, :, 1], ALU.subtract).then_inc(dl_ready, 1)
            mark(0)
            for b in range(B):
                dve.wait_ge(xc_hi, b + 1)
                dve.scalar_tensor_tensor(out=xc16[1][:, b].rearrange("p (r d) -> p r d", d=D),
                                         in0=sent[:, b, 0, :, 0:D], scalar=IN_UP,
                                         in1=xc16[0][:, b].rearrange("p (r d) -> p r d", d=D),
                                         op0=ALU.mult, op1=ALU.subtract).then_inc(xc_lo, 1)
            for e in range(EARLY):
                if e + 1 < EARLY:
                    mark(e + 1)
                copy_low(e)
                if PREPARED + e < E:
                    split_weights(PREPARED + e)
                if e:
                    split_h(e - 1)
                    if e >= 2:
                        add_bias(e - 2)
            dve.wait_ge(th_ready, 1)
            ts(p_sb[:, 0], th[:, :, :], 0.5, 0.5, ALU.mult, ALU.add)
            ts(p_sb[:, 1], th[:, :, :], -0.5, 0.5, ALU.mult, ALU.add).then_inc(p_ready, 1)
            for e in range(PREPARED + EARLY, E):
                split_weights(e)
            add_bias(EARLY - 2)
            split_h(EARLY - 1)
            copy_t(EARLY)
            for e in range(EARLY - 1, E):
                if e + 2 < E:
                    copy_t(e + 2)
                if e + 1 < E:
                    split_h(e + 1)
                add_bias(e)
                if e == EARLY - 1:
                    dve.wait_ge(early_in, 32 * EARLY)
                    for n in range(EARLY):
                        result_rows(n, tg_early[n].bitcast(I32)[:, :, D]).then_inc(id_ready, 1)
                        dve.wait_ge(id_ready, n + 1)

            dve.wait_ge(p_ready, 1)
            for b in range(B):
                dve.wait_ge(back1_in[b], 32)
                for r in range(R):
                    ins = dve.scalar_tensor_tensor(out=x_sb[:, b, r, :], in0=back[:, 0, b, r, :],
                                                   scalar=p_sb[:, 0, b, r:r + 1], in1=x_sb[:, b, r, :],
                                                   op0=ALU.mult, op1=ALU.add)
                step(ins)
                dve.wait_ge(weighted, b + 1)
                tt(x_sb[:, b], x_sb[:, b], back[:, 1, b], ALU.add).then_inc(r_ready, 1)


_INS = ['x', 'cond_1024', 'mask_Bx1x1xS_ff0', 'L0_cond_c_attn_w', 'L0_cond_c_attn_b', 'L0_cond_c_proj_w',
        'L0_cond_c_proj_b', 'L0_cond_uk_w', 'L0_cond_uk_b', 'L0_cond_uv_w', 'L0_cond_uv_b',
        'L0_ffn_expert_tokens', 'L0_ffn_W1', 'L0_ffn_b1', 'L0_ffn_W2', 'L0_ffn_b2', 'L0_ffn_W3', 'L0_ffn_b3',
        'L1_cond_weight', 'L1_ffn_gate_w', 'L1_ffn_c_fc', 'L1_ffn_fc_bias', 'L1_ffn_c_proj',
        'L1_ffn_proj_bias']
_OUTS = [((B, S, D), 'float32')]


def kernel(**inputs):
    import numpy as _np
    import concourse.bacc as _bacc
    from concourse import mybir as _mybir
    from concourse.bass_utils import run_bass_kernel_spmd as _run

    nc = _bacc.Bacc("TRN2", target_bir_lowering=False, num_devices=1)
    arrays, args = {}, []
    for name in _INS:
        a = _np.ascontiguousarray(inputs[name])
        arrays[f"in_{name}_dram"] = a
        args.append(nc.dram_tensor(f"in_{name}_dram", a.shape, _mybir.dt.from_np(a.dtype), kind="ExternalInput").ap())
    for i, (shape, dtype) in enumerate(_OUTS):
        dt = _mybir.dt.from_np(_np.dtype(dtype))
        args.append(nc.dram_tensor(f"out_{i}_dram", shape, dt, kind="ExternalOutput").ap())
    build(nc, *args)
    r = _run(nc, [arrays], core_ids=[0])
    return r.results[0]["out_0_dram"]
```
